# Optimizing a Trainium2 kernel written in Bass

```python
import numpy as np
import jax
import jax.numpy as jnp

def _softmax(x, axis=-1):
    return jax.nn.softmax(x, axis=axis)

def _gelu(x):
    return jax.nn.gelu(x, approximate=True)

def _silu(x):
    return jax.nn.silu(x)

def _sigmoid(x):
    return jax.nn.sigmoid(x)

def _layernorm(x, axis=-1, eps=1e-05):
    m = jnp.mean(x, axis=axis, keepdims=True)
    v = jnp.var(x, axis=axis, keepdims=True)
    return (x - m) / jnp.sqrt(v + eps)

def _scatter_add(tgt, idx, src, axis=0):
    return tgt.at[idx].add(src)

def _segment_sum(src, seg, n):
    return jax.ops.segment_sum(src, seg, n)
kernel_name = 'mk_lm_tower_d1_tok_ids1024_r4_ac8eb6'

def setup_inputs(seed: int=0):
    np.random.seed(seed)
    _w = jnp.asarray

    def _rec_inputs():
        import jax
        import jax.numpy as jnp
        _rk = jax.random.key(seed)
        x = jax.random.randint(jax.random.fold_in(_rk, 1), (2, 2048), 0, 31983, jnp.int32)
        return x
    x = _rec_inputs()

    def _L0_tok_setup():
        import jax, jax.numpy as jnp
        import numpy as np
        VOCAB, D_MODEL, OUT_DIM, N_HEADS = (8000, 256, 256, 16)
        D_K = D_MODEL // N_HEADS
        key = jax.random.key(seed)
        ks = jax.random.split(key, 10)
        s = 1.0 / np.sqrt(D_MODEL)
        return {'x': jax.random.randint(ks[0], (2, 512), 0, VOCAB), 'emb': jax.random.normal(ks[1], (VOCAB, D_MODEL), jnp.float32) * s, 'wq': jax.random.normal(ks[2], (D_MODEL, D_MODEL), jnp.float32) * s, 'bq': jnp.zeros((D_MODEL,), jnp.float32), 'wk': jax.random.normal(ks[3], (D_MODEL, D_MODEL), jnp.float32) * s, 'bk': jnp.zeros((D_MODEL,), jnp.float32), 'wv': jax.random.normal(ks[4], (D_MODEL, D_MODEL), jnp.float32) * s, 'bv': jnp.zeros((D_MODEL,), jnp.float32), 'wo': jax.random.normal(ks[5], (D_MODEL, OUT_DIM), jnp.float32) * s, 'bo': jnp.zeros((OUT_DIM,), jnp.float32)}
    _L0_tok_all = _L0_tok_setup()
    _L0_tok_in = {k: v for k, v in _L0_tok_all.items() if k in ('emb', 'wq', 'bq', 'wk', 'bk', 'wv', 'bv', 'wo', 'bo')}
    del _L0_tok_all

    def _L0_attn_setup():
        import jax, jax.numpy as jnp
        import numpy as np
        D_MODEL = 256
        D_STATE = 16
        D_CONV = 4
        EXPAND = 2
        D_INNER = EXPAND * D_MODEL
        DT_RANK = (D_MODEL + 15) // 16
        BATCH = 2
        SEQ = 256

        def _mamba(x, in_w, conv_w, conv_b, xproj_w, dt_w, dt_b, A_log, D_param, out_w):
            Bsz, L, _ = x.shape
            xz = x @ in_w.T
            xh, z = jnp.split(xz, 2, axis=-1)
            xp = jnp.pad(xh, ((0, 0), (D_CONV - 1, 0), (0, 0)))
            xc = conv_b + sum((xp[:, k:k + L, :] * conv_w[:, k] for k in range(D_CONV)))
            xc = jax.nn.silu(xc)
            proj = xc @ xproj_w.T
            dt = proj[..., :DT_RANK]
            Bm = proj[..., DT_RANK:DT_RANK + D_STATE]
            Cm = proj[..., DT_RANK + D_STATE:]
            delta = jax.nn.softplus(dt @ dt_w.T + dt_b)
            A = -jnp.exp(A_log)
            deltaA = jnp.exp(jnp.einsum('bld,dn->bldn', delta, A))
            deltaBu = jnp.einsum('bld,bln->bldn', delta * xc, Bm)

            def step(h, inp):
                dA, dBu, c = inp
                h = dA * h + dBu
                y = jnp.einsum('bdn,bn->bd', h, c)
                return (h, y)
            h0 = jnp.zeros((Bsz, D_INNER, D_STATE), x.dtype)
            _, ys = jax.lax.scan(step, h0, (deltaA.transpose(1, 0, 2, 3), deltaBu.transpose(1, 0, 2, 3), Cm.transpose(1, 0, 2)))
            y = ys.transpose(1, 0, 2) + xc * D_param
            y = y * jax.nn.silu(z)
            return y @ out_w.T
        key = jax.random.key(seed)
        ks = jax.random.split(key, 20)
        s = 0.02

        def mk(i, shape):
            return jax.random.normal(ks[i], shape, jnp.float32) * s
        A_log = jnp.log(jnp.arange(1, D_STATE + 1, dtype=jnp.float32))[None, :].repeat(D_INNER, 0)
        inp = {'x': jax.random.normal(ks[0], (BATCH, SEQ, D_MODEL), jnp.float32)}
        for p, base in (('f', 1), ('b', 10)):
            inp[f'{p}_in_w'] = mk(base + 0, (2 * D_INNER, D_MODEL))
            inp[f'{p}_conv_w'] = mk(base + 1, (D_INNER, D_CONV))
            inp[f'{p}_conv_b'] = jnp.zeros((D_INNER,), jnp.float32)
            inp[f'{p}_xproj_w'] = mk(base + 2, (DT_RANK + 2 * D_STATE, D_INNER))
            inp[f'{p}_dt_w'] = mk(base + 3, (D_INNER, DT_RANK))
            inp[f'{p}_dt_b'] = mk(base + 4, (D_INNER,))
            inp[f'{p}_A_log'] = A_log
            inp[f'{p}_D'] = jnp.ones((D_INNER,), jnp.float32)
            inp[f'{p}_out_w'] = mk(base + 5, (D_MODEL, D_INNER))
        return inp
    _L0_attn_all = _L0_attn_setup()
    _L0_attn_in = {k: v for k, v in _L0_attn_all.items() if k in ('f_in_w', 'f_conv_w', 'f_conv_b', 'f_xproj_w', 'f_dt_w', 'f_dt_b', 'f_A_log', 'f_D', 'f_out_w', 'b_in_w', 'b_conv_w', 'b_conv_b', 'b_xproj_w', 'b_dt_w', 'b_dt_b', 'b_A_log', 'b_D', 'b_out_w')}
    del _L0_attn_all

    def _L0_ffn_setup():
        import jax, jax.numpy as jnp
        import numpy as np
        D_MODEL, D_FF, RANK = (256, 1024, 64)
        B, S = (4, 1024)
        key = jax.random.key(seed)
        ks = jax.random.split(key, 7)
        return {'x': jax.random.normal(ks[0], (B, S, D_MODEL), dtype=jnp.float32), 'U1': jax.random.normal(ks[1], (D_MODEL, RANK), dtype=jnp.float32) * 0.02, 'V1': jax.random.normal(ks[2], (RANK, D_FF), dtype=jnp.float32) * 0.02, 'b1': jnp.zeros((D_FF,), dtype=jnp.float32), 'U2': jax.random.normal(ks[3], (D_FF, RANK), dtype=jnp.float32) * 0.02, 'V2': jax.random.normal(ks[4], (RANK, D_MODEL), dtype=jnp.float32) * 0.02, 'b2': jnp.zeros((D_MODEL,), dtype=jnp.float32)}
    _L0_ffn_all = _L0_ffn_setup()
    _L0_ffn_in = {k: v for k, v in _L0_ffn_all.items() if k in ('U1', 'V1', 'b1', 'U2', 'V2', 'b2')}
    del _L0_ffn_all
    return {'x': x, 'L0_tok_emb': _L0_tok_in['emb'], 'L0_tok_wq': _L0_tok_in['wq'], 'L0_tok_bq': _L0_tok_in['bq'], 'L0_tok_wk': _L0_tok_in['wk'], 'L0_tok_bk': _L0_tok_in['bk'], 'L0_tok_wv': _L0_tok_in['wv'], 'L0_tok_bv': _L0_tok_in['bv'], 'L0_tok_wo': _L0_tok_in['wo'], 'L0_tok_bo': _L0_tok_in['bo'], 'L0_attn_f_in_w': _L0_attn_in['f_in_w'], 'L0_attn_f_conv_w': _L0_attn_in['f_conv_w'], 'L0_attn_f_conv_b': _L0_attn_in['f_conv_b'], 'L0_attn_f_xproj_w': _L0_attn_in['f_xproj_w'], 'L0_attn_f_dt_w': _L0_attn_in['f_dt_w'], 'L0_attn_f_dt_b': _L0_attn_in['f_dt_b'], 'L0_attn_f_A_log': _L0_attn_in['f_A_log'], 'L0_attn_f_D': _L0_attn_in['f_D'], 'L0_attn_f_out_w': _L0_attn_in['f_out_w'], 'L0_attn_b_in_w': _L0_attn_in['b_in_w'], 'L0_attn_b_conv_w': _L0_attn_in['b_conv_w'], 'L0_attn_b_conv_b': _L0_attn_in['b_conv_b'], 'L0_attn_b_xproj_w': _L0_attn_in['b_xproj_w'], 'L0_attn_b_dt_w': _L0_attn_in['b_dt_w'], 'L0_attn_b_dt_b': _L0_attn_in['b_dt_b'], 'L0_attn_b_A_log': _L0_attn_in['b_A_log'], 'L0_attn_b_D': _L0_attn_in['b_D'], 'L0_attn_b_out_w': _L0_attn_in['b_out_w'], 'L0_ffn_U1': _L0_ffn_in['U1'], 'L0_ffn_V1': _L0_ffn_in['V1'], 'L0_ffn_b1': _L0_ffn_in['b1'], 'L0_ffn_U2': _L0_ffn_in['U2'], 'L0_ffn_V2': _L0_ffn_in['V2'], 'L0_ffn_b2': _L0_ffn_in['b2']}

def reference(x, L0_tok_emb, L0_tok_wq, L0_tok_bq, L0_tok_wk, L0_tok_bk, L0_tok_wv, L0_tok_bv, L0_tok_wo, L0_tok_bo, L0_attn_f_in_w, L0_attn_f_conv_w, L0_attn_f_conv_b, L0_attn_f_xproj_w, L0_attn_f_dt_w, L0_attn_f_dt_b, L0_attn_f_A_log, L0_attn_f_D, L0_attn_f_out_w, L0_attn_b_in_w, L0_attn_b_conv_w, L0_attn_b_conv_b, L0_attn_b_xproj_w, L0_attn_b_dt_w, L0_attn_b_dt_b, L0_attn_b_A_log, L0_attn_b_D, L0_attn_b_out_w, L0_ffn_U1, L0_ffn_V1, L0_ffn_b1, L0_ffn_U2, L0_ffn_V2, L0_ffn_b2):
    import jax
    import jax.numpy as jnp

    def _L0_tok_ref(x, emb, wq, bq, wk, bk, wv, bv, wo, bo):
        import jax, jax.numpy as jnp
        import numpy as np
        VOCAB, D_MODEL, OUT_DIM, N_HEADS = (8000, 256, 256, 16)
        D_K = D_MODEL // N_HEADS
        B, S = x.shape
        h = emb[x]

        def heads(w, b):
            p = h @ w + b
            return p.reshape(B, S, N_HEADS, D_K).transpose(0, 2, 1, 3)
        Q, K, V = (heads(wq, bq), heads(wk, bk), heads(wv, bv))
        score = jnp.einsum('bhsd,bhtd->bhst', Q, K) / jnp.sqrt(jnp.float32(D_K))
        attn = jax.nn.softmax(score, axis=-1)
        o = jnp.einsum('bhst,bhtd->bhsd', attn, V)
        o = o.transpose(0, 2, 1, 3).reshape(B, S, D_MODEL)
        return o @ wo + bo

    def _L0_attn_ref(x, f_in_w, f_conv_w, f_conv_b, f_xproj_w, f_dt_w, f_dt_b, f_A_log, f_D, f_out_w, b_in_w, b_conv_w, b_conv_b, b_xproj_w, b_dt_w, b_dt_b, b_A_log, b_D, b_out_w):
        import jax, jax.numpy as jnp
        import numpy as np
        D_MODEL = 256
        D_STATE = 16
        D_CONV = 4
        EXPAND = 2
        D_INNER = EXPAND * D_MODEL
        DT_RANK = (D_MODEL + 15) // 16
        BATCH = 2
        SEQ = 256

        def _mamba(x, in_w, conv_w, conv_b, xproj_w, dt_w, dt_b, A_log, D_param, out_w):
            Bsz, L, _ = x.shape
            xz = x @ in_w.T
            xh, z = jnp.split(xz, 2, axis=-1)
            xp = jnp.pad(xh, ((0, 0), (D_CONV - 1, 0), (0, 0)))
            xc = conv_b + sum((xp[:, k:k + L, :] * conv_w[:, k] for k in range(D_CONV)))
            xc = jax.nn.silu(xc)
            proj = xc @ xproj_w.T
            dt = proj[..., :DT_RANK]
            Bm = proj[..., DT_RANK:DT_RANK + D_STATE]
            Cm = proj[..., DT_RANK + D_STATE:]
            delta = jax.nn.softplus(dt @ dt_w.T + dt_b)
            A = -jnp.exp(A_log)
            deltaA = jnp.exp(jnp.einsum('bld,dn->bldn', delta, A))
            deltaBu = jnp.einsum('bld,bln->bldn', delta * xc, Bm)

            def step(h, inp):
                dA, dBu, c = inp
                h = dA * h + dBu
                y = jnp.einsum('bdn,bn->bd', h, c)
                return (h, y)
            h0 = jnp.zeros((Bsz, D_INNER, D_STATE), x.dtype)
            _, ys = jax.lax.scan(step, h0, (deltaA.transpose(1, 0, 2, 3), deltaBu.transpose(1, 0, 2, 3), Cm.transpose(1, 0, 2)))
            y = ys.transpose(1, 0, 2) + xc * D_param
            y = y * jax.nn.silu(z)
            return y @ out_w.T
        y_fwd = _mamba(x, f_in_w, f_conv_w, f_conv_b, f_xproj_w, f_dt_w, f_dt_b, f_A_log, f_D, f_out_w)
        y_bwd = jnp.flip(_mamba(jnp.flip(x, 1), b_in_w, b_conv_w, b_conv_b, b_xproj_w, b_dt_w, b_dt_b, b_A_log, b_D, b_out_w), 1)
        return y_fwd + y_bwd

    def _L0_ffn_ref(x, U1, V1, b1, U2, V2, b2):
        import jax, jax.numpy as jnp
        import numpy as np
        D_MODEL, D_FF, RANK = (256, 1024, 64)
        B, S = (4, 1024)
        P = jnp.einsum('bsd,dr->bsr', x, U1)
        H = jax.nn.gelu(jnp.einsum('bsr,rf->bsf', P, V1) + b1)
        Q = jnp.einsum('bsf,fr->bsr', H, U2)
        return jnp.einsum('bsr,rd->bsd', Q, V2) + b2
    h = _L0_tok_ref(x, L0_tok_emb, L0_tok_wq, L0_tok_bq, L0_tok_wk, L0_tok_bk, L0_tok_wv, L0_tok_bv, L0_tok_wo, L0_tok_bo)
    h = h + _L0_attn_ref(_layernorm(h, axis=-1), L0_attn_f_in_w, L0_attn_f_conv_w, L0_attn_f_conv_b, L0_attn_f_xproj_w, L0_attn_f_dt_w, L0_attn_f_dt_b, L0_attn_f_A_log, L0_attn_f_D, L0_attn_f_out_w, L0_attn_b_in_w, L0_attn_b_conv_w, L0_attn_b_conv_b, L0_attn_b_xproj_w, L0_attn_b_dt_w, L0_attn_b_dt_b, L0_attn_b_A_log, L0_attn_b_D, L0_attn_b_out_w)
    h = h + _L0_ffn_ref(_layernorm(h, axis=-1), L0_ffn_U1, L0_ffn_V1, L0_ffn_b1, L0_ffn_U2, L0_ffn_V2, L0_ffn_b2)
    return h

_drawn_inputs = setup_inputs


def setup_inputs(seed=0):
    import zlib

    import numpy as np

    out = dict(_drawn_inputs(seed))
    spreads = {'L0_tok_bq': (0.0, 0.8),
     'L0_tok_bk': (0.0, 0.8),
     'L0_tok_bv': (0.0, 0.1),
     'L0_tok_bo': (0.0, 0.1),
     'L0_attn_f_conv_b': (0.0, 0.464),
     'L0_attn_f_D': (1.0, 0.6),
     'L0_attn_b_conv_b': (0.0, 0.435),
     'L0_attn_b_D': (1.0, 0.6),
     'L0_ffn_b1': (0.0, 0.303),
     'L0_ffn_b2': (0.0, 0.1)}
    factors = {'L0_tok_wq': 8.0,
     'L0_tok_wk': 8.0,
     'L0_attn_f_in_w': 3.046,
     'L0_attn_f_conv_w': 8.0,
     'L0_attn_f_xproj_w': 8.0,
     'L0_attn_f_dt_w': 8.0,
     'L0_attn_f_dt_b': 8.0,
     'L0_attn_f_A_log': 8.0,
     'L0_attn_f_out_w': 3.27,
     'L0_attn_b_in_w': 2.849,
     'L0_attn_b_conv_w': 8.0,
     'L0_attn_b_xproj_w': 8.0,
     'L0_attn_b_dt_w': 8.0,
     'L0_attn_b_dt_b': 8.0,
     'L0_attn_b_A_log': 8.0,
     'L0_attn_b_out_w': 2.921,
     'L0_ffn_U1': 5.295,
     'L0_ffn_V1': 4.429}
    for name, (base, spread) in spreads.items():
        noise = np.random.default_rng([zlib.crc32(name.encode()), seed]).standard_normal(out[name].shape)
        drawn = base * np.exp(spread * noise) if base else spread * noise
        out[name] = jnp.asarray(drawn.astype(out[name].dtype))
    for name, factor in factors.items():
        out[name] = (out[name] * factor).astype(out[name].dtype)
    return out
```

```python
import concourse.bass as bass
from concourse import mybir
from contextlib import ExitStack, contextmanager
import numpy as np

FP32 = mybir.dt.float32
BF16 = mybir.dt.bfloat16
I32 = mybir.dt.int32
U32 = mybir.dt.uint32
ALU = mybir.AluOpType
ACT = mybir.ActivationFunctionType
AX = mybir.AxisListType

P = 128
B, S, D = 2, 2048, 256
T = B * S
VOCAB = 8000
H, DK = 16, 16
HG = 4
G = B * H // HG
PARTS = 3
Q_PART = [0, 0, 1, 1, 0, 2, 1]
K_PART = [0, 1, 0, 1, 2, 0, 2]
KQ = DK * len(Q_PART)
KQM = KQ + PARTS
CH = 512
NC = S // CH
NT = S // P
KD = D // P
VW = 32
LN_EPS = 1e-5
DI, DS, DC, R = 512, 16, 4, 16
ND = DI // P
TC = 1024
X_B, X_C, X_DT = 0, 32, 64
X_BC = (X_B, X_C)
XPW = X_DT + R
FF, RK = 1024, 64
TWO_BF16_ONES = float(np.array([0x3F803F80], np.uint32).view(np.float32)[0])


ONE = 1



@contextmanager
def semaphores(nc):
    taken = []

    def sem(name, start=ONE):
        taken.append(nc.alloc_semaphore(name=name))
        if start:
            nc.sync.sem_inc(taken[-1], start)
        return taken[-1]

    yield sem
    nc.clear_and_free_semaphores(taken)
    nc.all_engine_barrier()


def identity(pool, tile, cleared, done):
    pool.memset(tile, 0.0).then_inc(cleared, 1)
    pool.wait_ge(cleared, ONE + 1)
    pool.affine_select(out=tile, in_=tile, compare_op=ALU.not_equal, fill=1.0, base=0,
                       pattern=[[-1, tile.shape[1]]], channel_multiplier=1).then_inc(done, 1)


def embed_and_project(nc, sem, x, emb, weights, biases, q_scr, k_scr, v_all):
    with ExitStack() as ctx:
        def sb(name, shape, dt):
            return ctx.enter_context(nc.sbuf_tensor(name, shape, dt))

        def pb(name, shape, dt):
            return ctx.enter_context(nc.psum_tensor(name, shape, dt))

        ident = sb("p_ident", [P, P], FP32)
        w_sb = [sb(f"p_w{n}", [P, KD, D], FP32) for n in "qkv"]
        b_col = [sb(f"p_b{n}", [P, KD], FP32) for n in "qk"]
        bv_row = sb("p_bv", [P, D], FP32)
        NI = T // P
        ids_i = sb("p_ids_i", [NI, P], I32)
        ids_f = sb("p_ids_f", [NI, 4, P], FP32)
        ids_t = sb("p_ids_t", [P, NI], U32)
        ids_c = sb("p_ids_c", [P, 2, 4], U32)
        rows = sb("p_rows", [P, 2, 4, D], FP32)
        hT = sb("p_hT", [P, 2, KD, CH], FP32)
        full = [sb(f"p_full{n}", [P, KD, CH], FP32) for n in "qk"]
        rest = sb("p_rest", [P, KD, CH], FP32)
        parts = [sb(f"p_parts{n}", [P, 2, PARTS, KD, CH], BF16) for n in "qk"]
        ps_t = pb("p_ps_t", [P, KD, CH], FP32)
        ps_qk = [pb(f"p_ps_{n}", [P, KD, CH], FP32) for n in "qk"]
        ps_v = pb("p_ps_v", [P, 4, D], FP32)

        ids_in = sem("ids_in")
        w_in = sem("w_in")
        cleared, ident_ok = sem("p_cleared"), sem("p_ident_ok")
        ids_step, ids_col, ids_ok = sem("ids_step"), sem("ids_col"), sem("ids_ok")
        ids_copied = sem("ids_copied")
        rows_in = [sem("rows_in0", 0), sem("rows_in1", 0)]
        rows_free = sem("rows_free")
        ht_ps, ht_ok = sem("ht_ps"), sem("ht_ok")
        mm_done = [sem("q_mm"), sem("k_mm")]
        v_mm, v_ok = sem("v_mm"), sem("v_ok")
        full_ok = [sem("q_full"), sem("k_full")]
        step = sem("p_split_step")
        parts_ok = [sem("q_parts"), sem("k_parts")]
        stored = [[sem(f"{n}_stored{p}") for p in range(2)] for n in "qk"]

        def chunks(eng):
            with eng.Fori(0, B) as b:
                with eng.Fori(0, NC // 2) as j:
                    for buf in range(2):
                        yield b, j * 2 + buf, b * NC + j * 2 + buf, buf

        with nc.Block() as block:
            @block.sync
            def _(sp):
                sp.dma_start(ids_i[:, :], x.rearrange("b (n p) -> (b n) p", p=P)).then_inc(ids_in, 16)
                for w, src in zip(w_sb, weights):
                    sp.dma_start(w[:, :, :], src.rearrange("(k p) n -> p k n", p=P)).then_inc(w_in, 16)
                for bc, src in zip(b_col, biases):
                    sp.dma_start(bc[:, :], src.rearrange("(k p) -> p k", p=P),
                                 allow_slow_non_contiguous=True).then_inc(w_in, 16)
                sp.dma_start(bv_row[:, :], biases[2].partition_broadcast(P)).then_inc(w_in, 16)
                for b, c, n, buf in chunks(sp):
                    for a, scr in enumerate((q_scr, k_scr)):
                        sp.wait_ge(parts_ok[a], ONE + n + 1)
                        for i in range(PARTS):
                            dst = scr[i, bass.ds(b, 1), :, bass.ds(c * CH, CH)].rearrange("b (k p) s -> p (b k) s", p=P)
                            sp.dma_start(dst, parts[a][:, buf, i]).then_inc(stored[a][buf], 16)
                for a in range(2):
                    for buf in range(2):
                        sp.wait_ge(stored[a][buf], ONE + 16 * PARTS * B * NC // 2)

            @block.gpsimd
            def _(pool):
                identity(nc.gpsimd, ident[:, :], cleared, ident_ok)
                for b, c, n, buf in chunks(pool):
                    pool.wait_ge(rows_free, ONE + n + 1)
                    pool.wait_ge(ids_ok, ONE + 1)
                    nc.gpsimd.tensor_copy(ids_c[:, buf], ids_t[:, bass.ds(n * 4, 4)]).then_inc(ids_copied, 1)
                    pool.wait_ge(ids_copied, ONE + n + 1)
                    pool.nop(nofuse=True)
                    for t in range(4):
                        nc.gpsimd.indirect_dma_start(
                            rows[:, buf, t], None, emb,
                            bass.IndirectOffsetOnAxis(ids_c[:, buf, t:t + 1], 0)).then_inc(rows_in[buf], 16)

            @block.tensor
            def _(pe):
                pe.wait_ge(ident_ok, ONE + 1)
                pe.wait_ge(ids_step, ONE + 4)
                nc.tensor.transpose(ps_t[:, 0, 0:NI], ids_f[:, 3], ident[0:NI, 0:NI]).then_inc(ids_col, 1)
                pe.wait_ge(ids_ok, ONE + 1)
                pe.wait_ge(w_in, ONE + 96)
                pe.sem_inc(rows_free, 2)
                for b, c, n, buf in chunks(pe):
                    pe.wait_ge(rows_in[buf], (n - buf) * 32 + 64)
                    pe.wait_ge(ht_ok, ONE + n)
                    for t in range(4):
                        for k in range(KD):
                            last = nc.tensor.transpose(ps_t[:, k, t * P:(t + 1) * P],
                                                       rows[:, buf, t, k * P:(k + 1) * P], ident[:, :])
                            if t == 3 and k == KD - 1:
                                last.then_inc(ht_ps, 1)
                    pe.wait_ge(ht_ps, ONE + n + 1)
                    pe.sem_inc(rows_free, 1)
                    pe.wait_ge(ht_ok, ONE + n + 1)
                    for a in range(2):
                        pe.wait_ge(full_ok[a], ONE + KD * n)
                        for m in range(KD):
                            for k in range(KD):
                                last = nc.tensor.matmul(ps_qk[a][:, m], w_sb[a][:, k, m * P:(m + 1) * P],
                                                        hT[:, buf, k], start=k == 0, stop=k == KD - 1)
                        last.then_inc(mm_done[a], 1)
                    pe.wait_ge(v_ok, ONE + n)
                    for t in range(4):
                        for k in range(KD):
                            last = nc.tensor.matmul(ps_v[:, t], hT[:, buf, k, t * P:(t + 1) * P], w_sb[2][:, k],
                                                    start=k == 0, stop=k == KD - 1)
                    last.then_inc(v_mm, 1)

            @block.scalar
            def _(act):
                act.wait_ge(w_in, ONE + 96)
                for b, c, n, buf in chunks(act):
                    act.wait_ge(ht_ps, ONE + n + 1)
                    nc.scalar.activation(hT[:, buf], ps_t[:, :, :], ACT.Copy).then_inc(ht_ok, 1)
                    for a in range(2):
                        act.wait_ge(mm_done[a], ONE + n + 1)
                        act.wait_ge(parts_ok[a], ONE + n)
                        for m in range(KD):
                            nc.scalar.activation(full[a][:, m], ps_qk[a][:, m], ACT.Identity,
                                                 bias=b_col[a][:, m:m + 1]).then_inc(full_ok[a], 1)

            @block.vector
            def _(dve):
                dve.wait_ge(ids_in, ONE + 16)
                nc.vector.tensor_copy(ids_f[:, 0], ids_i[:, :]).then_inc(ids_step, 1)
                dve.wait_ge(ids_step, ONE + 1)
                nc.vector.tensor_scalar(ids_f[:, 1], ids_f[:, 0], 0.0, float(VOCAB), ALU.is_lt, ALU.mult).then_inc(ids_step, 1)
                dve.wait_ge(ids_step, ONE + 2)
                nc.vector.tensor_tensor(ids_f[:, 2], ids_f[:, 0], ids_f[:, 1], ALU.add).then_inc(ids_step, 1)
                dve.wait_ge(ids_step, ONE + 3)
                nc.vector.tensor_scalar(ids_f[:, 3], ids_f[:, 2], float(VOCAB - 1), 0.0, ALU.min, ALU.max).then_inc(ids_step, 1)
                dve.wait_ge(ids_col, ONE + 1)
                nc.vector.tensor_copy(ids_t[:, :], ps_t[:, 0, 0:NI]).then_inc(ids_ok, 1)
                dve.wait_ge(w_in, ONE + 96)
                for b, c, n, buf in chunks(dve):
                    for a in range(2):
                        dve.wait_ge(full_ok[a], ONE + KD * n + KD)
                        dve.wait_ge(stored[a][buf], ONE + (n - buf) * 8 * PARTS)
                        part = [parts[a][:, buf, i] for i in range(PARTS)]
                        done = (n * 2 + a) * 3
                        nc.vector.tensor_copy(part[0], full[a][:, :, :]).then_inc(step, 1)
                        dve.wait_ge(step, ONE + done + 1)
                        nc.vector.tensor_tensor(rest[:, :, :], full[a][:, :, :], part[0], ALU.subtract).then_inc(step, 1)
                        dve.wait_ge(step, ONE + done + 2)
                        nc.vector.tensor_copy(part[1], rest[:, :, :]).then_inc(step, 1)
                        dve.wait_ge(step, ONE + done + 3)
                        nc.vector.tensor_tensor(part[2], rest[:, :, :], part[1], ALU.subtract).then_inc(parts_ok[a], 1)
                        dve.wait_ge(parts_ok[a], ONE + n + 1)
                    dve.wait_ge(v_mm, ONE + n + 1)
                    for g in range(H // HG):
                        cols = slice(g * HG * DK, (g + 1) * HG * DK)
                        last = nc.vector.tensor_tensor(
                            v_all[:, bass.ds(b, 1), g, bass.ds(c * 4, 4)].rearrange("p b t d -> p (b t) d"),
                            ps_v[:, :, cols],
                            bv_row[:, None, cols].to_broadcast([P, 4, HG * DK]), ALU.add)
                    last.then_inc(v_ok, 1)


def attention(nc, sem, q_scr, k_scr, v_all, o_scr):
    with ExitStack() as ctx:
        def sb(name, shape, dt):
            return ctx.enter_context(nc.sbuf_tensor(name, shape, dt))

        def pb(name, shape, dt):
            return ctx.enter_context(nc.psum_tensor(name, shape, dt))

        k_st = sb("a_k", [P, 2, HG, S], BF16)
        q_st = sb("a_q", [P, 2, NC, HG, CH], BF16)
        v_st = sb("a_v", [P, 2, NT, HG, VW], FP32)
        probs = sb("a_probs", [P, 2, HG, CH], FP32)
        o_sb = sb("a_o", [P, 2, CH], FP32)
        ident = sb("a_ident", [P, P], BF16)
        NM = HG * NC
        mx = sb("a_mx", [P, NM, NC], FP32)
        neg = sb("a_neg", [P, NM], FP32)
        neg_rest = sb("a_neg_rest", [P, NM], FP32)
        neg_parts = sb("a_neg_parts", [P, PARTS, NM], BF16)
        neg_rows = sb("a_neg_rows", [PARTS * NM, P], BF16)
        ps_s = [pb(f"a_ps_s{i}", [P, 2, CH], FP32) for i in range(2)]
        ps_m = [pb(f"a_ps_m{i}", [P, CH], FP32) for i in range(2)]
        ps_o = pb("a_ps_o", [P, CH], FP32)
        ps_n = pb("a_ps_n", [PARTS * NM, P], BF16)

        a_cleared, a_ident_ok = sem("a_cleared"), sem("a_ident_ok")
        consts = sem("a_consts")
        ones_ok = sem("ones_ok")
        loaded = [[sem(f"loaded{p}{h}") for h in range(HG)] for p in range(2)]
        v_staged = sem("v_staged")
        scored = sem("scored")
        exped = sem("exped")
        pv_done = sem("pv_done")
        o_copied = sem("o_copied")
        o_stored = sem("o_stored")
        m_scored = sem("m_scored")
        m_maxed = sem("m_maxed")
        neg_ok = sem("neg_ok")
        neg_step, neg_split = sem("neg_step"), sem("neg_split")
        neg_ps, neg_t, neg_in = sem("neg_ps"), sem("neg_t"), sem("neg_in")

        BLK = NM * NC

        def groups(eng, body):
            with eng.Fori(0, (G - 2) // 2) as i:
                for buf in range(2):
                    body(i * 2 + buf, buf, False)
            body(G - 2, 0, False)
            body(G - 1, 1, True)

        with nc.Block() as block:
            @block.sync
            def _(sp):
                def load(g, buf):
                    for h in range(HG):
                        for stack, scr, part in ((k_st, k_scr, K_PART), (q_st, q_scr, Q_PART)):
                            src = scr.rearrange("a b (g h d) s -> a (b g) h d s", h=HG, d=DK)
                            for i, a in enumerate(part):
                                rows = src[a, bass.ds(g, 1), h].rearrange("g d s -> (g d) s")
                                dst = stack[i * DK:(i + 1) * DK, buf]
                                if stack is k_st:
                                    sp.dma_start(dst[:, h], rows).then_inc(loaded[buf][h], 16)
                                else:
                                    sp.dma_start(dst[:, :, h], rows.rearrange("d (c s) -> d c s", s=CH)
                                                 ).then_inc(loaded[buf][h], 16)

                def store_neg(m, buf, c):
                    sp.wait_ge(neg_t, ONE + m + 1)
                    for i in range(PARTS):
                        dst = q_st[KQ + i:KQ + i + 1, buf, bass.ds(c, 1)].rearrange("a c h (s n) -> a (c h s) n", n=P)
                        sp.dma_start(dst, neg_rows[i * NM:(i + 1) * NM, :]).then_inc(neg_in, 16)
                    sp.wait_ge(neg_in, ONE + 16 * PARTS * (m + 1))
                    sp.nop(nofuse=True)

                sp.wait_ge(ones_ok, ONE + 1)
                load(0, 0)
                sp.wait_ge(ones_ok, ONE + 2)
                load(1, 1)
                with sp.Fori(0, NC) as c:
                    store_neg(c, 0, c)

                def body(g, buf, last):
                    if not last:
                        with sp.Fori(0, NC - 1) as c:
                            store_neg(g * NC + NC + c, 1 - buf, c)
                    sp.wait_ge(scored, ONE + (g + 1) * NC * NT * 2)
                    if not last and not (isinstance(g, int) and g == G - 2):
                        load(g + 2, buf)
                    if not last:
                        store_neg(g * NC + NC + NC - 1, 1 - buf, NC - 1)
                groups(sp, body)

            @block.gpsimd
            def _(pool):
                nc.gpsimd.memset(v_st[:, :, :, :, :], 0.0).then_inc(consts, 1)
                pool.wait_ge(consts, ONE + 1)
                nc.gpsimd.memset(v_st[:, :, :, :, DK:DK + 1], 1.0).then_inc(consts, 1)
                pool.wait_ge(consts, ONE + 2)
                identity(nc.gpsimd, ident[:, :], a_cleared, a_ident_ok)
                pool.wait_ge(a_ident_ok, ONE + 1)

                def stage_v(g, buf):
                    pool.nop(nofuse=True)
                    nc.gpsimd.tensor_copy(
                        v_st[:, buf, :, :, 0:DK],
                        v_all.rearrange("p b g t (h d) -> p (b g) t h d", d=DK)[:, bass.ds(g, 1)]
                        .rearrange("p g t h d -> p (g t) h d")).then_inc(v_staged, 1)

                def split(m):
                    pool.wait_ge(neg_ok, ONE + m + 1)
                    pool.wait_ge(neg_ps, ONE + m)
                    pool.nop(nofuse=True)
                    nc.gpsimd.tensor_copy(neg_parts[:, 0], neg[:, :]).then_inc(neg_step, 1)
                    pool.wait_ge(neg_step, ONE + m * 3 + 1)
                    nc.gpsimd.tensor_tensor(neg_rest[:, :], neg[:, :], neg_parts[:, 0], ALU.subtract).then_inc(neg_step, 1)
                    pool.wait_ge(neg_step, ONE + m * 3 + 2)
                    pool.nop(nofuse=True)
                    nc.gpsimd.tensor_copy(neg_parts[:, 1], neg_rest[:, :]).then_inc(neg_step, 1)
                    pool.wait_ge(neg_step, ONE + m * 3 + 3)
                    nc.gpsimd.tensor_tensor(neg_parts[:, 2], neg_rest[:, :], neg_parts[:, 1], ALU.subtract).then_inc(neg_split, 1)
                    pool.wait_ge(neg_split, ONE + m + 1)

                stage_v(0, 0)
                with pool.Fori(0, NC) as c:
                    split(c)

                def body(g, buf, last):
                    if not last:
                        pool.wait_ge(pv_done, ONE + g * NC * NT)
                        pool.nop(nofuse=True)
                        stage_v(g + 1, 1 - buf)
                        with pool.Fori(0, NC) as c:
                            split(g * NC + NC + c)
                groups(pool, body)

            @block.tensor
            def _(pe):
                def max_blocks(m, buf, c, first, end, loads=None):
                    for i in range(first, end):
                        h, st, tc = i // 16, i // 4 % 4, i % 4
                        if i % 16 == 0 and loads is not None:
                            pe.wait_ge(loaded[buf][h], ONE + loads)
                        pe.wait_ge(m_maxed, ONE + m * BLK + i + 1)
                        nc.tensor.matmul(ps_m[i % 2][:, :], q_st[0:KQ, buf, bass.ds(c, 1), h, st * P:(st + 1) * P].rearrange("p c n -> p (c n)"),
                                         k_st[0:KQ, buf, h, tc * CH:(tc + 1) * CH],
                                         start=True, stop=True).then_inc(m_scored, 1)

                def transpose_neg(m):
                    pe.wait_ge(neg_split, ONE + m + 1)
                    pe.wait_ge(neg_t, ONE + m)
                    pe.nop(nofuse=True)
                    nc.tensor.transpose(ps_n[:, :], neg_parts[:, :, :].rearrange("p a m -> p (a m)"),
                                        ident[:, :]).then_inc(neg_ps, 1)

                def chunk(g, buf, c, with_max, with_neg):
                    e = g * NC + c
                    pe.wait_ge(neg_in, ONE + 16 * PARTS * (e + 1))
                    taken = 0

                    def maxima(n):
                        nonlocal taken
                        if with_max:
                            loads = 16 * len(Q_PART) * (g + (3 if buf else 2))
                            max_blocks(e + NC, 1 - buf, c, taken, min(taken + n, BLK), loads)
                            taken = min(taken + n, BLK)

                    for t in range(NT + 1):
                        if t < NT:
                            for half in range(2):
                                n = e * NT * 2 + t * 2 + half
                                pe.wait_ge(exped, ONE + n + 1)
                                for h in (2 * half, 2 * half + 1):
                                    last = nc.tensor.matmul(ps_s[half][:, h % 2], k_st[0:KQM, buf, h, t * P:(t + 1) * P],
                                                            q_st[0:KQM, buf, bass.ds(c, 1), h].rearrange("p c n -> p (c n)"),
                                                            start=True, stop=True)
                                last.then_inc(scored, 1)
                                if t > 0:
                                    maxima(1)
                        if with_neg and t == 3:
                            transpose_neg(e + NC - 1)
                        if t > 0:
                            if t == 1:
                                pe.wait_ge(o_copied, ONE + e)
                            pe.wait_ge(exped, ONE + e * NT * 2 + t * 2 + 2)
                            for h in range(HG):
                                last = nc.tensor.matmul(ps_o[h * VW:(h + 1) * VW, :], v_st[:, buf, t - 1, h],
                                                        probs[:, (t - 1) % 2, h], start=t == 1, stop=t == NT)
                            last.then_inc(pv_done, 1)
                            maxima(3 if t in (2, 5, 8, 11) else 2)

                pe.wait_ge(a_ident_ok, ONE + 1)
                pe.wait_ge(consts, ONE + 2)
                max_blocks(0, 0, 0, 0, BLK, 16 * 2 * len(Q_PART))
                with pe.Fori(1, NC) as c:
                    transpose_neg(c - 1)
                    max_blocks(c, 0, c, 0, BLK)

                def body(g, buf, last):
                    pe.wait_ge(v_staged, ONE + g + 1)
                    pe.nop(nofuse=True)
                    if last:
                        chunk(g, buf, 0, False, True)
                        with pe.Fori(1, NC) as c:
                            chunk(g, buf, c, False, False)
                    else:
                        with pe.Fori(0, NC) as c:
                            chunk(g, buf, c, True, True)
                groups(pe, body)

            @block.scalar
            def _(act):
                def copy_neg(m):
                    act.wait_ge(neg_ps, ONE + m + 1)
                    act.wait_ge(neg_in, ONE + 16 * PARTS * m)
                    nc.scalar.activation(neg_rows[:, :], ps_n[:, :], ACT.Copy).then_inc(neg_t, 1)

                def copy_out(g, c):
                    e = g * NC + c
                    act.wait_ge(pv_done, ONE + NT * (e + 1))
                    act.wait_ge(o_stored, ONE + 16 * HG * e)
                    nc.scalar.activation(o_sb[:, 0], ps_o[:, :], ACT.Copy).then_inc(o_copied, 1)
                    act.wait_ge(o_copied, ONE + e + 1)
                    for h in range(HG):
                        act.dma_start(o_scr[bass.ds(g, 1), h, :, bass.ds(c * CH, CH)].rearrange("g r s -> (g r) s"),
                                      o_sb[h * VW:h * VW + DK + 1, 0]).then_inc(o_stored, 16)

                def chunk(g, c, with_neg):
                    e = g * NC + c
                    for t in range(NT):
                        if with_neg and t == 4:
                            copy_neg(e + NC - 1)
                        if t >= 2:
                            act.wait_ge(pv_done, ONE + e * NT + t - 1)
                        for half in range(2):
                            act.wait_ge(scored, ONE + e * NT * 2 + t * 2 + half + 1)
                            nc.scalar.activation(probs[:, t % 2, 2 * half:2 * half + 2], ps_s[half][:, :, :], ACT.Exp,
                                                 scale=float(DK) ** -0.5).then_inc(exped, 1)
                    copy_out(g, c)

                act.sem_inc(exped, 2)
                with act.Fori(0, NC - 1) as c:
                    copy_neg(c)

                def body(g, buf, last):
                    if last:
                        chunk(g, 0, True)
                        with act.Fori(1, NC) as c:
                            chunk(g, c, False)
                    else:
                        with act.Fori(0, NC) as c:
                            chunk(g, c, True)
                groups(act, body)
                act.wait_ge(o_stored, ONE + 16 * HG * G * NC)

            @block.vector
            def _(dve):
                def maxima(m):
                    for i in range(BLK):
                        dve.wait_ge(m_scored, ONE + m * BLK + i + 1)
                        if i == 0:
                            dve.wait_ge(neg_ok, ONE + m)
                        nc.vector.reduce_max(mx[:, i // NC, i % NC:i % NC + 1], ps_m[i % 2][:, :], AX.X).then_inc(m_maxed, 1)
                    dve.wait_ge(m_maxed, ONE + m * BLK + BLK + 2)
                    dve.wait_ge(neg_split, ONE + m)
                    nc.vector.reduce_max(neg[:, :], mx[:, :, :], AX.X, negate=True).then_inc(neg_ok, 1)

                for buf in range(2):
                    nc.vector.memset(k_st[96:128, buf].rearrange("p h s -> p (h s)").bitcast(FP32),
                                     TWO_BF16_ONES).then_inc(ones_ok, 1)
                dve.sem_inc(m_maxed, 2)
                with dve.Fori(0, G * NC) as m:
                    maxima(m)


def transpose_weights(nc, sem, dirs, win_scr, xp_scr, dtw_scr, ow_scr):
    with ExitStack() as ctx:
        def sb(name, shape, dt):
            return ctx.enter_context(nc.sbuf_tensor(name, shape, dt))

        ident = sb("w_ident", [P, P], FP32)
        win = sb("w_in", [P, 2, 2 * DI // P, D], FP32)
        xp = sb("w_xp", [R + 2 * DS, 2, DI], FP32)
        dtw = sb("w_dt", [P, 2, ND, R], FP32)
        ow = sb("w_out", [P, 2, KD, DI], FP32)
        win_t = sb("w_in_t", [P, 2, KD, 2 * DI], FP32)
        xp_t = sb("w_xp_t", [P, 2, ND, XPW], FP32)
        dtw_t = sb("w_dt_t", [R, 2, DI], FP32)
        ow_t = sb("w_out_t", [P, 2, ND, D], FP32)
        NB = 4
        ps = [ctx.enter_context(nc.psum_tensor(f"w_ps{i}", [P, CH], FP32)) for i in range(NB)]
        loaded, cleared, ident_ok = sem("w_loaded"), sem("w_cleared"), sem("w_ident_ok")
        pads_ok = sem("w_pads_ok")
        transposed, copied, stored = sem("w_transposed"), sem("w_copied"), sem("w_stored")

        blocks = []
        for z in range(2):
            for m in range(2 * DI // P):
                for k in range(KD):
                    blocks.append((win[:, z, m, k * P:(k + 1) * P], P, P,
                                   [(win_t[:, z, k, m * P:(m + 1) * P], 0, P)]))
            for k in range(ND):
                cols = slice(k * P, (k + 1) * P)
                blocks.append((xp[:, z, cols], R + 2 * DS, P,
                               [(xp_t[:, z, k, X_DT:X_DT + R], 0, R), (xp_t[:, z, k, X_B:X_B + DS], R, R + DS),
                                (xp_t[:, z, k, X_C:X_C + DS], R + DS, R + 2 * DS)]))
                blocks.append((dtw[:, z, k], P, R, [(dtw_t[:, z, cols], 0, P)]))
                for m in range(KD):
                    blocks.append((ow[:, z, m, cols], P, P, [(ow_t[:, z, k, m * P:(m + 1) * P], 0, P)]))

        with nc.Block() as block:
            @block.sync
            def _(sp):
                for z, w in enumerate(dirs):
                    sp.dma_start(win[:, z], w["in_w"].rearrange("(m p) k -> p m k", p=P)).then_inc(loaded, 16)
                    sp.dma_start(xp[:, z], w["xproj_w"]).then_inc(loaded, 16)
                    sp.dma_start(dtw[:, z], w["dt_w"].rearrange("(k p) r -> p k r", p=P)).then_inc(loaded, 16)
                    sp.dma_start(ow[:, z], w["out_w"].rearrange("(m p) k -> p m k", p=P)).then_inc(loaded, 16)
                sp.wait_ge(copied, ONE + len(blocks))
                for z in range(2):
                    sp.dma_start(win_scr[z].rearrange("(k p) m -> p k m", p=P), win_t[:, z]).then_inc(stored, 16)
                    sp.dma_start(xp_scr[z], xp_t[:, z]).then_inc(stored, 16)
                    sp.dma_start(dtw_scr[z], dtw_t[:, z]).then_inc(stored, 16)
                    sp.dma_start(ow_scr[z], ow_t[:, z]).then_inc(stored, 16)
                sp.wait_ge(stored, ONE + 8 * 16)

            @block.gpsimd
            def _(pool):
                identity(nc.gpsimd, ident[:, :], cleared, ident_ok)

            @block.tensor
            def _(pe):
                pe.wait_ge(ident_ok, ONE + 1)
                pe.wait_ge(loaded, ONE + 8 * 16)
                for i, (src, rows, cols, _) in enumerate(blocks):
                    if i >= NB:
                        pe.wait_ge(copied, ONE + i - NB + 1)
                    nc.tensor.transpose(ps[i % NB][0:cols, 0:rows], src, ident[0:rows, 0:rows]).then_inc(transposed, 1)

            @block.vector
            def _(dve):
                nc.vector.memset(xp_t[:, :, :, :], 0.0).then_inc(pads_ok, 1)
                dve.wait_ge(pads_ok, ONE + 1)
                for i, (_, rows, cols, dsts) in enumerate(blocks):
                    dve.wait_ge(transposed, ONE + i + 1)
                    for dst, a, b in dsts:
                        last = nc.vector.tensor_copy(dst, ps[i % NB][0:cols, a:b])
                    last.then_inc(copied, 1)


def normalize(nc, dve, h, stats, mv, std, rstd, xn, sems, n):
    step, mv_ok, std_ok, xn_ok = sems
    for t in range(4):
        last = nc.vector.bn_stats(stats[:, t], h[:, t])
    last.then_inc(step, 1)
    dve.wait_ge(step, ONE + 2 * n + 1)
    dve.nop(nofuse=True)
    for t in range(4):
        last = nc.vector.bn_aggr(mv[:, t], stats[:, t])
    last.then_inc(mv_ok, 1)
    dve.wait_ge(std_ok, ONE + n + 1)
    nc.vector.reciprocal(rstd, std).then_inc(step, 1)
    dve.wait_ge(step, ONE + 2 * n + 2)
    for t in range(4):
        last = nc.vector.tensor_scalar(xn[:, t], h[:, t], mv[:, t, 0:1], rstd[:, t:t + 1], ALU.subtract, ALU.mult)
    last.then_inc(xn_ok, 1)


def batch_chunks(eng):
    with eng.Fori(0, B) as b:
        with eng.Fori(0, NC // 2) as j:
            for buf in range(2):
                yield b, j * 2 + buf, b * NC + j * 2 + buf, buf


def attention_out(nc, sem, o_scr, wo, bo, h_scr, xn_scr):
    with ExitStack() as ctx:
        def sb(name, shape, dt):
            return ctx.enter_context(nc.sbuf_tensor(name, shape, dt))

        def pb(name, shape, dt):
            return ctx.enter_context(nc.psum_tensor(name, shape, dt))

        ident = sb("o_ident", [P, P], FP32)
        w = sb("o_w", [P, KD, D], FP32)
        bias = sb("o_bias", [P, D], FP32)
        eps = sb("o_eps", [P, 1], FP32)
        o_in = sb("o_in", [P, 2, KD, CH], FP32)
        l_in = sb("o_l", [P, 2, KD, CH], FP32)
        inv = sb("o_inv", [P, KD, CH], FP32)
        o_n = sb("o_n", [P, 2, KD, CH], FP32)
        h = sb("o_h", [P, 2, 4, D], FP32)
        xn = sb("o_xn", [P, 2, 4, D], FP32)
        xt = sb("o_xt", [P, 2, KD, CH], FP32)
        stats = sb("o_stats", [P, 4, 6], FP32)
        mv = sb("o_mv", [P, 4, 2], FP32)
        std, rstd = sb("o_std", [P, 4], FP32), sb("o_rstd", [P, 4], FP32)
        ps_h = pb("o_ps_h", [P, 2, 4, D], FP32)
        ps_t = pb("o_ps_t", [P, 2, KD, CH], FP32)

        w_in, cleared, ident_ok = sem("o_w_in"), sem("o_cleared"), sem("o_ident_ok")
        in_ok = [sem("o_in0"), sem("o_in1")]
        inv_ok, on_ok, h_ps, h_ok = sem("o_inv_ok"), sem("o_on_ok"), sem("o_h_ps"), sem("o_h_ok")
        step, mv_ok, std_ok, xn_ok = sem("o_step"), sem("o_mv_ok"), sem("o_std_ok"), sem("o_xn_ok")
        eps_ok = sem("o_eps_ok")
        t_ps, t_ok = sem("o_t_ps"), sem("o_t_ok")
        h_stored, x_stored = [sem("o_hs0"), sem("o_hs1")], [sem("o_xs0"), sem("o_xs1")]

        with nc.Block() as block:
            @block.sync
            def _(sp):
                sp.dma_start(w[:, :, :], wo.rearrange("(k p) n -> p k n", p=P)).then_inc(w_in, 16)
                sp.dma_start(bias[:, :], bo.partition_broadcast(P)).then_inc(w_in, 16)
                heads = P // DK
                for b, c, n, buf in batch_chunks(sp):
                    sp.wait_ge(on_ok, ONE + n - buf)
                    for m in range(KD):
                        src = o_scr.rearrange("(b g) h r s -> b (g h) r s", b=B)[bass.ds(b, 1), m * heads:(m + 1) * heads, :,
                                                                               bass.ds(c * CH, CH)]
                        src = src.rearrange("b h r s -> (b h) r s")
                        sp.dma_start(o_in[:, buf, m], src[:, 0:DK]).then_inc(in_ok[buf], 16)
                        sp.dma_start(l_in[:, buf, m], src[:, DK:DK + 1].to_broadcast([heads, DK, CH])
                                     ).then_inc(in_ok[buf], 16)

            @block.gpsimd
            def _(pool):
                identity(nc.gpsimd, ident[:, :], cleared, ident_ok)
                nc.gpsimd.memset(eps[:, :], LN_EPS).then_inc(eps_ok, 1)

            @block.tensor
            def _(pe):
                pe.wait_ge(w_in, ONE + 32)
                pe.wait_ge(ident_ok, ONE + 1)

                def transposes(n, buf):
                    pe.wait_ge(xn_ok, ONE + n + 1)
                    for t in range(4):
                        for k in range(KD):
                            last = nc.tensor.transpose(ps_t[:, buf, k, t * P:(t + 1) * P], xn[:, buf, t, k * P:(k + 1) * P],
                                                       ident[:, :])
                    last.then_inc(t_ps, 1)

                for b, c, n, buf in batch_chunks(pe):
                    pe.wait_ge(on_ok, ONE + n + 1)
                    pe.wait_ge(h_ok, ONE + n - buf)
                    for t in range(4):
                        for k in range(KD):
                            last = nc.tensor.matmul(ps_h[:, buf, t], o_n[:, buf, k, t * P:(t + 1) * P], w[:, k],
                                                    start=k == 0, stop=k == KD - 1)
                    last.then_inc(h_ps, 1)
                    pe.wait_ge(t_ok, ONE + n - buf)
                    transposes(n, buf)

            @block.scalar
            def _(act):
                act.wait_ge(eps_ok, ONE + 1)
                for b, c, n, buf in batch_chunks(act):
                    act.wait_ge(mv_ok, ONE + n + 1)
                    nc.scalar.activation(std[:, :], mv[:, :, 1], ACT.Sqrt, bias=eps[:, :]).then_inc(std_ok, 1)
                    act.wait_ge(t_ps, ONE + n + 1)
                    act.wait_ge(x_stored[buf], ONE + (n - buf) * 8)
                    nc.scalar.activation(xt[:, buf], ps_t[:, buf], ACT.Copy).then_inc(t_ok, 1)
                    act.dma_start(h_scr[bass.ds(n * 4, 4)].rearrange("t p d -> p t d"), h[:, buf]).then_inc(h_stored[buf], 16)
                    act.wait_ge(t_ok, ONE + n + 1)
                    act.dma_start(xn_scr[bass.ds(b, 1), :, bass.ds(c * CH, CH)].rearrange("b (k p) s -> p (b k) s", p=P),
                                  xt[:, buf]).then_inc(x_stored[buf], 16)
                for buf in range(2):
                    act.wait_ge(h_stored[buf], ONE + 16 * B * NC // 2)
                    act.wait_ge(x_stored[buf], ONE + 16 * B * NC // 2)

            @block.vector
            def _(dve):
                dve.wait_ge(w_in, ONE + 32)
                for b, c, n, buf in batch_chunks(dve):
                    dve.wait_ge(in_ok[buf], ONE + (n - buf) * 32 + 64)
                    nc.vector.reciprocal(inv[:, :, :], l_in[:, buf]).then_inc(inv_ok, 1)
                    dve.wait_ge(inv_ok, ONE + n + 1)
                    dve.wait_ge(h_ps, ONE + n - buf)
                    nc.vector.tensor_tensor(o_n[:, buf], o_in[:, buf], inv[:, :, :], ALU.mult).then_inc(on_ok, 1)
                    dve.wait_ge(h_ps, ONE + n + 1)
                    dve.wait_ge(h_stored[buf], ONE + (n - buf) * 8)
                    nc.vector.tensor_tensor(h[:, buf], ps_h[:, buf], bias[:, None, :].to_broadcast([P, 4, D]),
                                            ALU.add).then_inc(h_ok, 1)
                    dve.wait_ge(h_ok, ONE + n + 1)
                    dve.wait_ge(t_ps, ONE + n - buf)
                    normalize(nc, dve, h[:, buf], stats, mv, std[:, :], rstd[:, :], xn[:, buf], (step, mv_ok, std_ok, xn_ok), n)


def mamba(nc, sem, tag, backward, w, win_scr, xp_scr, dtw_scr, xn_scr, y_scr):
    with ExitStack() as ctx:
        def sb(name, shape, dt):
            return ctx.enter_context(nc.sbuf_tensor(tag + name, shape, dt))

        def pb(name, shape, dt):
            return ctx.enter_context(nc.psum_tensor(tag + name, shape, dt))

        def sem_(name):
            return sem(tag + name)

        xc = sb("xc", [P, ND, S], FP32)
        zs = sb("zs", [P, ND, S], FP32)
        delta = sb("delta", [P, ND, S], FP32)
        du = sb("du", [P, ND, S], FP32)
        bc_parts = sb("bc_parts", [PARTS * DS, 2, S], BF16)
        sel = sb("sel", [PARTS * DS, DS, P], BF16)
        ident = sb("ident", [P, P], FP32)
        wxp = sb("wxp", [P, ND, XPW], FP32)
        wdt = sb("wdt", [R, DI], FP32)
        conv_w = sb("conv_w", [P, ND, DC], FP32)
        cols = sb("cols", [P, 3, ND], FP32)
        a_neg = sb("a_neg", [P, ND, DS], FP32)
        a_cur = sb("a_cur", [P, 2, DS], FP32)
        carry = sb("carry", [P, DS, 2], FP32)

        PAD = DC - 1
        XH = S + PAD + 1
        SPLIT = CH
        words = KD * S + 2 * XH + KD * 2 * DI + 2 * CH + 2 * PARTS * CH // 2 + CH
        stage = sb("stage", [P, max(words, 12 * TC)], FP32)
        at = 0

        def carve(shape):
            nonlocal at
            size = 1
            for s in shape:
                size *= s
            view = stage[:, at:at + size]
            at += size
            names = "abc"[:len(shape)]
            if len(shape) == 1:
                return view
            return view.rearrange(f"p ({' '.join(names)}) -> p {' '.join(names)}", **dict(zip(names, shape)))

        xn = carve([KD, S])
        xh = carve([2, XH])
        win = carve([KD, 2 * DI])
        dt_in = carve([2, CH])
        split = carve([2 * PARTS * CH // 2]).bitcast(BF16).rearrange("p (b a s) -> p b a s", b=2, a=PARTS)
        rest = carve([CH])
        at = 0
        bc = carve([4, TC]).rearrange("p (n i) s -> p n i s", i=2)
        da = carve([4, TC])
        hs = carve([4, TC])

        ps_y = pb("ps_y", [P, 2, TC], FP32)
        ps_bc = [pb(f"ps_bc{i}", [P, TC], FP32) for i in range(2)]
        NH = TC // CH

        w_in, cleared, ident_ok = sem_("w_in"), sem_("cleared"), sem_("ident_ok")
        sel_step, sel_ok, a_step, a_ok = sem_("sel_step"), sem_("sel_ok"), sem_("a_step"), sem_("a_ok")
        in_ok = sem_("in_ok")
        up_ps, up_ok = sem_("up_ps"), sem_("up_ok")
        pad_ok, conv_step, conv_ok, xc_ok = sem_("pad_ok"), sem_("conv_step"), sem_("conv_ok"), sem_("xc_ok")
        xp_ps, dt_ok, part1, rest_ok = sem_("xp_ps"), sem_("dt_ok"), sem_("part1"), sem_("rest_ok")
        part2, part3 = sem_("part2"), sem_("part3")
        bc_in = [sem_("bc_in0"), sem_("bc_in1")]
        dl_ps, dl_abs, dl_relu = sem_("dl_ps"), sem_("dl_abs"), sem_("dl_relu")
        dl_exp, dl_log, dl_sum, du_ok = sem_("dl_exp"), sem_("dl_log"), sem_("dl_sum"), sem_("du_ok")
        bc_ps = [sem_("b_ps"), sem_("c_ps")]
        bc_ok = [sem_("b_ok"), sem_("c_ok")]
        acur_ok, da_ok, u_ok, h_ok = sem_("acur_ok"), sem_("da_ok"), sem_("u_ok"), sem_("h_ok")
        g_ok = sem_("g_ok")
        summed = sem_("summed")
        carry_ok, y_step, y_ok, stored = sem_("carry_ok"), sem_("y_step"), sem_("y_ok"), sem_("stored")

        NCP = 2
        NTC = S // TC
        NBLK = NCP * NTC
        TILES = DS * 2

        CARRIES = 1 + NTC * TILES // 4

        def when(tc):
            return (NTC - 1) - tc if backward else tc

        def blocks(eng, before, body):
            def of_batch(b):
                with eng.Fori(0, NCP) as dp:
                    before(b, dp)
                    with eng.Fori(0, NTC) as tc:
                        body(b * NCP + dp, dp, tc, (b * NCP + dp) * NTC + tc)
            return of_batch

        def span(tile, dp, i, tc):
            return tile[:, bass.ds(dp * 2 + i, 1), bass.ds(when(tc) * TC, TC)].rearrange("p a s -> p (a s)")

        with nc.Block() as block:
            @block.sync
            def _(sp):
                sp.dma_start(wxp[:, :, :], xp_scr).then_inc(w_in, 16)
                sp.dma_start(wdt[:, :], dtw_scr).then_inc(w_in, 16)
                sp.dma_start(conv_w[:, :, :], w["conv_w"].rearrange("(k p) c -> p k c", p=P)).then_inc(w_in, 16)
                sp.dma_start(a_neg[:, :, :], w["A_log"].rearrange("(k p) n -> p k n", p=P)).then_inc(w_in, 16)
                for i, name in enumerate(("conv_b", "dt_b", "D")):
                    sp.dma_start(cols[:, i], w[name].rearrange("(k p) -> p k", p=P),
                                 allow_slow_non_contiguous=True).then_inc(w_in, 16)
                with sp.Fori(0, B) as b:
                    sp.wait_ge(y_ok, ONE + b * NBLK)
                    sp.dma_start(win, win_scr.rearrange("(k p) m -> p k m", p=P)).then_inc(in_ok, 16)
                    sp.dma_start(xn, xn_scr[bass.ds(b, 1)].rearrange("b (k p) s -> p (b k) s", p=P)).then_inc(in_ok, 16)
                    for c in range(NC):
                        sp.wait_ge(part3, ONE + b * NC + c + 1)
                        for i in range(PARTS):
                            for j in range(2):
                                sp.dma_start(bc_parts[i * DS:(i + 1) * DS, j, c * CH:(c + 1) * CH],
                                             split[X_BC[j]:X_BC[j] + DS, c % 2, i]).then_inc(bc_in[c % 2], 16)
                    sp.wait_ge(y_ok, ONE + (b + 1) * NBLK)
                    sp.dma_start(y_scr[bass.ds(b, 1)].rearrange("b (k p) s -> p (b k) s", p=P), zs[:, :, :]).then_inc(stored, 16)
                    sp.wait_ge(stored, ONE + 16 * (b + 1))
                    sp.nop(nofuse=True)

            @block.gpsimd
            def _(pool):
                identity(nc.gpsimd, ident[:, :], cleared, ident_ok)
                pool.wait_ge(ident_ok, ONE + 1)
                nc.gpsimd.memset(sel[:, :, :], 0.0).then_inc(sel_step, 1)
                for i in range(PARTS):
                    pool.wait_ge(sel_step, ONE + i + 1)
                    nc.gpsimd.affine_select(out=sel[:, :, :], in_=sel[:, :, :], compare_op=ALU.not_equal, fill=1.0,
                                            base=-i * DS, pattern=[[-1, DS], [0, P]], channel_multiplier=1
                                            ).then_inc(sel_step, 1)
                pool.wait_ge(sel_step, ONE + PARTS + 1)
                pool.sem_inc(g_ok, 4)
                pool.sem_inc(sel_ok, 1)

                def body(pair, dp, tc, q):
                    for k in range(TILES):
                        n = k // 2
                        pool.wait_ge(bc_ok[1], ONE + q * DS + n + 1)
                        pool.wait_ge(h_ok, ONE + q * TILES + k + 1)
                        nc.gpsimd.tensor_tensor(da[:, k % 4], hs[:, k % 4], bc[:, n % 2, 1], ALU.mult).then_inc(g_ok, 1)

                stage_b = blocks(pool, lambda b, dp: None, body)
                with pool.Fori(0, B) as b:
                    stage_b(b)

            @block.tensor
            def _(pe):
                def up(b, m, j):
                    for c in range(NC):
                        pe.wait_ge(up_ok, ONE + b * 8 * NC + j * NC + c + 1)
                        for k in range(KD):
                            last = nc.tensor.matmul(ps_y[:, c // NH, (c % NH) * CH:(c % NH + 1) * CH],
                                                    win[:, k, m * P:(m + 1) * P], xn[:, k, c * CH:(c + 1) * CH],
                                                    start=k == 0, stop=k == KD - 1)
                        last.then_inc(up_ps, 1)

                def spread(q, tc, n):
                    for j in range(2):
                        pe.wait_ge(bc_ok[j], ONE + q * DS + n)
                        pe.nop(nofuse=True)
                        for i in range(NH):
                            last = nc.tensor.matmul(ps_bc[j][:, i * CH:(i + 1) * CH], sel[:, n],
                                                    bc_parts[:, j, bass.ds(when(tc) * TC + i * CH, CH)],
                                                    start=True, stop=True)
                        last.then_inc(bc_ps[j], 1)

                def body(pair, dp, tc, q):
                    spread(q, tc, 0)
                    for n in range(DS):
                        if n + 1 < DS:
                            spread(q, tc, n + 1)
                        if n == 0:
                            pe.wait_ge(y_ok, ONE + q)
                        for i in range(2):
                            k = 2 * n + i
                            pe.wait_ge(g_ok, ONE + q * TILES + k + 5)
                            for c in range(NH):
                                last = nc.tensor.matmul(ps_y[:, i, c * CH:(c + 1) * CH], ident[:, :],
                                                        da[:, k % 4, c * CH:(c + 1) * CH],
                                                        start=n == 0, stop=n == DS - 1)
                            last.then_inc(summed, 1)

                stage_b = blocks(pe, lambda b, dp: None, body)
                pe.wait_ge(w_in, ONE + 7 * 16)
                pe.wait_ge(ident_ok, ONE + 1)
                pe.wait_ge(sel_ok, ONE + 1)
                pe.sem_inc(summed, 4)
                with pe.Fori(0, B) as b:
                    pe.wait_ge(in_ok, ONE + 32 * (b + 1))
                    for dt in range(ND):
                        up(b, dt, 2 * dt)
                        up(b, ND + dt, 2 * dt + 1)
                    pe.wait_ge(xc_ok, ONE + ND * (b + 1))
                    for c in range(NC):
                        pe.wait_ge(part1, ONE + b * NC + c)
                        pe.wait_ge(rest_ok, ONE + b * NC + c)
                        pe.wait_ge(dt_ok, ONE + b * NC + c)
                        for k in range(ND):
                            last = nc.tensor.matmul(ps_bc[0][0:XPW, 0:CH], wxp[:, k], xc[:, k, c * CH:(c + 1) * CH],
                                                    start=k == 0, stop=k == ND - 1)
                        last.then_inc(xp_ps, 1)
                        pe.wait_ge(dt_ok, ONE + b * NC + c + 1)
                        for dt in range(ND):
                            j = b * NC * ND + c * ND + dt
                            pe.wait_ge(dl_relu, ONE + j + 1)
                            nc.tensor.matmul(ps_bc[1][:, (dt % 2) * CH:(dt % 2 + 1) * CH], wdt[:, dt * P:(dt + 1) * P],
                                             dt_in[0:R, c % 2], start=True, stop=True).then_inc(dl_ps, 1)
                    pe.wait_ge(rest_ok, ONE + (b + 1) * NC)
                    pe.wait_ge(dl_relu, ONE + (b + 1) * NC * ND + 2)
                    for buf in range(2):
                        pe.wait_ge(bc_in[buf], ONE + (b + 1) * 16 * PARTS * 2 * NC // 2)
                    pe.nop(nofuse=True)
                    stage_b(b)

            @block.scalar
            def _(act):
                act.wait_ge(w_in, ONE + 7 * 16)
                nc.scalar.activation(a_neg[:, :, :], a_neg[:, :, :], ACT.Exp).then_inc(a_step, 1)
                act.wait_ge(a_step, ONE + 1)
                nc.scalar.activation(a_neg[:, :, :], a_neg[:, :, :], ACT.Copy, scale=-1.0).then_inc(a_ok, 1)
                act.wait_ge(a_ok, ONE + 1)
                act.sem_inc(up_ok, 4)

                def body(pair, dp, tc, q):
                    act.wait_ge(acur_ok, ONE + b * NCP + dp + 1)
                    for n in range(DS):
                        for j, used in ((0, u_ok), (1, g_ok)):
                            act.wait_ge(bc_ps[j], ONE + q * DS + n + 1)
                            act.wait_ge(used, ONE + q * TILES + 2 * max(n - 1, 0) + (4 if j else 0))
                            nc.scalar.activation(bc[:, n % 2, j], ps_bc[j][:, :], ACT.Copy).then_inc(bc_ok[j], 1)
                        for i in range(2):
                            k = 2 * n + i
                            act.wait_ge(summed, ONE + q * TILES + k + 1)
                            act.nop(nofuse=True)
                            nc.scalar.activation(da[:, k % 4], span(delta, dp, i, tc), ACT.Exp,
                                                 scale=a_cur[:, i, n:n + 1]).then_inc(da_ok, 1)

                def before(b, dp):
                    act.wait_ge(da_ok, ONE + (b * NCP + dp) * NTC * TILES)
                    act.nop(nofuse=True)
                    nc.scalar.activation(a_cur[:, :, :], a_neg[:, bass.ds(dp * 2, 2), :], ACT.Copy).then_inc(acur_ok, 1)

                stage_b = blocks(act, before, body)
                with act.Fori(0, B) as b:
                    for dt in range(ND):
                        for c in range(NC):
                            act.wait_ge(up_ps, ONE + b * 8 * NC + 2 * dt * NC + c + 1)
                            if dt >= 2 and c == 0:
                                act.wait_ge(conv_ok, ONE + b * ND + dt - 1)
                            off = (0 if backward else PAD) + c * CH
                            nc.scalar.activation(xh[:, dt % 2, off:off + CH], ps_y[:, c // NH, (c % NH) * CH:(c % NH + 1) * CH],
                                                 ACT.Copy).then_inc(up_ok, 1)
                        for c in range(NC):
                            act.wait_ge(up_ps, ONE + b * 8 * NC + (2 * dt + 1) * NC + c + 1)
                            act.wait_ge(stored, ONE + 16 * b)
                            nc.scalar.activation(zs[:, dt, c * CH:(c + 1) * CH], ps_y[:, c // NH, (c % NH) * CH:(c % NH + 1) * CH],
                                                 ACT.Silu).then_inc(up_ok, 1)
                        act.wait_ge(conv_ok, ONE + b * ND + dt + 1)
                        nc.scalar.activation(xc[:, dt], xc[:, dt], ACT.Silu).then_inc(xc_ok, 1)
                    for c in range(NC):
                        act.wait_ge(xp_ps, ONE + b * NC + c + 1)
                        act.wait_ge(dl_ps, ONE + (b * NC + c) * ND)
                        nc.scalar.activation(dt_in[0:R, c % 2], ps_bc[0][X_DT:X_DT + R, 0:CH], ACT.Copy).then_inc(dt_ok, 1)
                        if c >= 2:
                            act.wait_ge(bc_in[c % 2], ONE + b * 16 * PARTS * NC + 16 * PARTS * 2)
                        nc.scalar.activation(split[0:X_DT - 16, c % 2, 0], ps_bc[0][0:X_DT - 16, 0:CH], ACT.Copy).then_inc(part1, 1)
                        act.wait_ge(rest_ok, ONE + b * NC + c + 1)
                        nc.scalar.activation(split[0:X_DT - 16, c % 2, 1], rest[0:X_DT - 16, :], ACT.Copy).then_inc(part2, 1)
                        for dt in range(ND):
                            act.wait_ge(dl_ps, ONE + (b * NC + c) * ND + dt + 1)
                            nc.scalar.activation(delta[:, dt, c * CH:(c + 1) * CH], ps_bc[1][:, (dt % 2) * CH:(dt % 2 + 1) * CH],
                                                 ACT.Abs, bias=cols[:, 1, dt:dt + 1]).then_inc(dl_abs, 1)
                    act.wait_ge(dl_relu, ONE + (b + 1) * NC * ND + 2)
                    for dt in range(ND):
                        nc.scalar.activation(delta[:, dt], delta[:, dt], ACT.Exp, scale=-1.0).then_inc(dl_exp, 1)
                    for dt in range(ND):
                        act.wait_ge(dl_exp, ONE + b * ND + dt + 1)
                        nc.scalar.activation(delta[:, dt], delta[:, dt], ACT.Ln, bias=1.0).then_inc(dl_log, 1)
                    act.wait_ge(du_ok, ONE + (b + 1) * ND)
                    stage_b(b)

            @block.vector
            def _(dve):
                dve.wait_ge(w_in, ONE + 7 * 16)
                dve.sem_inc(dl_relu, 2)

                def body(pair, dp, tc, q):
                    first = q * TILES

                    def inputs(k):
                        dve.wait_ge(bc_ok[0], ONE + q * DS + k // 2 + 1)
                        dve.wait_ge(g_ok, ONE + first + k + 1)
                        nc.vector.tensor_tensor(hs[:, k % 4], span(du, dp, k % 2, tc), bc[:, k // 2 % 2, 0],
                                                ALU.mult).then_inc(u_ok, 1)

                    def scan(k):
                        dve.wait_ge(da_ok, ONE + first + k + 1)
                        dve.wait_ge(u_ok, ONE + first + k + 1)
                        rev = slice(None, None, -1) if backward else slice(None)
                        nc.vector.tensor_tensor_scan(hs[:, k % 4, rev], da[:, k % 4, rev], hs[:, k % 4, rev],
                                                     carry[:, k // 2, k % 2:k % 2 + 1], ALU.mult, ALU.add).then_inc(h_ok, 1)

                    dve.wait_ge(carry_ok, ONE + pair * CARRIES + 1 + tc * (TILES // 4))
                    inputs(0)
                    for k in range(TILES):
                        if k % 4 < 3:
                            inputs(k + 1)
                        scan(k)
                        if k % 4 == 3:
                            dve.wait_ge(h_ok, ONE + first + k + 1)
                            end = 0 if backward else TC - 1
                            nc.vector.tensor_copy(carry[:, k // 2 - 1:k // 2 + 1, :].rearrange("p n i -> p (n i)"),
                                                  hs[:, :, end]).then_inc(carry_ok, 1)
                            dve.wait_ge(carry_ok, ONE + pair * CARRIES + 1 + tc * (TILES // 4) + k // 4 + 1)
                            if k + 1 < TILES:
                                inputs(k + 1)
                    dve.wait_ge(summed, ONE + first + TILES + 4)
                    for i in range(2):
                        nc.vector.scalar_tensor_tensor(out=span(xc, dp, i, tc), in0=span(xc, dp, i, tc),
                                                       scalar=cols[:, 2, bass.ds(dp * 2 + i, 1)], in1=ps_y[:, i],
                                                       op0=ALU.mult, op1=ALU.add).then_inc(y_step, 1)
                    for i in range(2):
                        dve.wait_ge(y_step, ONE + q * 2 + i + 1)
                        last = nc.vector.tensor_tensor(span(zs, dp, i, tc), span(xc, dp, i, tc), span(zs, dp, i, tc), ALU.mult)
                    last.then_inc(y_ok, 1)

                def before(b, dp):
                    dve.wait_ge(carry_ok, ONE + (b * NCP + dp) * CARRIES)
                    dve.wait_ge(h_ok, ONE + (b * NCP + dp) * NTC * TILES)
                    nc.vector.memset(carry[:, :, :], 0.0).then_inc(carry_ok, 1)

                stage_b = blocks(dve, before, body)
                with dve.Fori(0, B) as b:
                    dve.wait_ge(in_ok, ONE + 32 * (b + 1))
                    pad = slice(S, S + PAD) if backward else slice(0, PAD)
                    nc.vector.memset(xh[:, :, pad], 0.0).then_inc(pad_ok, 1)
                    dve.wait_ge(pad_ok, ONE + b + 1)
                    for dt in range(ND):
                        dve.wait_ge(up_ok, ONE + b * 8 * NC + (2 * dt + 1) * NC + 4)
                        for tap in range(DC):
                            lo = PAD - tap if backward else tap
                            src = xh[:, dt % 2, lo:lo + S]
                            if tap == 0:
                                nc.vector.tensor_scalar(xc[:, dt], src, conv_w[:, dt, 0:1], cols[:, 0, dt:dt + 1],
                                                        ALU.mult, ALU.add).then_inc(conv_step, 1)
                            else:
                                dve.wait_ge(conv_step, ONE + (b * ND + dt) * (DC - 1) + tap)
                                nc.vector.scalar_tensor_tensor(out=xc[:, dt], in0=src, scalar=conv_w[:, dt, tap:tap + 1],
                                                               in1=xc[:, dt], op0=ALU.mult, op1=ALU.add
                                                               ).then_inc(conv_ok if tap == DC - 1 else conv_step, 1)
                    for c in range(NC):
                        n = b * NC + c
                        dve.wait_ge(part1, ONE + n + 1)
                        dve.wait_ge(part3, ONE + n)
                        nc.vector.tensor_tensor(rest[0:X_DT - 16, :], ps_bc[0][0:X_DT - 16, 0:CH], split[0:X_DT - 16, c % 2, 0],
                                                ALU.subtract).then_inc(rest_ok, 1)
                        dve.wait_ge(part2, ONE + n + 1)
                        nc.vector.tensor_tensor(split[0:X_DT - 16, c % 2, 2], rest[0:X_DT - 16, :], split[0:X_DT - 16, c % 2, 1],
                                                ALU.subtract).then_inc(part3, 1)
                        for dt in range(ND):
                            dve.wait_ge(dl_abs, ONE + n * ND + dt + 1)
                            nc.vector.tensor_scalar(du[:, dt, c * CH:(c + 1) * CH], ps_bc[1][:, (dt % 2) * CH:(dt % 2 + 1) * CH],
                                                    cols[:, 1, dt:dt + 1], 0.0, ALU.add, ALU.max).then_inc(dl_relu, 1)
                    dve.wait_ge(dl_relu, ONE + (b + 1) * NC * ND + 2)
                    for dt in range(ND):
                        dve.wait_ge(dl_log, ONE + b * ND + dt + 1)
                        nc.vector.tensor_tensor(delta[:, dt], delta[:, dt], du[:, dt], ALU.add).then_inc(dl_sum, 1)
                        dve.wait_ge(dl_sum, ONE + b * ND + dt + 1)
                        nc.vector.tensor_tensor(du[:, dt], delta[:, dt], xc[:, dt], ALU.mult).then_inc(du_ok, 1)
                    dve.wait_ge(du_ok, ONE + (b + 1) * ND)
                    dve.nop(nofuse=True)
                    stage_b(b)


def mamba_out_and_ffn(nc, sem, y_scr, ow_scr, h_scr, u1, v1, b1, u2, v2, b2, out):
    NF = FF // P
    NY = 2 * DI // P
    NCH = T // CH
    with ExitStack() as ctx:
        def sb(name, shape, dt):
            return ctx.enter_context(nc.sbuf_tensor("ffn_" + name, shape, dt))

        def pb(name, shape, dt):
            return ctx.enter_context(nc.psum_tensor("ffn_" + name, shape, dt))

        ident = sb("ident", [P, P], FP32)
        wo = sb("wo", [P, NY, D], FP32)
        wu1 = sb("u1", [P, KD, RK], FP32)
        wv1 = sb("v1", [RK, FF], FP32)
        bias1 = sb("b1", [P, NF], FP32)
        wu2 = sb("u2", [P, NF, RK], FP32)
        wv2 = sb("v2", [RK, D], FP32)
        bias2 = sb("b2", [P, D], FP32)
        eps = sb("eps", [P, 1], FP32)
        y = sb("y", [P, 2, NY, CH], FP32)
        h = sb("h", [P, 2, 4, D], FP32)
        xn = sb("xn", [P, 2, 4, D], FP32)
        xt = sb("xt", [P, KD, CH], FP32)
        pt = sb("pt", [RK, CH], FP32)
        hid = sb("hid", [P, 2, NF, CH], FP32)
        qt = sb("qt", [RK, CH], FP32)
        res = sb("res", [P, 2, 4, D], FP32)
        stats = sb("stats", [P, 4, 6], FP32)
        mv = sb("mv", [P, 4, 2], FP32)
        std, rstd = sb("std", [P, 4], FP32), sb("rstd", [P, 4], FP32)
        ps_h = pb("ps_h", [P, 4, D], FP32)
        ps_t = pb("ps_t", [P, KD, CH], FP32)
        ps_o = ps_t[:, :, :].rearrange("p k (t d) -> p (k t) d", d=D)
        ps_g = [pb(f"ps_g{i}", [P, CH], FP32) for i in range(2)]
        ps_p, ps_q = pb("ps_p", [RK, CH], FP32), pb("ps_q", [RK, CH], FP32)

        def s_(name, start=ONE):
            return sem("ffn_" + name, start)

        w_in, cleared, ident_ok, eps_ok = s_("w_in"), s_("cleared"), s_("ident_ok"), s_("eps_ok")
        y_in = [s_("y_in0", 0), s_("y_in1", 0)]
        h_ps, h_ok = s_("h_ps"), s_("h_ok")
        step, mv_ok, std_ok, xn_ok = s_("step"), s_("mv_ok"), s_("std_ok"), s_("xn_ok")
        t_ps, t_ok, p_ps, p_ok = s_("t_ps"), s_("t_ok"), s_("p_ps"), s_("p_ok")
        g_ps, g_ok, q_ps, q_ok, o_ps = s_("g_ps"), s_("g_ok"), s_("q_ps"), s_("q_ok"), s_("o_ps")
        hb_ok, res_ok = s_("hb_ok"), s_("res_ok")
        stored = [s_("stored0"), s_("stored1")]

        def in_steps(eng, begin, finish):
            begin(0, 0)
            with eng.Fori(0, NCH // 2 - 1) as i:
                for buf in (1, 0):
                    n = 2 * i + 2 - buf
                    begin(n, buf)
                    finish(n - 1, 1 - buf)
            begin(NCH - 1, 1)
            finish(NCH - 2, 0)
            finish(NCH - 1, 1)

        with nc.Block() as block:
            @block.sync
            def _(sp):
                for z in range(2):
                    sp.dma_start(wo[:, z * ND:(z + 1) * ND], ow_scr[z]).then_inc(w_in, 16)
                sp.dma_start(wu1[:, :, :], u1.rearrange("(k p) r -> p k r", p=P)).then_inc(w_in, 16)
                sp.dma_start(wv1[:, :], v1).then_inc(w_in, 16)
                sp.dma_start(bias1[:, :], b1.rearrange("(k p) -> p k", p=P), allow_slow_non_contiguous=True).then_inc(w_in, 16)
                sp.dma_start(wu2[:, :, :], u2.rearrange("(k p) r -> p k r", p=P)).then_inc(w_in, 16)
                sp.dma_start(wv2[:, :], v2).then_inc(w_in, 16)
                sp.dma_start(bias2[:, :], b2.partition_broadcast(P)).then_inc(w_in, 16)
                for b, c, n, buf in batch_chunks(sp):
                    sp.wait_ge(res_ok, ONE + n + 1)
                    sp.dma_start(out[bass.ds(n * 4, 4)].rearrange("t p d -> p t d"), res[:, buf]).then_inc(stored[buf], 16)
                for buf in range(2):
                    sp.wait_ge(stored[buf], ONE + 16 * NCH // 2)

            @block.gpsimd
            def _(pool):
                identity(nc.gpsimd, ident[:, :], cleared, ident_ok)
                nc.gpsimd.memset(eps[:, :], LN_EPS).then_inc(eps_ok, 1)
                for b, c, n, buf in batch_chunks(pool):
                    pool.wait_ge(h_ps, ONE + n - buf)
                    pool.wait_ge(hb_ok, ONE + n - buf)
                    for z in range(2):
                        pool.dma_start(y[:, buf, z * ND:(z + 1) * ND],
                                       y_scr[z, bass.ds(b, 1), :, bass.ds(c * CH, CH)].rearrange("b (k p) s -> p (b k) s", p=P)
                                       ).then_inc(y_in[buf], 16)
                    pool.dma_start(h[:, buf], h_scr[bass.ds(n * 4, 4)].rearrange("t p d -> p t d")).then_inc(y_in[buf], 16)

            @block.tensor
            def _(pe):
                def project(n, buf):
                    pe.wait_ge(y_in[buf], (n - buf) * 24 + 48)
                    pe.wait_ge(h_ok, ONE + n)
                    for t in range(4):
                        for k in range(NY):
                            last = nc.tensor.matmul(ps_h[:, t], y[:, buf, k, t * P:(t + 1) * P], wo[:, k],
                                                    start=k == 0, stop=k == NY - 1)
                    last.then_inc(h_ps, 1)

                def ffn(n, buf):
                    pe.wait_ge(xn_ok, ONE + n + 1)
                    pe.wait_ge(res_ok, ONE + n)
                    for t in range(4):
                        for k in range(KD):
                            last = nc.tensor.transpose(ps_t[:, k, t * P:(t + 1) * P], xn[:, buf, t, k * P:(k + 1) * P], ident[:, :])
                    last.then_inc(t_ps, 1)
                    pe.wait_ge(t_ok, ONE + n + 1)
                    for k in range(KD):
                        last = nc.tensor.matmul(ps_p[:, :], wu1[:, k], xt[:, k], start=k == 0, stop=k == KD - 1)
                    last.then_inc(p_ps, 1)
                    pe.wait_ge(p_ok, ONE + n + 1)

                    def down(k):
                        pe.wait_ge(g_ok, ONE + n * NF + k + 3)
                        return nc.tensor.matmul(ps_q[:, :], wu2[:, k], hid[:, buf, k], start=k == 0, stop=k == NF - 1)

                    for m in range(NF):
                        pe.wait_ge(g_ok, ONE + n * NF + m + 1)
                        nc.tensor.matmul(ps_g[m % 2][:, :], wv1[:, m * P:(m + 1) * P], pt[:, :], start=True, stop=True
                                         ).then_inc(g_ps, 1)
                        if m >= 2:
                            down(m - 2)
                    down(NF - 2)
                    down(NF - 1).then_inc(q_ps, 1)
                    pe.wait_ge(q_ok, ONE + n + 1)
                    for t in range(4):
                        last = nc.tensor.matmul(ps_o[:, t], qt[:, t * P:(t + 1) * P], wv2[:, :], start=True, stop=True)
                    last.then_inc(o_ps, 1)

                pe.wait_ge(w_in, ONE + 8 * 16)
                pe.wait_ge(ident_ok, ONE + 1)
                in_steps(pe, project, ffn)

            @block.scalar
            def _(act):
                def root(n, buf):
                    act.wait_ge(mv_ok, ONE + n + 1)
                    nc.scalar.activation(std[:, :], mv[:, :, 1], ACT.Sqrt, bias=eps[:, :]).then_inc(std_ok, 1)

                def ffn(n, buf):
                    act.wait_ge(t_ps, ONE + n + 1)
                    nc.scalar.activation(xt[:, :, :], ps_t[:, :, :], ACT.Copy).then_inc(t_ok, 1)
                    act.wait_ge(p_ps, ONE + n + 1)
                    nc.scalar.activation(pt[:, :], ps_p[:, :], ACT.Copy).then_inc(p_ok, 1)
                    for m in range(NF):
                        act.wait_ge(g_ps, ONE + n * NF + m + 1)
                        nc.scalar.activation(hid[:, buf, m], ps_g[m % 2][:, :], ACT.Gelu_apprx_tanh,
                                             bias=bias1[:, m:m + 1]).then_inc(g_ok, 1)
                    act.wait_ge(q_ps, ONE + n + 1)
                    nc.scalar.activation(qt[:, :], ps_q[:, :], ACT.Copy).then_inc(q_ok, 1)

                act.wait_ge(eps_ok, ONE + 1)
                act.wait_ge(w_in, ONE + 8 * 16)
                act.sem_inc(g_ok, 2)
                in_steps(act, root, ffn)

            @block.vector
            def _(dve):
                def norm(n, buf):
                    dve.wait_ge(h_ps, ONE + n + 1)
                    dve.wait_ge(y_in[buf], (n - buf) * 24 + 48)
                    nc.vector.tensor_tensor(h[:, buf], ps_h[:, :, :], h[:, buf], ALU.add).then_inc(h_ok, 1)
                    dve.wait_ge(h_ok, ONE + n + 1)
                    normalize(nc, dve, h[:, buf], stats, mv, std[:, :], rstd[:, :], xn[:, buf], (step, mv_ok, std_ok, xn_ok), n)
                    dve.wait_ge(stored[buf], ONE + (n - buf) * 8)
                    nc.vector.tensor_tensor(res[:, buf], h[:, buf], bias2[:, None, :].to_broadcast([P, 4, D]),
                                            ALU.add).then_inc(hb_ok, 1)

                def finish(n, buf):
                    dve.wait_ge(hb_ok, ONE + n + 1)
                    dve.wait_ge(o_ps, ONE + n + 1)
                    nc.vector.tensor_tensor(res[:, buf], ps_o[:, :, :], res[:, buf], ALU.add).then_inc(res_ok, 1)

                dve.wait_ge(w_in, ONE + 8 * 16)
                in_steps(dve, norm, finish)


def lm_tower(nc, a, out):
    def scratch(name, shape, dt):
        return nc.dram_tensor(name, shape, dt, kind="Internal").ap()

    q_scr = scratch("q_scr", [PARTS, B, D, S], BF16)
    k_scr = scratch("k_scr", [PARTS, B, D, S], BF16)
    o_scr = scratch("o_scr", [G, HG, DK + 1, S], FP32)
    h_scr = scratch("h_scr", [T // P, P, D], FP32)
    xn_scr = scratch("xn_scr", [B, D, S], FP32)
    y_scr = scratch("y_scr", [2, B, DI, S], FP32)
    win_scr = scratch("win_scr", [2, D, 2 * DI], FP32)
    xp_scr = scratch("xp_scr", [2, P, ND, XPW], FP32)
    dtw_scr = scratch("dtw_scr", [2, R, DI], FP32)
    ow_scr = scratch("ow_scr", [2, P, ND, D], FP32)
    names = ("in_w", "conv_w", "conv_b", "xproj_w", "dt_w", "dt_b", "A_log", "D", "out_w")
    dirs = [{n: a[f"L0_attn_{z}_{n}"] for n in names} for z in "fb"]

    with semaphores(nc) as sem:
        transpose_weights(nc, sem, dirs, win_scr, xp_scr, dtw_scr, ow_scr)
    with nc.sbuf_tensor("v_all", [P, B, H // HG, NT, HG * DK], FP32) as v_all:
        with semaphores(nc) as sem:
            embed_and_project(nc, sem, a["x"], a["L0_tok_emb"], [a[f"L0_tok_w{n}"] for n in "qkv"],
                              [a[f"L0_tok_b{n}"] for n in "qkv"], q_scr, k_scr, v_all)
        with semaphores(nc) as sem:
            attention(nc, sem, q_scr, k_scr, v_all, o_scr)
    with semaphores(nc) as sem:
        attention_out(nc, sem, o_scr, a["L0_tok_wo"], a["L0_tok_bo"], h_scr, xn_scr)
    for z in range(2):
        with semaphores(nc) as sem:
            mamba(nc, sem, "fb"[z] + "_", z == 1, dirs[z], win_scr[z], xp_scr[z], dtw_scr[z], xn_scr, y_scr[z])
    with semaphores(nc) as sem:
        mamba_out_and_ffn(nc, sem, y_scr, ow_scr, h_scr, a["L0_ffn_U1"], a["L0_ffn_V1"], a["L0_ffn_b1"],
                          a["L0_ffn_U2"], a["L0_ffn_V2"], a["L0_ffn_b2"],
                          out.rearrange("b (t p) d -> (b t) p d", p=P))


def kernel(**inputs):
    import concourse.bacc as bacc
    from concourse.bass_utils import run_bass_kernel_spmd

    nc = bacc.Bacc("TRN2", target_bir_lowering=False, num_devices=1)
    arrays, args = {}, {}
    for name, value in inputs.items():
        value = np.ascontiguousarray(value)
        arrays[f"in_{name}_dram"] = value
        args[name] = nc.dram_tensor(f"in_{name}_dram", value.shape, mybir.dt.from_np(value.dtype), kind="ExternalInput").ap()
    out = nc.dram_tensor("out_0_dram", (B, S, D), FP32, kind="ExternalOutput").ap()
    lm_tower(nc, args, out)
    result = run_bass_kernel_spmd(nc, [arrays], core_ids=[0])
    return result.results[0]["out_0_dram"]
```

```python
import concourse.bass as bass
from concourse import mybir
from contextlib import ExitStack, contextmanager
import numpy as np

FP32 = mybir.dt.float32
BF16 = mybir.dt.bfloat16
I32 = mybir.dt.int32
U32 = mybir.dt.uint32
ALU = mybir.AluOpType
ACT = mybir.ActivationFunctionType
AX = mybir.AxisListType

P = 128
B, S, D = 2, 2048, 256
T = B * S
VOCAB = 8000
H, DK = 16, 16
HG = 4
G = B * H // HG
PARTS = 3
Q_PART = [0, 0, 1, 1, 0, 2, 1]
K_PART = [0, 1, 0, 1, 2, 0, 2]
KQ = DK * len(Q_PART)
KQM = KQ + PARTS
CH = 512
NC = S // CH
NT = S // P
KD = D // P
VW = 32
LN_EPS = 1e-5
DI, DS, DC, R = 512, 16, 4, 16
ND = DI // P
TC = 1024
X_B, X_C, X_DT = 0, 32, 64
X_BC = (X_B, X_C)
XPW = X_DT + R
FF, RK = 1024, 64
TWO_BF16_ONES = float(np.array([0x3F803F80], np.uint32).view(np.float32)[0])


ONE = 1



@contextmanager
def semaphores(nc):
    taken = []

    def sem(name, start=ONE):
        taken.append(nc.alloc_semaphore(name=name))
        if start:
            nc.sync.sem_inc(taken[-1], start)
        return taken[-1]

    yield sem
    nc.clear_and_free_semaphores(taken)
    nc.all_engine_barrier()


def identity(pool, tile, cleared, done):
    pool.memset(tile, 0.0).then_inc(cleared, 1)
    pool.wait_ge(cleared, ONE + 1)
    pool.affine_select(out=tile, in_=tile, compare_op=ALU.not_equal, fill=1.0, base=0,
                       pattern=[[-1, tile.shape[1]]], channel_multiplier=1).then_inc(done, 1)


def embed_and_project(nc, sem, x, emb, weights, biases, q_scr, k_scr, v_all):
    with ExitStack() as ctx:
        def sb(name, shape, dt):
            return ctx.enter_context(nc.sbuf_tensor(name, shape, dt))

        def pb(name, shape, dt):
            return ctx.enter_context(nc.psum_tensor(name, shape, dt))

        ident = sb("p_ident", [P, P], FP32)
        w_sb = [sb(f"p_w{n}", [P, KD, D], FP32) for n in "qkv"]
        b_col = [sb(f"p_b{n}", [P, KD], FP32) for n in "qk"]
        bv_row = sb("p_bv", [P, D], FP32)
        NI = T // P
        ids_i = sb("p_ids_i", [NI, P], I32)
        ids_f = sb("p_ids_f", [NI, 4, P], FP32)
        ids_t = sb("p_ids_t", [P, NI], U32)
        ids_c = sb("p_ids_c", [P, 2, 4], U32)
        rows = sb("p_rows", [P, 2, 4, D], FP32)
        hT = sb("p_hT", [P, 2, KD, CH], FP32)
        full = [sb(f"p_full{n}", [P, KD, CH], FP32) for n in "qk"]
        rest = sb("p_rest", [P, KD, CH], FP32)
        parts = [sb(f"p_parts{n}", [P, 2, PARTS, KD, CH], BF16) for n in "qk"]
        ps_t = pb("p_ps_t", [P, KD, CH], FP32)
        ps_qk = [pb(f"p_ps_{n}", [P, KD, CH], FP32) for n in "qk"]
        ps_v = pb("p_ps_v", [P, 4, D], FP32)

        ids_in = sem("ids_in")
        w_in = sem("w_in")
        cleared, ident_ok = sem("p_cleared"), sem("p_ident_ok")
        ids_step, ids_col, ids_ok = sem("ids_step"), sem("ids_col"), sem("ids_ok")
        ids_copied = sem("ids_copied")
        rows_in = [sem("rows_in0", 0), sem("rows_in1", 0)]
        rows_free = sem("rows_free")
        ht_ps, ht_ok = sem("ht_ps"), sem("ht_ok")
        mm_done = [sem("q_mm"), sem("k_mm")]
        v_mm, v_ok = sem("v_mm"), sem("v_ok")
        full_ok = [sem("q_full"), sem("k_full")]
        step = sem("p_split_step")
        parts_ok = [sem("q_parts"), sem("k_parts")]
        stored = [[sem(f"{n}_stored{p}") for p in range(2)] for n in "qk"]

        def chunks(eng):
            with eng.Fori(0, B) as b:
                with eng.Fori(0, NC // 2) as j:
                    for buf in range(2):
                        yield b, j * 2 + buf, b * NC + j * 2 + buf, buf

        with nc.Block() as block:
            @block.sync
            def _(sp):
                sp.dma_start(ids_i[:, :], x.rearrange("b (n p) -> (b n) p", p=P)).then_inc(ids_in, 16)
                for w, src in zip(w_sb, weights):
                    sp.dma_start(w[:, :, :], src.rearrange("(k p) n -> p k n", p=P)).then_inc(w_in, 16)
                for bc, src in zip(b_col, biases):
                    sp.dma_start(bc[:, :], src.rearrange("(k p) -> p k", p=P),
                                 allow_slow_non_contiguous=True).then_inc(w_in, 16)
                sp.dma_start(bv_row[:, :], biases[2].partition_broadcast(P)).then_inc(w_in, 16)
                for b, c, n, buf in chunks(sp):
                    for a, scr in enumerate((q_scr, k_scr)):
                        sp.wait_ge(parts_ok[a], ONE + n + 1)
                        for i in range(PARTS):
                            dst = scr[i, bass.ds(b, 1), :, bass.ds(c * CH, CH)].rearrange("b (k p) s -> p (b k) s", p=P)
                            sp.dma_start(dst, parts[a][:, buf, i]).then_inc(stored[a][buf], 16)
                for a in range(2):
                    for buf in range(2):
                        sp.wait_ge(stored[a][buf], ONE + 16 * PARTS * B * NC // 2)

            @block.gpsimd
            def _(pool):
                identity(nc.gpsimd, ident[:, :], cleared, ident_ok)
                for b, c, n, buf in chunks(pool):
                    pool.wait_ge(rows_free, ONE + n + 1)
                    pool.wait_ge(ids_ok, ONE + 1)
                    nc.gpsimd.tensor_copy(ids_c[:, buf], ids_t[:, bass.ds(n * 4, 4)]).then_inc(ids_copied, 1)
                    pool.wait_ge(ids_copied, ONE + n + 1)
                    pool.nop(nofuse=True)
                    for t in range(4):
                        nc.gpsimd.indirect_dma_start(
                            rows[:, buf, t], None, emb,
                            bass.IndirectOffsetOnAxis(ids_c[:, buf, t:t + 1], 0)).then_inc(rows_in[buf], 16)

            @block.tensor
            def _(pe):
                pe.wait_ge(ident_ok, ONE + 1)
                pe.wait_ge(ids_step, ONE + 4)
                nc.tensor.transpose(ps_t[:, 0, 0:NI], ids_f[:, 3], ident[0:NI, 0:NI]).then_inc(ids_col, 1)
                pe.wait_ge(ids_ok, ONE + 1)
                pe.wait_ge(w_in, ONE + 96)
                pe.sem_inc(rows_free, 2)
                for b, c, n, buf in chunks(pe):
                    pe.wait_ge(rows_in[buf], (n - buf) * 32 + 64)
                    pe.wait_ge(ht_ok, ONE + n)
                    for t in range(4):
                        for k in range(KD):
                            last = nc.tensor.transpose(ps_t[:, k, t * P:(t + 1) * P],
                                                       rows[:, buf, t, k * P:(k + 1) * P], ident[:, :])
                            if t == 3 and k == KD - 1:
                                last.then_inc(ht_ps, 1)
                    pe.wait_ge(ht_ps, ONE + n + 1)
                    pe.sem_inc(rows_free, 1)
                    pe.wait_ge(ht_ok, ONE + n + 1)
                    for a in range(2):
                        pe.wait_ge(full_ok[a], ONE + KD * n)
                        for m in range(KD):
                            for k in range(KD):
                                last = nc.tensor.matmul(ps_qk[a][:, m], w_sb[a][:, k, m * P:(m + 1) * P],
                                                        hT[:, buf, k], start=k == 0, stop=k == KD - 1)
                        last.then_inc(mm_done[a], 1)
                    pe.wait_ge(v_ok, ONE + n)
                    for t in range(4):
                        for k in range(KD):
                            last = nc.tensor.matmul(ps_v[:, t], hT[:, buf, k, t * P:(t + 1) * P], w_sb[2][:, k],
                                                    start=k == 0, stop=k == KD - 1)
                    last.then_inc(v_mm, 1)

            @block.scalar
            def _(act):
                act.wait_ge(w_in, ONE + 96)
                for b, c, n, buf in chunks(act):
                    act.wait_ge(ht_ps, ONE + n + 1)
                    nc.scalar.activation(hT[:, buf], ps_t[:, :, :], ACT.Copy).then_inc(ht_ok, 1)
                    for a in range(2):
                        act.wait_ge(mm_done[a], ONE + n + 1)
                        act.wait_ge(parts_ok[a], ONE + n)
                        for m in range(KD):
                            nc.scalar.activation(full[a][:, m], ps_qk[a][:, m], ACT.Identity,
                                                 bias=b_col[a][:, m:m + 1]).then_inc(full_ok[a], 1)

            @block.vector
            def _(dve):
                dve.wait_ge(ids_in, ONE + 16)
                nc.vector.tensor_copy(ids_f[:, 0], ids_i[:, :]).then_inc(ids_step, 1)
                dve.wait_ge(ids_step, ONE + 1)
                nc.vector.tensor_scalar(ids_f[:, 1], ids_f[:, 0], 0.0, float(VOCAB), ALU.is_lt, ALU.mult).then_inc(ids_step, 1)
                dve.wait_ge(ids_step, ONE + 2)
                nc.vector.tensor_tensor(ids_f[:, 2], ids_f[:, 0], ids_f[:, 1], ALU.add).then_inc(ids_step, 1)
                dve.wait_ge(ids_step, ONE + 3)
                nc.vector.tensor_scalar(ids_f[:, 3], ids_f[:, 2], float(VOCAB - 1), 0.0, ALU.min, ALU.max).then_inc(ids_step, 1)
                dve.wait_ge(ids_col, ONE + 1)
                nc.vector.tensor_copy(ids_t[:, :], ps_t[:, 0, 0:NI]).then_inc(ids_ok, 1)
                dve.wait_ge(w_in, ONE + 96)
                for b, c, n, buf in chunks(dve):
                    for a in range(2):
                        dve.wait_ge(full_ok[a], ONE + KD * n + KD)
                        dve.wait_ge(stored[a][buf], ONE + (n - buf) * 8 * PARTS)
                        part = [parts[a][:, buf, i] for i in range(PARTS)]
                        done = (n * 2 + a) * 3
                        nc.vector.tensor_copy(part[0], full[a][:, :, :]).then_inc(step, 1)
                        dve.wait_ge(step, ONE + done + 1)
                        nc.vector.tensor_tensor(rest[:, :, :], full[a][:, :, :], part[0], ALU.subtract).then_inc(step, 1)
                        dve.wait_ge(step, ONE + done + 2)
                        nc.vector.tensor_copy(part[1], rest[:, :, :]).then_inc(step, 1)
                        dve.wait_ge(step, ONE + done + 3)
                        nc.vector.tensor_tensor(part[2], rest[:, :, :], part[1], ALU.subtract).then_inc(parts_ok[a], 1)
                        dve.wait_ge(parts_ok[a], ONE + n + 1)
                    dve.wait_ge(v_mm, ONE + n + 1)
                    for g in range(H // HG):
                        cols = slice(g * HG * DK, (g + 1) * HG * DK)
                        last = nc.vector.tensor_tensor(
                            v_all[:, bass.ds(b, 1), g, bass.ds(c * 4, 4)].rearrange("p b t d -> p (b t) d"),
                            ps_v[:, :, cols],
                            bv_row[:, None, cols].to_broadcast([P, 4, HG * DK]), ALU.add)
                    last.then_inc(v_ok, 1)


def attention(nc, sem, q_scr, k_scr, v_all, o_scr):
    with ExitStack() as ctx:
        def sb(name, shape, dt):
            return ctx.enter_context(nc.sbuf_tensor(name, shape, dt))

        def pb(name, shape, dt):
            return ctx.enter_context(nc.psum_tensor(name, shape, dt))

        k_st = sb("a_k", [P, 2, HG, S], BF16)
        q_st = sb("a_q", [P, 2, NC, HG, CH], BF16)
        v_st = sb("a_v", [P, 2, NT, HG, VW], FP32)
        probs = sb("a_probs", [P, 2, HG, CH], FP32)
        o_sb = sb("a_o", [P, 2, CH], FP32)
        ident = sb("a_ident", [P, P], BF16)
        NM = HG * NC
        mx = sb("a_mx", [P, NM, NC], FP32)
        neg = sb("a_neg", [P, NM], FP32)
        neg_rest = sb("a_neg_rest", [P, NM], FP32)
        neg_parts = sb("a_neg_parts", [P, PARTS, NM], BF16)
        neg_rows = sb("a_neg_rows", [PARTS * NM, P], BF16)
        ps_s = [pb(f"a_ps_s{i}", [P, 2, CH], FP32) for i in range(2)]
        ps_m = pb("a_ps_m", [P, 3, CH], FP32)
        ps_o = pb("a_ps_o", [P, CH], FP32)

        a_cleared, a_ident_ok = sem("a_cleared"), sem("a_ident_ok")
        consts = sem("a_consts")
        ones_ok = sem("ones_ok")
        loaded = [[sem(f"loaded{p}{h}") for h in range(HG)] for p in range(2)]
        v_staged = sem("v_staged")
        scored = sem("scored")
        exped = sem("exped")
        pv_done = sem("pv_done")
        o_copied = sem("o_copied")
        o_stored = sem("o_stored")
        m_scored = sem("m_scored")
        m_maxed = sem("m_maxed")
        neg_ok = sem("neg_ok")
        neg_step, neg_split = sem("neg_step"), sem("neg_split")
        neg_ps, neg_t, neg_in = sem("neg_ps"), sem("neg_t"), sem("neg_in")

        BLK = NM * NC
        AHEAD = 2
        NEG = 15
        ITEMS = BLK + 1

        def item(i):
            return i if i < NEG else i + 1

        def bank(i):
            return ps_m[:, item(i) % 3]

        ps_n = ps_m[0:PARTS * NM, NEG % 3].bitcast(BF16)[:, 0:P]

        def groups(eng, body):
            with eng.Fori(0, (G - 2) // 2) as i:
                for buf in range(2):
                    body(i * 2 + buf, buf, False)
            body(G - 2, 0, False)
            body(G - 1, 1, True)

        with nc.Block() as block:
            @block.sync
            def _(sp):
                def load(g, buf):
                    for h in range(HG):
                        for stack, scr, part in ((k_st, k_scr, K_PART), (q_st, q_scr, Q_PART)):
                            src = scr.rearrange("a b (g h d) s -> a (b g) h d s", h=HG, d=DK)
                            for i, a in enumerate(part):
                                rows = src[a, bass.ds(g, 1), h].rearrange("g d s -> (g d) s")
                                dst = stack[i * DK:(i + 1) * DK, buf]
                                if stack is k_st:
                                    sp.dma_start(dst[:, h], rows).then_inc(loaded[buf][h], 16)
                                else:
                                    sp.dma_start(dst[:, :, h], rows.rearrange("d (c s) -> d c s", s=CH)
                                                 ).then_inc(loaded[buf][h], 16)

                def store_neg(m, buf, c):
                    sp.wait_ge(neg_t, ONE + m + 1)
                    for i in range(PARTS):
                        dst = q_st[KQ + i:KQ + i + 1, buf, bass.ds(c, 1)].rearrange("a c h (s n) -> a (c h s) n", n=P)
                        sp.dma_start(dst, neg_rows[i * NM:(i + 1) * NM, :]).then_inc(neg_in, 16)
                    sp.wait_ge(neg_in, ONE + 16 * PARTS * (m + 1))
                    sp.nop(nofuse=True)

                sp.wait_ge(ones_ok, ONE + 1)
                load(0, 0)
                store_neg(0, 0, 0)
                sp.wait_ge(ones_ok, ONE + 2)
                load(1, 1)

                def body(g, buf, last):
                    with sp.Fori(1, NC) as c:
                        store_neg(g * NC + c, buf, c)
                    if not last:
                        store_neg(g * NC + NC, 1 - buf, 0)
                        if not (isinstance(g, int) and g == G - 2):
                            sp.wait_ge(scored, ONE + (g + 1) * NC * NT * 2)
                            load(g + 2, buf)
                groups(sp, body)

            @block.gpsimd
            def _(pool):
                nc.gpsimd.memset(v_st[:, :, :, :, :], 0.0).then_inc(consts, 1)
                pool.wait_ge(consts, ONE + 1)
                nc.gpsimd.memset(v_st[:, :, :, :, DK:DK + 1], 1.0).then_inc(consts, 1)
                pool.wait_ge(consts, ONE + 2)
                identity(nc.gpsimd, ident[:, :], a_cleared, a_ident_ok)
                pool.wait_ge(a_ident_ok, ONE + 1)

                def stage_v(g, buf):
                    pool.nop(nofuse=True)
                    nc.gpsimd.tensor_copy(
                        v_st[:, buf, :, :, 0:DK],
                        v_all.rearrange("p b g t (h d) -> p (b g) t h d", d=DK)[:, bass.ds(g, 1)]
                        .rearrange("p g t h d -> p (g t) h d")).then_inc(v_staged, 1)

                def split(m):
                    pool.wait_ge(neg_ok, ONE + m + 1)
                    pool.wait_ge(neg_ps, ONE + m)
                    pool.nop(nofuse=True)
                    nc.gpsimd.tensor_copy(neg_parts[:, 0], neg[:, :]).then_inc(neg_step, 1)
                    pool.wait_ge(neg_step, ONE + m * 3 + 1)
                    nc.gpsimd.tensor_tensor(neg_rest[:, :], neg[:, :], neg_parts[:, 0], ALU.subtract).then_inc(neg_step, 1)
                    pool.wait_ge(neg_step, ONE + m * 3 + 2)
                    pool.nop(nofuse=True)
                    nc.gpsimd.tensor_copy(neg_parts[:, 1], neg_rest[:, :]).then_inc(neg_step, 1)
                    pool.wait_ge(neg_step, ONE + m * 3 + 3)
                    nc.gpsimd.tensor_tensor(neg_parts[:, 2], neg_rest[:, :], neg_parts[:, 1], ALU.subtract).then_inc(neg_split, 1)
                    pool.wait_ge(neg_split, ONE + m + 1)

                stage_v(0, 0)
                with pool.Fori(0, AHEAD) as c:
                    split(c)

                def body(g, buf, last):
                    if not last:
                        pool.wait_ge(pv_done, ONE + g * NC * NT)
                        pool.nop(nofuse=True)
                        stage_v(g + 1, 1 - buf)
                    with pool.Fori(AHEAD, NC if last else NC + AHEAD) as c:
                        split(g * NC + c)
                groups(pool, body)

            @block.tensor
            def _(pe):
                def max_blocks(m, buf, c, first, end, loads=None):
                    for i in range(first, end):
                        h, st, tc = i // 16, i // 4 % 4, i % 4
                        if i % 16 == 0 and loads is not None:
                            pe.wait_ge(loaded[buf][h], ONE + loads)
                        before = item(i) - 3
                        if before == NEG:
                            pe.wait_ge(neg_t, ONE + m)
                        elif before > NEG:
                            pe.wait_ge(m_maxed, ONE + m * BLK + before + 2)
                        elif before >= 0:
                            pe.wait_ge(m_maxed, ONE + m * BLK + before + 3)
                        else:
                            pe.wait_ge(m_maxed, ONE + m * BLK + (1, 2, 0)[i])
                        nc.tensor.matmul(bank(i), q_st[0:KQ, buf, bass.ds(c, 1), h, st * P:(st + 1) * P].rearrange("p c n -> p (c n)"),
                                         k_st[0:KQ, buf, h, tc * CH:(tc + 1) * CH],
                                         start=True, stop=True).then_inc(m_scored, 1)

                def transpose_neg(m, read):
                    pe.wait_ge(neg_split, ONE + m + 1)
                    pe.wait_ge(m_maxed, ONE + read)
                    pe.nop(nofuse=True)
                    nc.tensor.transpose(ps_n, neg_parts[:, :, :].rearrange("p a m -> p (a m)"),
                                        ident[:, :]).then_inc(neg_ps, 1)

                def values(buf, t):
                    for h in range(HG):
                        last = nc.tensor.matmul(ps_o[h * VW:(h + 1) * VW, :], v_st[:, buf, t, h],
                                                probs[:, t % 2, h], start=t == 0, stop=t == NT - 1)
                    last.then_inc(pv_done, 1)

                def chunk(g, buf, c, first, m_buf, m_c, with_neg):
                    e = g * NC + c
                    pe.wait_ge(neg_in, ONE + 16 * PARTS * (e + 1))
                    taken = 0

                    def maximum():
                        nonlocal taken
                        if m_buf is not None:
                            loads = 16 * len(Q_PART) * (g + (3 if buf else 2)) if m_buf != buf else None
                            max_blocks(e + AHEAD, m_buf, m_c, taken, taken + 1, loads)
                            taken += 1

                    for t in range(NT):
                        maximum()
                        for half in range(2):
                            pe.wait_ge(exped, ONE + e * NT * 2 + t * 2 + half + 1)
                            for i in range(2):
                                last = nc.tensor.matmul(ps_s[half][:, i], k_st[0:KQM, buf, 2 * half + i, t * P:(t + 1) * P],
                                                        q_st[0:KQM, buf, bass.ds(c, 1), 2 * half + i].rearrange("p c n -> p (c n)"),
                                                        start=True, stop=True)
                                if i == 1:
                                    last.then_inc(scored, 1)
                                if i == half:
                                    maximum()
                        if with_neg and t == 3:
                            if m_buf is None:
                                transpose_neg(e + 1, G * NC * BLK + 2)
                            else:
                                transpose_neg(e + 1, (e + AHEAD) * BLK + NEG)
                        maximum()
                        if t > 0 or not first:
                            pe.wait_ge(exped, ONE + e * NT * 2 + t * 2 + 2)
                            if t == 1:
                                pe.wait_ge(o_copied, ONE + e)
                            values(buf, (t - 1) % NT)

                pe.wait_ge(a_ident_ok, ONE + 1)
                pe.wait_ge(consts, ONE + 2)
                max_blocks(0, 0, 0, 0, BLK, 16 * 2 * len(Q_PART))
                max_blocks(1, 0, 1, 0, NEG)
                transpose_neg(0, BLK + NEG)
                max_blocks(1, 0, 1, NEG, BLK)

                def body(g, buf, last):
                    pe.wait_ge(v_staged, ONE + g + 1)
                    pe.nop(nofuse=True)
                    chunk(g, buf, 0, True, buf, AHEAD, True)
                    with pe.Fori(1, NC - AHEAD) as c:
                        chunk(g, buf, c, False, buf, c + AHEAD, True)
                    if last:
                        with pe.Fori(NC - AHEAD, NC - 1) as c:
                            chunk(g, buf, c, False, None, None, True)
                        chunk(g, buf, NC - 1, False, None, None, False)
                    else:
                        with pe.Fori(NC - AHEAD, NC) as c:
                            chunk(g, buf, c, False, 1 - buf, c - (NC - AHEAD), True)
                    pe.wait_ge(exped, ONE + (g * NC + NC) * NT * 2 + 2)
                    values(buf, NT - 1)
                groups(pe, body)

            @block.scalar
            def _(act):
                def copy_neg(m):
                    act.wait_ge(neg_ps, ONE + m + 1)
                    act.wait_ge(neg_in, ONE + 16 * PARTS * m)
                    nc.scalar.activation(neg_rows[:, :], ps_n, ACT.Copy).then_inc(neg_t, 1)

                def copy_out(g, c, e):
                    act.wait_ge(pv_done, ONE + NT * e)
                    act.wait_ge(o_stored, ONE + 16 * HG * (e - 1))
                    nc.scalar.activation(o_sb[:, 0], ps_o[:, :], ACT.Copy).then_inc(o_copied, 1)
                    act.wait_ge(o_copied, ONE + e)
                    for h in range(HG):
                        act.dma_start(o_scr[bass.ds(g, 1), h, :, bass.ds(c * CH, CH)].rearrange("g r s -> (g r) s"),
                                      o_sb[h * VW:h * VW + DK + 1, 0]).then_inc(o_stored, 16)

                def chunk(g, c, first, with_neg):
                    e = g * NC + c
                    for t in range(NT):
                        if with_neg and t == 4:
                            copy_neg(e + 1)
                        if t >= 1 or not first:
                            act.wait_ge(pv_done, ONE + e * NT + t - 1)
                        for half in range(2):
                            act.wait_ge(scored, ONE + e * NT * 2 + t * 2 + half + 1)
                            nc.scalar.activation(probs[:, t % 2, 2 * half:2 * half + 2], ps_s[half][:, :, :], ACT.Exp,
                                                 scale=float(DK) ** -0.5).then_inc(exped, 1)
                        if t == 0 and not first:
                            copy_out(g, c - 1, e)

                act.sem_inc(exped, 2)
                copy_neg(0)

                def body(g, buf, last):
                    chunk(g, 0, True, True)
                    with act.Fori(1, NC - 1 if last else NC) as c:
                        chunk(g, c, False, True)
                    if last:
                        chunk(g, NC - 1, False, False)
                    copy_out(g, NC - 1, g * NC + NC)
                groups(act, body)
                act.wait_ge(o_stored, ONE + 16 * HG * G * NC)

            @block.vector
            def _(dve):
                def maxima(m):
                    for i in range(BLK):
                        dve.wait_ge(m_scored, ONE + m * BLK + i + 1)
                        if i == 0:
                            dve.wait_ge(neg_ok, ONE + m)
                        nc.vector.reduce_max(mx[:, i // NC, i % NC:i % NC + 1], bank(i), AX.X).then_inc(m_maxed, 1)
                    dve.wait_ge(m_maxed, ONE + m * BLK + BLK + 2)
                    dve.wait_ge(neg_split, ONE + m)
                    nc.vector.reduce_max(neg[:, :], mx[:, :, :], AX.X, negate=True).then_inc(neg_ok, 1)

                for buf in range(2):
                    nc.vector.memset(k_st[96:128, buf].rearrange("p h s -> p (h s)").bitcast(FP32),
                                     TWO_BF16_ONES).then_inc(ones_ok, 1)
                dve.sem_inc(m_maxed, 2)
                with dve.Fori(0, G * NC) as m:
                    maxima(m)


def transpose_weights(nc, sem, dirs, win_scr, xp_scr, dtw_scr, ow_scr):
    with ExitStack() as ctx:
        def sb(name, shape, dt):
            return ctx.enter_context(nc.sbuf_tensor(name, shape, dt))

        ident = sb("w_ident", [P, P], FP32)
        win = sb("w_in", [P, 2, 2 * DI // P, D], FP32)
        xp = sb("w_xp", [R + 2 * DS, 2, DI], FP32)
        dtw = sb("w_dt", [P, 2, ND, R], FP32)
        ow = sb("w_out", [P, 2, KD, DI], FP32)
        win_t = sb("w_in_t", [P, 2, KD, 2 * DI], FP32)
        xp_t = sb("w_xp_t", [P, 2, ND, XPW], FP32)
        dtw_t = sb("w_dt_t", [R, 2, DI], FP32)
        ow_t = sb("w_out_t", [P, 2, ND, D], FP32)
        NB = 4
        ps = [ctx.enter_context(nc.psum_tensor(f"w_ps{i}", [P, CH], FP32)) for i in range(NB)]
        loaded, cleared, ident_ok = sem("w_loaded"), sem("w_cleared"), sem("w_ident_ok")
        pads_ok = sem("w_pads_ok")
        transposed, copied, stored = sem("w_transposed"), sem("w_copied"), sem("w_stored")

        blocks = []
        for z in range(2):
            for m in range(2 * DI // P):
                for k in range(KD):
                    blocks.append((win[:, z, m, k * P:(k + 1) * P], P, P,
                                   [(win_t[:, z, k, m * P:(m + 1) * P], 0, P)]))
            for k in range(ND):
                cols = slice(k * P, (k + 1) * P)
                blocks.append((xp[:, z, cols], R + 2 * DS, P,
                               [(xp_t[:, z, k, X_DT:X_DT + R], 0, R), (xp_t[:, z, k, X_B:X_B + DS], R, R + DS),
                                (xp_t[:, z, k, X_C:X_C + DS], R + DS, R + 2 * DS)]))
                blocks.append((dtw[:, z, k], P, R, [(dtw_t[:, z, cols], 0, P)]))
                for m in range(KD):
                    blocks.append((ow[:, z, m, cols], P, P, [(ow_t[:, z, k, m * P:(m + 1) * P], 0, P)]))

        with nc.Block() as block:
            @block.sync
            def _(sp):
                for z, w in enumerate(dirs):
                    sp.dma_start(win[:, z], w["in_w"].rearrange("(m p) k -> p m k", p=P)).then_inc(loaded, 16)
                    sp.dma_start(xp[:, z], w["xproj_w"]).then_inc(loaded, 16)
                    sp.dma_start(dtw[:, z], w["dt_w"].rearrange("(k p) r -> p k r", p=P)).then_inc(loaded, 16)
                    sp.dma_start(ow[:, z], w["out_w"].rearrange("(m p) k -> p m k", p=P)).then_inc(loaded, 16)
                sp.wait_ge(copied, ONE + len(blocks))
                for z in range(2):
                    sp.dma_start(win_scr[z].rearrange("(k p) m -> p k m", p=P), win_t[:, z]).then_inc(stored, 16)
                    sp.dma_start(xp_scr[z], xp_t[:, z]).then_inc(stored, 16)
                    sp.dma_start(dtw_scr[z], dtw_t[:, z]).then_inc(stored, 16)
                    sp.dma_start(ow_scr[z], ow_t[:, z]).then_inc(stored, 16)
                sp.wait_ge(stored, ONE + 8 * 16)

            @block.gpsimd
            def _(pool):
                identity(nc.gpsimd, ident[:, :], cleared, ident_ok)

            @block.tensor
            def _(pe):
                pe.wait_ge(ident_ok, ONE + 1)
                pe.wait_ge(loaded, ONE + 8 * 16)
                for i, (src, rows, cols, _) in enumerate(blocks):
                    if i >= NB:
                        pe.wait_ge(copied, ONE + i - NB + 1)
                    nc.tensor.transpose(ps[i % NB][0:cols, 0:rows], src, ident[0:rows, 0:rows]).then_inc(transposed, 1)

            @block.vector
            def _(dve):
                nc.vector.memset(xp_t[:, :, :, :], 0.0).then_inc(pads_ok, 1)
                dve.wait_ge(pads_ok, ONE + 1)
                for i, (_, rows, cols, dsts) in enumerate(blocks):
                    dve.wait_ge(transposed, ONE + i + 1)
                    for dst, a, b in dsts:
                        last = nc.vector.tensor_copy(dst, ps[i % NB][0:cols, a:b])
                    last.then_inc(copied, 1)


def normalize(nc, dve, h, stats, mv, std, rstd, xn, sems, n):
    step, mv_ok, std_ok, xn_ok = sems
    for t in range(4):
        last = nc.vector.bn_stats(stats[:, t], h[:, t])
    last.then_inc(step, 1)
    dve.wait_ge(step, ONE + 2 * n + 1)
    dve.nop(nofuse=True)
    for t in range(4):
        last = nc.vector.bn_aggr(mv[:, t], stats[:, t])
    last.then_inc(mv_ok, 1)
    dve.wait_ge(std_ok, ONE + n + 1)
    nc.vector.reciprocal(rstd, std).then_inc(step, 1)
    dve.wait_ge(step, ONE + 2 * n + 2)
    for t in range(4):
        last = nc.vector.tensor_scalar(xn[:, t], h[:, t], mv[:, t, 0:1], rstd[:, t:t + 1], ALU.subtract, ALU.mult)
    last.then_inc(xn_ok, 1)


def batch_chunks(eng):
    with eng.Fori(0, B) as b:
        with eng.Fori(0, NC // 2) as j:
            for buf in range(2):
                yield b, j * 2 + buf, b * NC + j * 2 + buf, buf


def attention_out(nc, sem, o_scr, wo, bo, h_scr, xn_scr):
    with ExitStack() as ctx:
        def sb(name, shape, dt):
            return ctx.enter_context(nc.sbuf_tensor(name, shape, dt))

        def pb(name, shape, dt):
            return ctx.enter_context(nc.psum_tensor(name, shape, dt))

        ident = sb("o_ident", [P, P], FP32)
        w = sb("o_w", [P, KD, D], FP32)
        bias = sb("o_bias", [P, D], FP32)
        eps = sb("o_eps", [P, 1], FP32)
        o_in = sb("o_in", [P, 2, KD, CH], FP32)
        l_in = sb("o_l", [P, 2, KD, CH], FP32)
        inv = sb("o_inv", [P, KD, CH], FP32)
        o_n = sb("o_n", [P, 2, KD, CH], FP32)
        h = sb("o_h", [P, 2, 4, D], FP32)
        xn = sb("o_xn", [P, 2, 4, D], FP32)
        xt = sb("o_xt", [P, 2, KD, CH], FP32)
        stats = sb("o_stats", [P, 4, 6], FP32)
        mv = sb("o_mv", [P, 4, 2], FP32)
        std, rstd = sb("o_std", [P, 4], FP32), sb("o_rstd", [P, 4], FP32)
        ps_h = pb("o_ps_h", [P, 2, 4, D], FP32)
        ps_t = pb("o_ps_t", [P, 2, KD, CH], FP32)

        w_in, cleared, ident_ok = sem("o_w_in"), sem("o_cleared"), sem("o_ident_ok")
        in_ok = [sem("o_in0"), sem("o_in1")]
        inv_ok, on_ok, h_ps, h_ok = sem("o_inv_ok"), sem("o_on_ok"), sem("o_h_ps"), sem("o_h_ok")
        step, mv_ok, std_ok, xn_ok = sem("o_step"), sem("o_mv_ok"), sem("o_std_ok"), sem("o_xn_ok")
        eps_ok = sem("o_eps_ok")
        t_ps, t_ok = sem("o_t_ps"), sem("o_t_ok")
        h_stored, x_stored = [sem("o_hs0"), sem("o_hs1")], [sem("o_xs0"), sem("o_xs1")]

        with nc.Block() as block:
            @block.sync
            def _(sp):
                sp.dma_start(w[:, :, :], wo.rearrange("(k p) n -> p k n", p=P)).then_inc(w_in, 16)
                sp.dma_start(bias[:, :], bo.partition_broadcast(P)).then_inc(w_in, 16)
                heads = P // DK
                for b, c, n, buf in batch_chunks(sp):
                    sp.wait_ge(on_ok, ONE + n - buf)
                    for m in range(KD):
                        src = o_scr.rearrange("(b g) h r s -> b (g h) r s", b=B)[bass.ds(b, 1), m * heads:(m + 1) * heads, :,
                                                                               bass.ds(c * CH, CH)]
                        src = src.rearrange("b h r s -> (b h) r s")
                        sp.dma_start(o_in[:, buf, m], src[:, 0:DK]).then_inc(in_ok[buf], 16)
                        sp.dma_start(l_in[:, buf, m], src[:, DK:DK + 1].to_broadcast([heads, DK, CH])
                                     ).then_inc(in_ok[buf], 16)

            @block.gpsimd
            def _(pool):
                identity(nc.gpsimd, ident[:, :], cleared, ident_ok)
                nc.gpsimd.memset(eps[:, :], LN_EPS).then_inc(eps_ok, 1)

            @block.tensor
            def _(pe):
                pe.wait_ge(w_in, ONE + 32)
                pe.wait_ge(ident_ok, ONE + 1)

                def transposes(n, buf):
                    pe.wait_ge(xn_ok, ONE + n + 1)
                    for t in range(4):
                        for k in range(KD):
                            last = nc.tensor.transpose(ps_t[:, buf, k, t * P:(t + 1) * P], xn[:, buf, t, k * P:(k + 1) * P],
                                                       ident[:, :])
                    last.then_inc(t_ps, 1)

                for b, c, n, buf in batch_chunks(pe):
                    pe.wait_ge(on_ok, ONE + n + 1)
                    pe.wait_ge(h_ok, ONE + n - buf)
                    for t in range(4):
                        for k in range(KD):
                            last = nc.tensor.matmul(ps_h[:, buf, t], o_n[:, buf, k, t * P:(t + 1) * P], w[:, k],
                                                    start=k == 0, stop=k == KD - 1)
                    last.then_inc(h_ps, 1)
                    pe.wait_ge(t_ok, ONE + n - buf)
                    transposes(n, buf)

            @block.scalar
            def _(act):
                act.wait_ge(eps_ok, ONE + 1)
                for b, c, n, buf in batch_chunks(act):
                    act.wait_ge(mv_ok, ONE + n + 1)
                    nc.scalar.activation(std[:, :], mv[:, :, 1], ACT.Sqrt, bias=eps[:, :]).then_inc(std_ok, 1)
                    act.wait_ge(t_ps, ONE + n + 1)
                    act.wait_ge(x_stored[buf], ONE + (n - buf) * 8)
                    nc.scalar.activation(xt[:, buf], ps_t[:, buf], ACT.Copy).then_inc(t_ok, 1)
                    act.dma_start(h_scr[bass.ds(n * 4, 4)].rearrange("t p d -> p t d"), h[:, buf]).then_inc(h_stored[buf], 16)
                    act.wait_ge(t_ok, ONE + n + 1)
                    act.dma_start(xn_scr[bass.ds(b, 1), :, bass.ds(c * CH, CH)].rearrange("b (k p) s -> p (b k) s", p=P),
                                  xt[:, buf]).then_inc(x_stored[buf], 16)
                for buf in range(2):
                    act.wait_ge(h_stored[buf], ONE + 16 * B * NC // 2)
                    act.wait_ge(x_stored[buf], ONE + 16 * B * NC // 2)

            @block.vector
            def _(dve):
                dve.wait_ge(w_in, ONE + 32)
                for b, c, n, buf in batch_chunks(dve):
                    dve.wait_ge(in_ok[buf], ONE + (n - buf) * 32 + 64)
                    nc.vector.reciprocal(inv[:, :, :], l_in[:, buf]).then_inc(inv_ok, 1)
                    dve.wait_ge(inv_ok, ONE + n + 1)
                    dve.wait_ge(h_ps, ONE + n - buf)
                    nc.vector.tensor_tensor(o_n[:, buf], o_in[:, buf], inv[:, :, :], ALU.mult).then_inc(on_ok, 1)
                    dve.wait_ge(h_ps, ONE + n + 1)
                    dve.wait_ge(h_stored[buf], ONE + (n - buf) * 8)
                    nc.vector.tensor_tensor(h[:, buf], ps_h[:, buf], bias[:, None, :].to_broadcast([P, 4, D]),
                                            ALU.add).then_inc(h_ok, 1)
                    dve.wait_ge(h_ok, ONE + n + 1)
                    dve.wait_ge(t_ps, ONE + n - buf)
                    normalize(nc, dve, h[:, buf], stats, mv, std[:, :], rstd[:, :], xn[:, buf], (step, mv_ok, std_ok, xn_ok), n)


def mamba(nc, sem, tag, backward, w, win_scr, xp_scr, dtw_scr, xn_scr, y_scr):
    with ExitStack() as ctx:
        def sb(name, shape, dt):
            return ctx.enter_context(nc.sbuf_tensor(tag + name, shape, dt))

        def pb(name, shape, dt):
            return ctx.enter_context(nc.psum_tensor(tag + name, shape, dt))

        def sem_(name):
            return sem(tag + name)

        xc = sb("xc", [P, ND, S], FP32)
        zs = sb("zs", [P, ND, S], FP32)
        delta = sb("delta", [P, ND, S], FP32)
        du = sb("du", [P, ND, S], FP32)
        bc_parts = sb("bc_parts", [PARTS * DS, 2, S], BF16)
        sel = sb("sel", [PARTS * DS, DS, P], BF16)
        ident = sb("ident", [P, P], FP32)
        wxp = sb("wxp", [P, ND, XPW], FP32)
        wdt = sb("wdt", [R, DI], FP32)
        conv_w = sb("conv_w", [P, ND, DC], FP32)
        cols = sb("cols", [P, 3, ND], FP32)
        a_neg = sb("a_neg", [P, ND, DS], FP32)
        a_cur = sb("a_cur", [P, 2, DS], FP32)
        diag = sb("diag", [P, 2, P], FP32)
        carry = sb("carry", [P, DS, 2], FP32)

        PAD = DC - 1
        XH = S + PAD + 1
        SPLIT = CH
        words = KD * S + 2 * XH + KD * 2 * DI + 2 * CH + 2 * PARTS * CH // 2 + CH
        stage = sb("stage", [P, max(words, 12 * TC)], FP32)
        at = 0

        def carve(shape):
            nonlocal at
            size = 1
            for s in shape:
                size *= s
            view = stage[:, at:at + size]
            at += size
            names = "abc"[:len(shape)]
            if len(shape) == 1:
                return view
            return view.rearrange(f"p ({' '.join(names)}) -> p {' '.join(names)}", **dict(zip(names, shape)))

        xn = carve([KD, S])
        xh = carve([2, XH])
        win = carve([KD, 2 * DI])
        dt_in = carve([2, CH])
        split = carve([2 * PARTS * CH // 2]).bitcast(BF16).rearrange("p (b a s) -> p b a s", b=2, a=PARTS)
        rest = carve([CH])
        at = 0
        bc = carve([4, TC]).rearrange("p (n i) s -> p n i s", i=2)
        da = carve([4, TC])
        hs = carve([4, TC])

        ps_y = pb("ps_y", [P, 2, TC], FP32)
        ps_bc = [pb(f"ps_bc{i}", [P, TC], FP32) for i in range(2)]
        NH = TC // CH

        w_in, cleared, ident_ok = sem_("w_in"), sem_("cleared"), sem_("ident_ok")
        sel_step, sel_ok, a_step, a_ok = sem_("sel_step"), sem_("sel_ok"), sem_("a_step"), sem_("a_ok")
        in_ok = sem_("in_ok")
        up_ps, up_ok = sem_("up_ps"), sem_("up_ok")
        pad_ok, conv_step, conv_ok, xc_ok = sem_("pad_ok"), sem_("conv_step"), sem_("conv_ok"), sem_("xc_ok")
        xp_ps, dt_ok, part1, rest_ok = sem_("xp_ps"), sem_("dt_ok"), sem_("part1"), sem_("rest_ok")
        part2, part3 = sem_("part2"), sem_("part3")
        bc_in = [sem_("bc_in0"), sem_("bc_in1")]
        dl_ps, dl_abs, dl_relu = sem_("dl_ps"), sem_("dl_abs"), sem_("dl_relu")
        dl_exp, dl_log, dl_sum, du_ok = sem_("dl_exp"), sem_("dl_log"), sem_("dl_sum"), sem_("du_ok")
        bc_ps = [sem_("b_ps"), sem_("c_ps")]
        bc_ok = [sem_("b_ok"), sem_("c_ok")]
        acur_ok, da_ok, h_ok = sem_("acur_ok"), sem_("da_ok"), sem_("h_ok")
        u_ok = sem_("u_ok")
        g_ok = sem_("g_ok")
        summed = sem_("summed")
        y_ok = sem_("y_ok")
        carry_ok, diag_ok, stored = sem_("carry_ok"), sem_("diag_ok"), sem_("stored")

        NCP = ND // 2
        NTC = S // TC
        STEPS = NTC * DS
        TILES = 2 * STEPS
        PER_TC = 2 * DS

        def when(tc):
            return (NTC - 1) - tc if backward else tc

        def pairs(eng, body):
            def of_batch(b):
                with eng.Fori(0, NCP) as dp:
                    body(b * NCP + dp, dp)
            return of_batch

        def span(tile, dp, i, tc):
            return tile[:, bass.ds(dp * 2 + i, 1), when(tc) * TC:(when(tc) + 1) * TC].rearrange("p a s -> p (a s)")

        with nc.Block() as block:
            @block.sync
            def _(sp):
                sp.dma_start(wxp[:, :, :], xp_scr).then_inc(w_in, 16)
                sp.dma_start(wdt[:, :], dtw_scr).then_inc(w_in, 16)
                sp.dma_start(conv_w[:, :, :], w["conv_w"].rearrange("(k p) c -> p k c", p=P)).then_inc(w_in, 16)
                sp.dma_start(a_neg[:, :, :], w["A_log"].rearrange("(k p) n -> p k n", p=P)).then_inc(w_in, 16)
                for i, name in enumerate(("conv_b", "dt_b", "D")):
                    sp.dma_start(cols[:, i], w[name].rearrange("(k p) -> p k", p=P),
                                 allow_slow_non_contiguous=True).then_inc(w_in, 16)
                with sp.Fori(0, B) as b:
                    sp.wait_ge(y_ok, ONE + b * NCP * NTC * 2 + 1)
                    sp.dma_start(win, win_scr.rearrange("(k p) m -> p k m", p=P)).then_inc(in_ok, 16)
                    sp.dma_start(xn, xn_scr[bass.ds(b, 1)].rearrange("b (k p) s -> p (b k) s", p=P)).then_inc(in_ok, 16)
                    for c in range(NC):
                        sp.wait_ge(part3, ONE + b * NC + c + 1)
                        for i in range(PARTS):
                            for j in range(2):
                                sp.dma_start(bc_parts[i * DS:(i + 1) * DS, j, c * CH:(c + 1) * CH],
                                             split[X_BC[j]:X_BC[j] + DS, c % 2, i]).then_inc(bc_in[c % 2], 16)
                    sp.wait_ge(y_ok, ONE + (b + 1) * NCP * NTC * 2 + 1)
                    sp.dma_start(y_scr[bass.ds(b, 1)].rearrange("b (k p) s -> p (b k) s", p=P), zs[:, :, :]).then_inc(stored, 16)
                    sp.wait_ge(stored, ONE + 16 * (b + 1))
                    sp.nop(nofuse=True)

            @block.gpsimd
            def _(pool):
                identity(nc.gpsimd, ident[:, :], cleared, ident_ok)
                pool.wait_ge(ident_ok, ONE + 1)
                nc.gpsimd.memset(sel[:, :, :], 0.0).then_inc(sel_step, 1)
                for i in range(PARTS):
                    pool.wait_ge(sel_step, ONE + i + 1)
                    nc.gpsimd.affine_select(out=sel[:, :, :], in_=sel[:, :, :], compare_op=ALU.not_equal, fill=1.0,
                                            base=-i * DS, pattern=[[-1, DS], [0, P]], channel_multiplier=1
                                            ).then_inc(sel_step, 1)
                pool.wait_ge(sel_step, ONE + PARTS + 1)
                pool.sem_inc(g_ok, 4)
                pool.sem_inc(sel_ok, 1)

                def body(pair, dp):
                    for k in range(TILES):
                        m = k // 2
                        pool.wait_ge(bc_ok[1], ONE + pair * STEPS + m + 1)
                        pool.wait_ge(h_ok, ONE + pair * TILES + k + 1)
                        nc.gpsimd.tensor_tensor(da[:, k % 4], hs[:, k % 4], bc[:, m % 2, 1], ALU.mult).then_inc(g_ok, 1)

                stage_b = pairs(pool, body)
                with pool.Fori(0, B) as b:
                    stage_b(b)

            @block.tensor
            def _(pe):
                def up(b, m, j):
                    for c in range(NC):
                        pe.wait_ge(up_ok, ONE + b * 8 * NC + j * NC + c + 1)
                        for k in range(KD):
                            last = nc.tensor.matmul(ps_y[:, c // NH, (c % NH) * CH:(c % NH + 1) * CH],
                                                    win[:, k, m * P:(m + 1) * P], xn[:, k, c * CH:(c + 1) * CH],
                                                    start=k == 0, stop=k == KD - 1)
                        last.then_inc(up_ps, 1)

                def spread(pair, m, j):
                    if m >= STEPS:
                        return
                    pe.wait_ge(bc_ok[j], ONE + pair * STEPS + m)
                    pe.nop(nofuse=True)
                    for i in range(NH):
                        at = when(m // DS) * TC + i * CH
                        last = nc.tensor.matmul(ps_bc[j][:, i * CH:(i + 1) * CH], sel[:, m % DS],
                                                bc_parts[:, j, at:at + CH], start=True, stop=True)
                    last.then_inc(bc_ps[j], 1)

                def body(pair, dp):
                    spread(pair, 0, 0)
                    spread(pair, 0, 1)
                    spread(pair, 1, 0)
                    spread(pair, 1, 1)
                    spread(pair, 2, 0)
                    for k in range(TILES):
                        m, i = divmod(k, 2)
                        tc, n = divmod(m, DS)
                        if n == 0:
                            if k < 2:
                                pe.wait_ge(diag_ok, ONE + (pair * 2 + i) + 1)
                            pe.wait_ge(y_ok, ONE + (pair * NTC + tc) * 2 + i)
                            pe.nop(nofuse=True)
                            for c in range(NH):
                                nc.tensor.matmul(ps_y[:, i, c * CH:(c + 1) * CH], diag[:, i],
                                                 xc[:, bass.ds(dp * 2 + i, 1), when(tc) * TC + c * CH:when(tc) * TC + (c + 1) * CH
                                                    ].rearrange("p a s -> p (a s)"), start=True, stop=False)
                        pe.wait_ge(g_ok, ONE + pair * TILES + k + 5)
                        for c in range(NH):
                            last = nc.tensor.matmul(ps_y[:, i, c * CH:(c + 1) * CH], ident[:, :],
                                                    da[:, k % 4, c * CH:(c + 1) * CH],
                                                    start=False, stop=n == DS - 1)
                        last.then_inc(summed, 1)
                        if i == 0:
                            spread(pair, m + 2, 1)
                            spread(pair, m + 3, 0)

                stage_b = pairs(pe, body)
                pe.wait_ge(w_in, ONE + 7 * 16)
                pe.wait_ge(ident_ok, ONE + 1)
                pe.wait_ge(sel_ok, ONE + 1)
                pe.sem_inc(summed, 4)
                with pe.Fori(0, B) as b:
                    pe.wait_ge(in_ok, ONE + 32 * (b + 1))
                    for dt in range(ND):
                        up(b, dt, 2 * dt)
                        up(b, ND + dt, 2 * dt + 1)
                    pe.wait_ge(xc_ok, ONE + ND * (b + 1))
                    for c in range(NC):
                        pe.wait_ge(part1, ONE + b * NC + c)
                        pe.wait_ge(rest_ok, ONE + b * NC + c)
                        pe.wait_ge(dt_ok, ONE + b * NC + c)
                        for k in range(ND):
                            last = nc.tensor.matmul(ps_bc[0][0:XPW, 0:CH], wxp[:, k], xc[:, k, c * CH:(c + 1) * CH],
                                                    start=k == 0, stop=k == ND - 1)
                        last.then_inc(xp_ps, 1)
                        pe.wait_ge(dt_ok, ONE + b * NC + c + 1)
                        for dt in range(ND):
                            j = b * NC * ND + c * ND + dt
                            pe.wait_ge(dl_relu, ONE + j + 1)
                            nc.tensor.matmul(ps_bc[1][:, (dt % 2) * CH:(dt % 2 + 1) * CH], wdt[:, dt * P:(dt + 1) * P],
                                             dt_in[0:R, c % 2], start=True, stop=True).then_inc(dl_ps, 1)
                    pe.wait_ge(rest_ok, ONE + (b + 1) * NC)
                    pe.wait_ge(dl_relu, ONE + (b + 1) * NC * ND + 2)
                    for buf in range(2):
                        pe.wait_ge(bc_in[buf], ONE + (b + 1) * 16 * PARTS * 2 * NC // 2)
                    pe.nop(nofuse=True)
                    stage_b(b)

            @block.scalar
            def _(act):
                act.wait_ge(w_in, ONE + 7 * 16)
                nc.scalar.activation(a_neg[:, :, :], a_neg[:, :, :], ACT.Exp).then_inc(a_step, 1)
                act.wait_ge(a_step, ONE + 1)
                nc.scalar.activation(a_neg[:, :, :], a_neg[:, :, :], ACT.Copy, scale=-1.0).then_inc(a_ok, 1)
                act.wait_ge(a_ok, ONE + 1)
                act.sem_inc(up_ok, 4)

                def copy(pair, m, j, used):
                    if m >= STEPS:
                        return
                    act.wait_ge(bc_ps[j], ONE + pair * STEPS + m + 1)
                    act.wait_ge(used, ONE + pair * TILES + 2 * m + 2)
                    nc.scalar.activation(bc[:, m % 2, j], ps_bc[j][:, :], ACT.Copy).then_inc(bc_ok[j], 1)

                def body(pair, dp):
                    act.wait_ge(da_ok, ONE + pair * TILES)
                    act.nop(nofuse=True)
                    nc.scalar.activation(a_cur[:, :, :], a_neg[:, bass.ds(dp * 2, 2), :], ACT.Copy).then_inc(acur_ok, 1)
                    copy(pair, 0, 0, u_ok)
                    act.wait_ge(acur_ok, ONE + pair + 1)
                    for k in range(TILES):
                        m, i = divmod(k, 2)
                        act.wait_ge(summed, ONE + pair * TILES + k + 1)
                        act.nop(nofuse=True)
                        nc.scalar.activation(da[:, k % 4], span(delta, dp, i, m // DS), ACT.Exp,
                                             scale=a_cur[:, i, m % DS:m % DS + 1]).then_inc(da_ok, 1)
                        if i == 0:
                            copy(pair, m, 1, g_ok)
                            copy(pair, m + 1, 0, u_ok)

                stage_b = pairs(act, body)
                with act.Fori(0, B) as b:
                    for dt in range(ND):
                        for c in range(NC):
                            act.wait_ge(up_ps, ONE + b * 8 * NC + 2 * dt * NC + c + 1)
                            if dt >= 2 and c == 0:
                                act.wait_ge(conv_ok, ONE + b * ND + dt - 1)
                            off = (0 if backward else PAD) + c * CH
                            nc.scalar.activation(xh[:, dt % 2, off:off + CH], ps_y[:, c // NH, (c % NH) * CH:(c % NH + 1) * CH],
                                                 ACT.Copy).then_inc(up_ok, 1)
                        for c in range(NC):
                            act.wait_ge(up_ps, ONE + b * 8 * NC + (2 * dt + 1) * NC + c + 1)
                            act.wait_ge(stored, ONE + 16 * b)
                            nc.scalar.activation(zs[:, dt, c * CH:(c + 1) * CH], ps_y[:, c // NH, (c % NH) * CH:(c % NH + 1) * CH],
                                                 ACT.Silu).then_inc(up_ok, 1)
                        act.wait_ge(conv_ok, ONE + b * ND + dt + 1)
                        nc.scalar.activation(xc[:, dt], xc[:, dt], ACT.Silu).then_inc(xc_ok, 1)
                    for c in range(NC):
                        act.wait_ge(xp_ps, ONE + b * NC + c + 1)
                        act.wait_ge(dl_ps, ONE + (b * NC + c) * ND)
                        nc.scalar.activation(dt_in[0:R, c % 2], ps_bc[0][X_DT:X_DT + R, 0:CH], ACT.Copy).then_inc(dt_ok, 1)
                        if c >= 2:
                            act.wait_ge(bc_in[c % 2], ONE + b * 16 * PARTS * NC + 16 * PARTS * 2)
                        nc.scalar.activation(split[0:X_DT - 16, c % 2, 0], ps_bc[0][0:X_DT - 16, 0:CH], ACT.Copy).then_inc(part1, 1)
                        act.wait_ge(rest_ok, ONE + b * NC + c + 1)
                        nc.scalar.activation(split[0:X_DT - 16, c % 2, 1], rest[0:X_DT - 16, :], ACT.Copy).then_inc(part2, 1)
                        for dt in range(ND):
                            act.wait_ge(dl_ps, ONE + (b * NC + c) * ND + dt + 1)
                            nc.scalar.activation(delta[:, dt, c * CH:(c + 1) * CH], ps_bc[1][:, (dt % 2) * CH:(dt % 2 + 1) * CH],
                                                 ACT.Abs, bias=cols[:, 1, dt:dt + 1]).then_inc(dl_abs, 1)
                    act.wait_ge(dl_relu, ONE + (b + 1) * NC * ND + 2)
                    for dt in range(ND):
                        nc.scalar.activation(delta[:, dt], delta[:, dt], ACT.Exp, scale=-1.0).then_inc(dl_exp, 1)
                    for dt in range(ND):
                        act.wait_ge(dl_exp, ONE + b * ND + dt + 1)
                        nc.scalar.activation(delta[:, dt], delta[:, dt], ACT.Ln, bias=1.0).then_inc(dl_log, 1)
                    act.wait_ge(du_ok, ONE + (b + 1) * ND)
                    stage_b(b)

            @block.vector
            def _(dve):
                dve.wait_ge(w_in, ONE + 7 * 16)
                dve.wait_ge(ident_ok, ONE + 1)
                dve.sem_inc(dl_relu, 2)
                dve.sem_inc(u_ok, 2)
                dve.sem_inc(y_ok, 1)

                def body(pair, dp):
                    first = pair * TILES

                    def inputs(k):
                        if k >= TILES:
                            return
                        m, i = divmod(k, 2)
                        if i == 0:
                            dve.wait_ge(bc_ok[0], ONE + pair * STEPS + m + 1)
                        dve.wait_ge(g_ok, ONE + first + k + 1)
                        if i == 0 and 2 <= m < DS + 2:
                            dve.wait_ge(carry_ok, ONE + pair * DS + m - 1)
                            dve.nop(nofuse=True)
                        nc.vector.tensor_tensor(hs[:, k % 4], span(du, dp, i, m // DS), bc[:, m % 2, 0],
                                                ALU.mult).then_inc(u_ok, 1)

                    def scan(k):
                        m, i = divmod(k, 2)
                        tc, n = divmod(m, DS)
                        dve.wait_ge(da_ok, ONE + first + k + 1)
                        dve.wait_ge(u_ok, ONE + first + k + 3)
                        rev = slice(None, None, -1) if backward else slice(None)
                        nc.vector.tensor_tensor_scan(hs[:, k % 4, rev], da[:, k % 4, rev], hs[:, k % 4, rev],
                                                     carry[:, n, i:i + 1] if tc else 0.0, ALU.mult, ALU.add
                                                     ).then_inc(h_ok, 1)

                    def keep(m):
                        if 0 <= m < DS:
                            dve.wait_ge(h_ok, ONE + first + 2 * m + 2)
                            end = 0 if backward else TC - 1
                            k = 2 * m % 4
                            nc.vector.tensor_copy(carry[:, m, :], hs[:, k:k + 2, end]).then_inc(carry_ok, 1)

                    def gate(tc, i):
                        dve.wait_ge(summed, ONE + first + tc * PER_TC + PER_TC + 4 - 1 + i)
                        nc.vector.tensor_tensor(span(zs, dp, i, tc), ps_y[:, i], span(zs, dp, i, tc), ALU.mult
                                                ).then_inc(y_ok, 1)

                    for i in range(2):
                        nc.vector.tensor_scalar(diag[:, i], ident[:, :], cols[:, 2, bass.ds(dp * 2 + i, 1)], None,
                                                ALU.mult).then_inc(diag_ok, 1)
                    inputs(0)
                    for k in range(TILES):
                        inputs(k + 1)
                        if k % 2 == 0:
                            keep(k // 2 - 1)
                        scan(k)
                        if k - PER_TC in (GATE_AT, GATE_AT + 1):
                            gate(0, k - PER_TC - GATE_AT)
                    for i in range(2):
                        gate(1, i)

                GATE_AT = 1
                stage_b = pairs(dve, body)
                with dve.Fori(0, B) as b:
                    dve.wait_ge(in_ok, ONE + 32 * (b + 1))
                    pad = slice(S, S + PAD) if backward else slice(0, PAD)
                    nc.vector.memset(xh[:, :, pad], 0.0).then_inc(pad_ok, 1)
                    dve.wait_ge(pad_ok, ONE + b + 1)
                    for dt in range(ND):
                        dve.wait_ge(up_ok, ONE + b * 8 * NC + (2 * dt + 1) * NC + 4)
                        for tap in range(DC):
                            lo = PAD - tap if backward else tap
                            src = xh[:, dt % 2, lo:lo + S]
                            if tap == 0:
                                nc.vector.tensor_scalar(xc[:, dt], src, conv_w[:, dt, 0:1], cols[:, 0, dt:dt + 1],
                                                        ALU.mult, ALU.add).then_inc(conv_step, 1)
                            else:
                                dve.wait_ge(conv_step, ONE + (b * ND + dt) * (DC - 1) + tap)
                                nc.vector.scalar_tensor_tensor(out=xc[:, dt], in0=src, scalar=conv_w[:, dt, tap:tap + 1],
                                                               in1=xc[:, dt], op0=ALU.mult, op1=ALU.add
                                                               ).then_inc(conv_ok if tap == DC - 1 else conv_step, 1)
                    for c in range(NC):
                        n = b * NC + c
                        dve.wait_ge(part1, ONE + n + 1)
                        dve.wait_ge(part3, ONE + n)
                        nc.vector.tensor_tensor(rest[0:X_DT - 16, :], ps_bc[0][0:X_DT - 16, 0:CH], split[0:X_DT - 16, c % 2, 0],
                                                ALU.subtract).then_inc(rest_ok, 1)
                        dve.wait_ge(part2, ONE + n + 1)
                        nc.vector.tensor_tensor(split[0:X_DT - 16, c % 2, 2], rest[0:X_DT - 16, :], split[0:X_DT - 16, c % 2, 1],
                                                ALU.subtract).then_inc(part3, 1)
                        for dt in range(ND):
                            dve.wait_ge(dl_abs, ONE + n * ND + dt + 1)
                            nc.vector.tensor_scalar(du[:, dt, c * CH:(c + 1) * CH], ps_bc[1][:, (dt % 2) * CH:(dt % 2 + 1) * CH],
                                                    cols[:, 1, dt:dt + 1], 0.0, ALU.add, ALU.max).then_inc(dl_relu, 1)
                    dve.wait_ge(dl_relu, ONE + (b + 1) * NC * ND + 2)
                    for dt in range(ND):
                        dve.wait_ge(dl_log, ONE + b * ND + dt + 1)
                        nc.vector.tensor_tensor(delta[:, dt], delta[:, dt], du[:, dt], ALU.add).then_inc(dl_sum, 1)
                        dve.wait_ge(dl_sum, ONE + b * ND + dt + 1)
                        nc.vector.tensor_tensor(du[:, dt], delta[:, dt], xc[:, dt], ALU.mult).then_inc(du_ok, 1)
                    dve.wait_ge(du_ok, ONE + (b + 1) * ND)
                    dve.nop(nofuse=True)
                    stage_b(b)


def mamba_out_and_ffn(nc, sem, y_scr, ow_scr, h_scr, u1, v1, b1, u2, v2, b2, out):
    NF = FF // P
    NY = 2 * DI // P
    NCH = T // CH
    with ExitStack() as ctx:
        def sb(name, shape, dt):
            return ctx.enter_context(nc.sbuf_tensor("ffn_" + name, shape, dt))

        def pb(name, shape, dt):
            return ctx.enter_context(nc.psum_tensor("ffn_" + name, shape, dt))

        ident = sb("ident", [P, P], FP32)
        wo = sb("wo", [P, NY, D], FP32)
        wu1 = sb("u1", [P, KD, RK], FP32)
        wv1 = sb("v1", [RK, FF], FP32)
        bias1 = sb("b1", [P, NF], FP32)
        wu2 = sb("u2", [P, NF, RK], FP32)
        wv2 = sb("v2", [RK, D], FP32)
        bias2 = sb("b2", [P, D], FP32)
        eps = sb("eps", [P, 1], FP32)
        y = sb("y", [P, 2, NY, CH], FP32)
        h = sb("h", [P, 2, 4, D], FP32)
        xn = sb("xn", [P, 2, 4, D], FP32)
        xt = sb("xt", [P, KD, CH], FP32)
        pt = sb("pt", [RK, CH], FP32)
        hid = sb("hid", [P, 2, NF, CH], FP32)
        qt = sb("qt", [RK, CH], FP32)
        res = sb("res", [P, 2, 4, D], FP32)
        stats = sb("stats", [P, 4, 6], FP32)
        mv = sb("mv", [P, 4, 2], FP32)
        std, rstd = sb("std", [P, 4], FP32), sb("rstd", [P, 4], FP32)
        ps_h = pb("ps_h", [P, 4, D], FP32)
        ps_t = pb("ps_t", [P, KD, CH], FP32)
        ps_o = ps_t[:, :, :].rearrange("p k (t d) -> p (k t) d", d=D)
        ps_g = [pb(f"ps_g{i}", [P, CH], FP32) for i in range(2)]
        ps_p, ps_q = pb("ps_p", [RK, CH], FP32), pb("ps_q", [RK, CH], FP32)

        def s_(name, start=ONE):
            return sem("ffn_" + name, start)

        w_in, cleared, ident_ok, eps_ok = s_("w_in"), s_("cleared"), s_("ident_ok"), s_("eps_ok")
        y_in = [s_("y_in0", 0), s_("y_in1", 0)]
        h_ps, h_ok = s_("h_ps"), s_("h_ok")
        step, mv_ok, std_ok, xn_ok = s_("step"), s_("mv_ok"), s_("std_ok"), s_("xn_ok")
        t_ps, t_ok, p_ps, p_ok = s_("t_ps"), s_("t_ok"), s_("p_ps"), s_("p_ok")
        g_ps, g_ok, q_ps, q_ok, o_ps = s_("g_ps"), s_("g_ok"), s_("q_ps"), s_("q_ok"), s_("o_ps")
        hb_ok, res_ok = s_("hb_ok"), s_("res_ok")
        stored = [s_("stored0"), s_("stored1")]

        def in_steps(eng, begin, finish):
            begin(0, 0)
            with eng.Fori(0, NCH // 2 - 1) as i:
                for buf in (1, 0):
                    n = 2 * i + 2 - buf
                    begin(n, buf)
                    finish(n - 1, 1 - buf)
            begin(NCH - 1, 1)
            finish(NCH - 2, 0)
            finish(NCH - 1, 1)

        with nc.Block() as block:
            @block.sync
            def _(sp):
                for z in range(2):
                    sp.dma_start(wo[:, z * ND:(z + 1) * ND], ow_scr[z]).then_inc(w_in, 16)
                sp.dma_start(wu1[:, :, :], u1.rearrange("(k p) r -> p k r", p=P)).then_inc(w_in, 16)
                sp.dma_start(wv1[:, :], v1).then_inc(w_in, 16)
                sp.dma_start(bias1[:, :], b1.rearrange("(k p) -> p k", p=P), allow_slow_non_contiguous=True).then_inc(w_in, 16)
                sp.dma_start(wu2[:, :, :], u2.rearrange("(k p) r -> p k r", p=P)).then_inc(w_in, 16)
                sp.dma_start(wv2[:, :], v2).then_inc(w_in, 16)
                sp.dma_start(bias2[:, :], b2.partition_broadcast(P)).then_inc(w_in, 16)
                for b, c, n, buf in batch_chunks(sp):
                    sp.wait_ge(res_ok, ONE + n + 1)
                    sp.dma_start(out[bass.ds(n * 4, 4)].rearrange("t p d -> p t d"), res[:, buf]).then_inc(stored[buf], 16)
                for buf in range(2):
                    sp.wait_ge(stored[buf], ONE + 16 * NCH // 2)

            @block.gpsimd
            def _(pool):
                identity(nc.gpsimd, ident[:, :], cleared, ident_ok)
                nc.gpsimd.memset(eps[:, :], LN_EPS).then_inc(eps_ok, 1)
                for b, c, n, buf in batch_chunks(pool):
                    pool.wait_ge(h_ps, ONE + n - buf)
                    pool.wait_ge(hb_ok, ONE + n - buf)
                    for z in range(2):
                        pool.dma_start(y[:, buf, z * ND:(z + 1) * ND],
                                       y_scr[z, bass.ds(b, 1), :, bass.ds(c * CH, CH)].rearrange("b (k p) s -> p (b k) s", p=P)
                                       ).then_inc(y_in[buf], 16)
                    pool.dma_start(h[:, buf], h_scr[bass.ds(n * 4, 4)].rearrange("t p d -> p t d")).then_inc(y_in[buf], 16)

            @block.tensor
            def _(pe):
                def project(n, buf):
                    pe.wait_ge(y_in[buf], (n - buf) * 24 + 48)
                    pe.wait_ge(h_ok, ONE + n)
                    for t in range(4):
                        for k in range(NY):
                            last = nc.tensor.matmul(ps_h[:, t], y[:, buf, k, t * P:(t + 1) * P], wo[:, k],
                                                    start=k == 0, stop=k == NY - 1)
                    last.then_inc(h_ps, 1)

                def ffn(n, buf):
                    pe.wait_ge(xn_ok, ONE + n + 1)
                    pe.wait_ge(res_ok, ONE + n)
                    for t in range(4):
                        for k in range(KD):
                            last = nc.tensor.transpose(ps_t[:, k, t * P:(t + 1) * P], xn[:, buf, t, k * P:(k + 1) * P], ident[:, :])
                    last.then_inc(t_ps, 1)
                    pe.wait_ge(t_ok, ONE + n + 1)
                    for k in range(KD):
                        last = nc.tensor.matmul(ps_p[:, :], wu1[:, k], xt[:, k], start=k == 0, stop=k == KD - 1)
                    last.then_inc(p_ps, 1)
                    pe.wait_ge(p_ok, ONE + n + 1)

                    def down(k):
                        pe.wait_ge(g_ok, ONE + n * NF + k + 3)
                        return nc.tensor.matmul(ps_q[:, :], wu2[:, k], hid[:, buf, k], start=k == 0, stop=k == NF - 1)

                    for m in range(NF):
                        pe.wait_ge(g_ok, ONE + n * NF + m + 1)
                        nc.tensor.matmul(ps_g[m % 2][:, :], wv1[:, m * P:(m + 1) * P], pt[:, :], start=True, stop=True
                                         ).then_inc(g_ps, 1)
                        if m >= 2:
                            down(m - 2)
                    down(NF - 2)
                    down(NF - 1).then_inc(q_ps, 1)
                    pe.wait_ge(q_ok, ONE + n + 1)
                    for t in range(4):
                        last = nc.tensor.matmul(ps_o[:, t], qt[:, t * P:(t + 1) * P], wv2[:, :], start=True, stop=True)
                    last.then_inc(o_ps, 1)

                pe.wait_ge(w_in, ONE + 8 * 16)
                pe.wait_ge(ident_ok, ONE + 1)
                in_steps(pe, project, ffn)

            @block.scalar
            def _(act):
                def root(n, buf):
                    act.wait_ge(mv_ok, ONE + n + 1)
                    nc.scalar.activation(std[:, :], mv[:, :, 1], ACT.Sqrt, bias=eps[:, :]).then_inc(std_ok, 1)

                def ffn(n, buf):
                    act.wait_ge(t_ps, ONE + n + 1)
                    nc.scalar.activation(xt[:, :, :], ps_t[:, :, :], ACT.Copy).then_inc(t_ok, 1)
                    act.wait_ge(p_ps, ONE + n + 1)
                    nc.scalar.activation(pt[:, :], ps_p[:, :], ACT.Copy).then_inc(p_ok, 1)
                    for m in range(NF):
                        act.wait_ge(g_ps, ONE + n * NF + m + 1)
                        nc.scalar.activation(hid[:, buf, m], ps_g[m % 2][:, :], ACT.Gelu_apprx_tanh,
                                             bias=bias1[:, m:m + 1]).then_inc(g_ok, 1)
                    act.wait_ge(q_ps, ONE + n + 1)
                    nc.scalar.activation(qt[:, :], ps_q[:, :], ACT.Copy).then_inc(q_ok, 1)

                act.wait_ge(eps_ok, ONE + 1)
                act.wait_ge(w_in, ONE + 8 * 16)
                act.sem_inc(g_ok, 2)
                in_steps(act, root, ffn)

            @block.vector
            def _(dve):
                def norm(n, buf):
                    dve.wait_ge(h_ps, ONE + n + 1)
                    dve.wait_ge(y_in[buf], (n - buf) * 24 + 48)
                    nc.vector.tensor_tensor(h[:, buf], ps_h[:, :, :], h[:, buf], ALU.add).then_inc(h_ok, 1)
                    dve.wait_ge(h_ok, ONE + n + 1)
                    normalize(nc, dve, h[:, buf], stats, mv, std[:, :], rstd[:, :], xn[:, buf], (step, mv_ok, std_ok, xn_ok), n)
                    dve.wait_ge(stored[buf], ONE + (n - buf) * 8)
                    nc.vector.tensor_tensor(res[:, buf], h[:, buf], bias2[:, None, :].to_broadcast([P, 4, D]),
                                            ALU.add).then_inc(hb_ok, 1)

                def finish(n, buf):
                    dve.wait_ge(hb_ok, ONE + n + 1)
                    dve.wait_ge(o_ps, ONE + n + 1)
                    nc.vector.tensor_tensor(res[:, buf], ps_o[:, :, :], res[:, buf], ALU.add).then_inc(res_ok, 1)

                dve.wait_ge(w_in, ONE + 8 * 16)
                in_steps(dve, norm, finish)


def lm_tower(nc, a, out):
    def scratch(name, shape, dt):
        return nc.dram_tensor(name, shape, dt, kind="Internal").ap()

    q_scr = scratch("q_scr", [PARTS, B, D, S], BF16)
    k_scr = scratch("k_scr", [PARTS, B, D, S], BF16)
    o_scr = scratch("o_scr", [G, HG, DK + 1, S], FP32)
    h_scr = scratch("h_scr", [T // P, P, D], FP32)
    xn_scr = scratch("xn_scr", [B, D, S], FP32)
    y_scr = scratch("y_scr", [2, B, DI, S], FP32)
    win_scr = scratch("win_scr", [2, D, 2 * DI], FP32)
    xp_scr = scratch("xp_scr", [2, P, ND, XPW], FP32)
    dtw_scr = scratch("dtw_scr", [2, R, DI], FP32)
    ow_scr = scratch("ow_scr", [2, P, ND, D], FP32)
    names = ("in_w", "conv_w", "conv_b", "xproj_w", "dt_w", "dt_b", "A_log", "D", "out_w")
    dirs = [{n: a[f"L0_attn_{z}_{n}"] for n in names} for z in "fb"]

    with semaphores(nc) as sem:
        transpose_weights(nc, sem, dirs, win_scr, xp_scr, dtw_scr, ow_scr)
    with nc.sbuf_tensor("v_all", [P, B, H // HG, NT, HG * DK], FP32) as v_all:
        with semaphores(nc) as sem:
            embed_and_project(nc, sem, a["x"], a["L0_tok_emb"], [a[f"L0_tok_w{n}"] for n in "qkv"],
                              [a[f"L0_tok_b{n}"] for n in "qkv"], q_scr, k_scr, v_all)
        with semaphores(nc) as sem:
            attention(nc, sem, q_scr, k_scr, v_all, o_scr)
    with semaphores(nc) as sem:
        attention_out(nc, sem, o_scr, a["L0_tok_wo"], a["L0_tok_bo"], h_scr, xn_scr)
    for z in range(2):
        with semaphores(nc) as sem:
            mamba(nc, sem, "fb"[z] + "_", z == 1, dirs[z], win_scr[z], xp_scr[z], dtw_scr[z], xn_scr, y_scr[z])
    with semaphores(nc) as sem:
        mamba_out_and_ffn(nc, sem, y_scr, ow_scr, h_scr, a["L0_ffn_U1"], a["L0_ffn_V1"], a["L0_ffn_b1"],
                          a["L0_ffn_U2"], a["L0_ffn_V2"], a["L0_ffn_b2"],
                          out.rearrange("b (t p) d -> (b t) p d", p=P))


def kernel(**inputs):
    import concourse.bacc as bacc
    from concourse.bass_utils import run_bass_kernel_spmd

    nc = bacc.Bacc("TRN2", target_bir_lowering=False, num_devices=1)
    arrays, args = {}, {}
    for name, value in inputs.items():
        value = np.ascontiguousarray(value)
        arrays[f"in_{name}_dram"] = value
        args[name] = nc.dram_tensor(f"in_{name}_dram", value.shape, mybir.dt.from_np(value.dtype), kind="ExternalInput").ap()
    out = nc.dram_tensor("out_0_dram", (B, S, D), FP32, kind="ExternalOutput").ap()
    lm_tower(nc, args, out)
    result = run_bass_kernel_spmd(nc, [arrays], core_ids=[0])
    return result.results[0]["out_0_dram"]
```

```python
import concourse.bass as bass
from concourse import mybir
from contextlib import ExitStack, contextmanager
import numpy as np

FP32 = mybir.dt.float32
BF16 = mybir.dt.bfloat16
I32 = mybir.dt.int32
U32 = mybir.dt.uint32
ALU = mybir.AluOpType
ACT = mybir.ActivationFunctionType
AX = mybir.AxisListType

P = 128
B, S, D = 2, 2048, 256
T = B * S
VOCAB = 8000
H, DK = 16, 16
HG = 4
G = B * H // HG
PARTS = 3
Q_PART = [0, 0, 1, 1, 0, 2, 1]
K_PART = [0, 1, 0, 1, 2, 0, 2]
KQ = DK * len(Q_PART)
KQM = KQ + PARTS
CH = 512
NC = S // CH
NT = S // P
KD = D // P
VW = 32
LN_EPS = 1e-5
DI, DS, DC, R = 512, 16, 4, 16
ND = DI // P
TC = 1024
X_B, X_C, X_DT = 0, 32, 64
X_BC = (X_B, X_C)
XPW = X_DT + R
FF, RK = 1024, 64
TWO_BF16_ONES = float(np.array([0x3F803F80], np.uint32).view(np.float32)[0])


ONE = 1



@contextmanager
def semaphores(nc):
    taken = []

    def sem(name, start=ONE):
        taken.append(nc.alloc_semaphore(name=name))
        if start:
            nc.sync.sem_inc(taken[-1], start)
        return taken[-1]

    yield sem
    nc.clear_and_free_semaphores(taken)
    nc.all_engine_barrier()


def identity(pool, tile, cleared, done):
    pool.memset(tile, 0.0).then_inc(cleared, 1)
    pool.wait_ge(cleared, ONE + 1)
    pool.affine_select(out=tile, in_=tile, compare_op=ALU.not_equal, fill=1.0, base=0,
                       pattern=[[-1, tile.shape[1]]], channel_multiplier=1).then_inc(done, 1)


def embed_and_project(nc, sem, x, emb, weights, biases, q_scr, k_scr, v_all):
    with ExitStack() as ctx:
        def sb(name, shape, dt):
            return ctx.enter_context(nc.sbuf_tensor(name, shape, dt))

        def pb(name, shape, dt):
            return ctx.enter_context(nc.psum_tensor(name, shape, dt))

        ident = sb("p_ident", [P, P], FP32)
        w_sb = [sb(f"p_w{n}", [P, KD, D], FP32) for n in "qkv"]
        b_col = [sb(f"p_b{n}", [P, KD], FP32) for n in "qk"]
        bv_row = sb("p_bv", [P, D], FP32)
        NI = T // P
        ids_i = sb("p_ids_i", [NI, P], I32)
        ids_f = sb("p_ids_f", [NI, 4, P], FP32)
        ids_t = sb("p_ids_t", [P, NI], U32)
        ids_c = sb("p_ids_c", [P, 2, 4], U32)
        rows = sb("p_rows", [P, 2, 4, D], FP32)
        hT = sb("p_hT", [P, 2, KD, CH], FP32)
        full = [sb(f"p_full{n}", [P, KD, CH], FP32) for n in "qk"]
        rest = sb("p_rest", [P, KD, CH], FP32)
        parts = [sb(f"p_parts{n}", [P, 2, PARTS, KD, CH], BF16) for n in "qk"]
        ps_t = pb("p_ps_t", [P, KD, CH], FP32)
        ps_qk = [pb(f"p_ps_{n}", [P, KD, CH], FP32) for n in "qk"]
        ps_v = pb("p_ps_v", [P, 4, D], FP32)

        ids_in = sem("ids_in")
        w_in = sem("w_in")
        cleared, ident_ok = sem("p_cleared"), sem("p_ident_ok")
        ids_step, ids_col, ids_ok = sem("ids_step"), sem("ids_col"), sem("ids_ok")
        ids_copied = sem("ids_copied")
        rows_in = [sem("rows_in0", 0), sem("rows_in1", 0)]
        rows_free = sem("rows_free")
        ht_ps, ht_ok = sem("ht_ps"), sem("ht_ok")
        mm_done = [sem("q_mm"), sem("k_mm")]
        v_mm, v_ok = sem("v_mm"), sem("v_ok")
        full_ok = [sem("q_full"), sem("k_full")]
        step = sem("p_split_step")
        parts_ok = [sem("q_parts"), sem("k_parts")]
        stored = [[sem(f"{n}_stored{p}") for p in range(2)] for n in "qk"]

        def chunks(eng):
            with eng.Fori(0, B) as b:
                with eng.Fori(0, NC // 2) as j:
                    for buf in range(2):
                        yield b, j * 2 + buf, b * NC + j * 2 + buf, buf

        with nc.Block() as block:
            @block.sync
            def _(sp):
                sp.dma_start(ids_i[:, :], x.rearrange("b (n p) -> (b n) p", p=P)).then_inc(ids_in, 16)
                for w, src in zip(w_sb, weights):
                    sp.dma_start(w[:, :, :], src.rearrange("(k p) n -> p k n", p=P)).then_inc(w_in, 16)
                for bc, src in zip(b_col, biases):
                    sp.dma_start(bc[:, :], src.rearrange("(k p) -> p k", p=P),
                                 allow_slow_non_contiguous=True).then_inc(w_in, 16)
                sp.dma_start(bv_row[:, :], biases[2].partition_broadcast(P)).then_inc(w_in, 16)
                for b, c, n, buf in chunks(sp):
                    for a, scr in enumerate((q_scr, k_scr)):
                        sp.wait_ge(parts_ok[a], ONE + n + 1)
                        for i in range(PARTS):
                            dst = scr[i, bass.ds(b, 1), :, bass.ds(c * CH, CH)].rearrange("b (k p) s -> p (b k) s", p=P)
                            sp.dma_start(dst, parts[a][:, buf, i]).then_inc(stored[a][buf], 16)
                for a in range(2):
                    for buf in range(2):
                        sp.wait_ge(stored[a][buf], ONE + 16 * PARTS * B * NC // 2)

            @block.gpsimd
            def _(pool):
                identity(nc.gpsimd, ident[:, :], cleared, ident_ok)
                for b, c, n, buf in chunks(pool):
                    pool.wait_ge(rows_free, ONE + n + 1)
                    pool.wait_ge(ids_ok, ONE + 1)
                    nc.gpsimd.tensor_copy(ids_c[:, buf], ids_t[:, bass.ds(n * 4, 4)]).then_inc(ids_copied, 1)
                    pool.wait_ge(ids_copied, ONE + n + 1)
                    pool.nop(nofuse=True)
                    for t in range(4):
                        nc.gpsimd.indirect_dma_start(
                            rows[:, buf, t], None, emb,
                            bass.IndirectOffsetOnAxis(ids_c[:, buf, t:t + 1], 0)).then_inc(rows_in[buf], 16)

            @block.tensor
            def _(pe):
                pe.wait_ge(ident_ok, ONE + 1)
                pe.wait_ge(ids_step, ONE + 4)
                nc.tensor.transpose(ps_t[:, 0, 0:NI], ids_f[:, 3], ident[0:NI, 0:NI]).then_inc(ids_col, 1)
                pe.wait_ge(ids_ok, ONE + 1)
                pe.wait_ge(w_in, ONE + 96)
                pe.sem_inc(rows_free, 2)
                for b, c, n, buf in chunks(pe):
                    pe.wait_ge(rows_in[buf], (n - buf) * 32 + 64)
                    pe.wait_ge(ht_ok, ONE + n)
                    for t in range(4):
                        for k in range(KD):
                            last = nc.tensor.transpose(ps_t[:, k, t * P:(t + 1) * P],
                                                       rows[:, buf, t, k * P:(k + 1) * P], ident[:, :])
                            if t == 3 and k == KD - 1:
                                last.then_inc(ht_ps, 1)
                    pe.wait_ge(ht_ps, ONE + n + 1)
                    pe.sem_inc(rows_free, 1)
                    pe.wait_ge(ht_ok, ONE + n + 1)
                    for a in range(2):
                        pe.wait_ge(full_ok[a], ONE + KD * n)
                        for m in range(KD):
                            for k in range(KD):
                                last = nc.tensor.matmul(ps_qk[a][:, m], w_sb[a][:, k, m * P:(m + 1) * P],
                                                        hT[:, buf, k], start=k == 0, stop=k == KD - 1)
                        last.then_inc(mm_done[a], 1)
                    pe.wait_ge(v_ok, ONE + n)
                    for t in range(4):
                        for k in range(KD):
                            last = nc.tensor.matmul(ps_v[:, t], hT[:, buf, k, t * P:(t + 1) * P], w_sb[2][:, k],
                                                    start=k == 0, stop=k == KD - 1)
                    last.then_inc(v_mm, 1)

            @block.scalar
            def _(act):
                act.wait_ge(w_in, ONE + 96)
                for b, c, n, buf in chunks(act):
                    act.wait_ge(ht_ps, ONE + n + 1)
                    nc.scalar.activation(hT[:, buf], ps_t[:, :, :], ACT.Copy).then_inc(ht_ok, 1)
                    for a in range(2):
                        act.wait_ge(mm_done[a], ONE + n + 1)
                        act.wait_ge(parts_ok[a], ONE + n)
                        for m in range(KD):
                            nc.scalar.activation(full[a][:, m], ps_qk[a][:, m], ACT.Identity,
                                                 bias=b_col[a][:, m:m + 1]).then_inc(full_ok[a], 1)

            @block.vector
            def _(dve):
                dve.wait_ge(ids_in, ONE + 16)
                nc.vector.tensor_copy(ids_f[:, 0], ids_i[:, :]).then_inc(ids_step, 1)
                dve.wait_ge(ids_step, ONE + 1)
                nc.vector.tensor_scalar(ids_f[:, 1], ids_f[:, 0], 0.0, float(VOCAB), ALU.is_lt, ALU.mult).then_inc(ids_step, 1)
                dve.wait_ge(ids_step, ONE + 2)
                nc.vector.tensor_tensor(ids_f[:, 2], ids_f[:, 0], ids_f[:, 1], ALU.add).then_inc(ids_step, 1)
                dve.wait_ge(ids_step, ONE + 3)
                nc.vector.tensor_scalar(ids_f[:, 3], ids_f[:, 2], float(VOCAB - 1), 0.0, ALU.min, ALU.max).then_inc(ids_step, 1)
                dve.wait_ge(ids_col, ONE + 1)
                nc.vector.tensor_copy(ids_t[:, :], ps_t[:, 0, 0:NI]).then_inc(ids_ok, 1)
                dve.wait_ge(w_in, ONE + 96)
                for b, c, n, buf in chunks(dve):
                    for a in range(2):
                        dve.wait_ge(full_ok[a], ONE + KD * n + KD)
                        dve.wait_ge(stored[a][buf], ONE + (n - buf) * 8 * PARTS)
                        part = [parts[a][:, buf, i] for i in range(PARTS)]
                        done = (n * 2 + a) * 3
                        nc.vector.tensor_copy(part[0], full[a][:, :, :]).then_inc(step, 1)
                        dve.wait_ge(step, ONE + done + 1)
                        nc.vector.tensor_tensor(rest[:, :, :], full[a][:, :, :], part[0], ALU.subtract).then_inc(step, 1)
                        dve.wait_ge(step, ONE + done + 2)
                        nc.vector.tensor_copy(part[1], rest[:, :, :]).then_inc(step, 1)
                        dve.wait_ge(step, ONE + done + 3)
                        nc.vector.tensor_tensor(part[2], rest[:, :, :], part[1], ALU.subtract).then_inc(parts_ok[a], 1)
                        dve.wait_ge(parts_ok[a], ONE + n + 1)
                    dve.wait_ge(v_mm, ONE + n + 1)
                    for g in range(H // HG):
                        cols = slice(g * HG * DK, (g + 1) * HG * DK)
                        last = nc.vector.tensor_tensor(
                            v_all[:, bass.ds(b, 1), g, bass.ds(c * 4, 4)].rearrange("p b t d -> p (b t) d"),
                            ps_v[:, :, cols],
                            bv_row[:, None, cols].to_broadcast([P, 4, HG * DK]), ALU.add)
                    last.then_inc(v_ok, 1)


def weight_transposes(nc, sem, sb, ident, banks, dirs, win_scr, xp_scr, dtw_scr, ow_scr):
    win = sb("w_in", [P, 2, 2 * DI // P, D], FP32)
    xp = sb("w_xp", [R + 2 * DS, 2, DI], FP32)
    dtw = sb("w_dt", [P, 2, ND, R], FP32)
    ow = sb("w_out", [P, 2, KD, DI], FP32)
    win_t = sb("w_in_t", [P, 2, KD, 2 * DI], FP32)
    xp_t = sb("w_xp_t", [P, 2, ND, XPW], FP32)
    dtw_t = sb("w_dt_t", [R, 2, DI], FP32)
    ow_t = sb("w_out_t", [P, 2, ND, D], FP32)
    loaded, pads_ok = sem("w_loaded"), sem("w_pads_ok")
    transposed, copied, stored = sem("w_transposed"), sem("w_copied"), sem("w_stored")

    blocks = []
    for z in range(2):
        for m in range(2 * DI // P):
            for k in range(KD):
                blocks.append((win[:, z, m, k * P:(k + 1) * P], P, P,
                               [(win_t[:, z, k, m * P:(m + 1) * P], 0, P)]))
        for k in range(ND):
            cols = slice(k * P, (k + 1) * P)
            blocks.append((xp[:, z, cols], R + 2 * DS, P,
                           [(xp_t[:, z, k, X_DT:X_DT + R], 0, R), (xp_t[:, z, k, X_B:X_B + DS], R, R + DS),
                            (xp_t[:, z, k, X_C:X_C + DS], R + DS, R + 2 * DS)]))
            blocks.append((dtw[:, z, k], P, R, [(dtw_t[:, z, cols], 0, P)]))
            for m in range(KD):
                blocks.append((ow[:, z, m, cols], P, P, [(ow_t[:, z, k, m * P:(m + 1) * P], 0, P)]))


    def load(eng):
        for z, w in enumerate(dirs):
            eng.dma_start(win[:, z], w["in_w"].rearrange("(m p) k -> p m k", p=P)).then_inc(loaded, 16)
            eng.dma_start(xp[:, z], w["xproj_w"]).then_inc(loaded, 16)
            eng.dma_start(dtw[:, z], w["dt_w"].rearrange("(k p) r -> p k r", p=P)).then_inc(loaded, 16)
            eng.dma_start(ow[:, z], w["out_w"].rearrange("(m p) k -> p m k", p=P)).then_inc(loaded, 16)

    def clear():
        nc.gpsimd.memset(xp_t[:, :, :, :], 0.0).then_inc(pads_ok, 1)

    def transpose(pe, i):
        src, rows, cols, _ = blocks[i]
        if i == 0:
            pe.wait_ge(loaded, ONE + 8 * 16)
        if i >= len(banks):
            pe.wait_ge(copied, ONE + i - len(banks) + 1)
        nc.tensor.transpose(banks[i % len(banks)][0:cols, 0:rows], src, ident[0:rows, 0:rows]).then_inc(transposed, 1)

    def copy(act, i):
        _, rows, cols, dsts = blocks[i]
        if i == 0:
            act.wait_ge(pads_ok, ONE + 1)
        act.wait_ge(transposed, ONE + i + 1)
        for dst, a, b in dsts:
            last = nc.scalar.activation(dst, banks[i % len(banks)][0:cols, a:b], ACT.Copy)
        last.then_inc(copied, 1)

    def store(eng):
        eng.wait_ge(copied, ONE + len(blocks))
        for z in range(2):
            eng.dma_start(win_scr[z].rearrange("(k p) m -> p k m", p=P), win_t[:, z]).then_inc(stored, 16)
            eng.dma_start(xp_scr[z], xp_t[:, z]).then_inc(stored, 16)
            eng.dma_start(dtw_scr[z], dtw_t[:, z]).then_inc(stored, 16)
            eng.dma_start(ow_scr[z], ow_t[:, z]).then_inc(stored, 16)

    return load, clear, transpose, copy, store, len(blocks), copied, stored


def attention(nc, sem, q_scr, k_scr, v_all, o_scr, weights):
    with ExitStack() as ctx:
        def sb(name, shape, dt):
            return ctx.enter_context(nc.sbuf_tensor(name, shape, dt))

        def pb(name, shape, dt):
            return ctx.enter_context(nc.psum_tensor(name, shape, dt))

        k_st = sb("a_k", [P, 2, HG, S], BF16)
        q_st = sb("a_q", [P, 2, NC, HG, CH], BF16)
        v_st = sb("a_v", [P, 2, NT, HG, VW], FP32)
        probs = sb("a_probs", [P, 2, HG, CH], FP32)
        o_sb = sb("a_o", [P, CH], FP32)
        ident = sb("a_ident", [P, P], BF16)
        NM = HG * NC
        mx = sb("a_mx", [P, NM, NC], FP32)
        neg = sb("a_neg", [P, NM], FP32)
        neg_rest = sb("a_neg_rest", [P, NM], FP32)
        neg_parts = sb("a_neg_parts", [P, PARTS, NM], BF16)
        neg_rows = sb("a_neg_rows", [PARTS * NM, P], BF16)
        ps_s = [pb(f"a_ps_s{i}", [P, 2, CH], FP32) for i in range(2)]
        ps_m = pb("a_ps_m", [P, 3, CH], FP32)
        ps_o = pb("a_ps_o", [P, CH], FP32)

        ident32 = sb("a_ident32", [P, P], FP32)
        w_load, w_clear, w_transpose, w_copy, w_store, w_count, w_copied, w_stored = weight_transposes(
            nc, sem, sb, ident32, [ps_s[i // 2][:, i % 2] for i in range(4)], *weights)

        a_cleared, a_ident_ok = sem("a_cleared"), sem("a_ident_ok")
        ident32_ok = sem("a_ident32_ok")
        consts = sem("a_consts")
        ones_ok = sem("ones_ok")
        loaded = [[sem(f"loaded{p}{h}") for h in range(HG)] for p in range(2)]
        v_staged = sem("v_staged")
        scored = sem("scored")
        exped = sem("exped")
        pv_done = sem("pv_done")
        o_copied = sem("o_copied")
        o_stored = sem("o_stored")
        m_scored = sem("m_scored")
        m_maxed = sem("m_maxed")
        neg_ok = sem("neg_ok")
        neg_step, neg_split = sem("neg_step"), sem("neg_split")
        neg_ps, neg_t, neg_in = sem("neg_ps"), sem("neg_t"), sem("neg_in")

        BLK = NM * NC
        AHEAD = 2
        NEG = 15
        ITEMS = BLK + 1

        def item(i):
            return i if i < NEG else i + 1

        def bank(i):
            return ps_m[:, item(i) % 3]

        ps_n = ps_m[0:PARTS * NM, NEG % 3].bitcast(BF16)[:, 0:P]

        def groups(eng, body):
            with eng.Fori(0, (G - 2) // 2) as i:
                for buf in range(2):
                    body(i * 2 + buf, buf, False)
            body(G - 2, 0, False)
            body(G - 1, 1, True)

        def groups_first(eng, body):
            body(0, 0, True, False)
            with eng.Fori(0, (G - 2) // 2) as i:
                body(i * 2 + 1, 1, False, False)
                body(i * 2 + 2, 0, False, False)
            body(G - 1, 1, False, True)

        with nc.Block() as block:
            @block.sync
            def _(sp):
                def load(g, buf, heads=range(HG), parts=range(len(Q_PART))):
                    for h in heads:
                        for stack, scr, part in ((k_st, k_scr, K_PART), (q_st, q_scr, Q_PART)):
                            src = scr.rearrange("a b (g h d) s -> a (b g) h d s", h=HG, d=DK)
                            for i in parts:
                                a = part[i]
                                rows = src[a, bass.ds(g, 1), h].rearrange("g d s -> (g d) s")
                                dst = stack[i * DK:(i + 1) * DK, buf]
                                if stack is k_st:
                                    sp.dma_start(dst[:, h], rows).then_inc(loaded[buf][h], 16)
                                else:
                                    sp.dma_start(dst[:, :, h], rows.rearrange("d (c s) -> d c s", s=CH)
                                                 ).then_inc(loaded[buf][h], 16)

                def store_neg(m, buf, c):
                    sp.wait_ge(neg_t, ONE + m + 1)
                    for i in range(PARTS):
                        dst = q_st[KQ + i:KQ + i + 1, buf, bass.ds(c, 1)].rearrange("a c h (s n) -> a (c h s) n", n=P)
                        sp.dma_start(dst, neg_rows[i * NM:(i + 1) * NM, :]).then_inc(neg_in, 16)
                    sp.wait_ge(neg_in, ONE + 16 * PARTS * (m + 1))
                    sp.nop(nofuse=True)

                first_parts, last_part = range(len(Q_PART) - 1), [len(Q_PART) - 1]
                load(0, 0, [0], first_parts)
                sp.wait_ge(ones_ok, ONE + 1)
                load(0, 0, [0], last_part)
                load(0, 0, range(1, HG))
                store_neg(0, 0, 0)
                sp.wait_ge(ones_ok, ONE + 2)
                load(1, 1)

                def store_out(g, c):
                    sp.wait_ge(o_copied, ONE + g * NC + c + 1)
                    for h in range(HG):
                        sp.dma_start(o_scr[bass.ds(g, 1), h, :, bass.ds(c * CH, CH)].rearrange("g r s -> (g r) s"),
                                     o_sb[h * VW:h * VW + DK + 1, :]).then_inc(o_stored, 16)

                def body(g, buf, last):
                    with sp.Fori(1, NC) as c:
                        store_neg(g * NC + c, buf, c)
                        store_out(g, c - 1)
                    if not last:
                        store_neg(g * NC + NC, 1 - buf, 0)
                    store_out(g, NC - 1)
                    if not last:
                        if not (isinstance(g, int) and g == G - 2):
                            sp.wait_ge(scored, ONE + (g + 1) * NC * NT * 2)
                            load(g + 2, buf)
                groups(sp, body)
                sp.wait_ge(o_stored, ONE + 16 * HG * G * NC)

            @block.gpsimd
            def _(pool):
                nc.gpsimd.memset(v_st[:, :, :, :, :], 0.0).then_inc(consts, 1)
                pool.wait_ge(consts, ONE + 1)
                nc.gpsimd.memset(v_st[:, :, :, :, DK:DK + 1], 1.0).then_inc(consts, 1)
                pool.wait_ge(consts, ONE + 2)
                identity(nc.gpsimd, ident[:, :], a_cleared, a_ident_ok)
                pool.wait_ge(a_ident_ok, ONE + 1)
                nc.gpsimd.tensor_copy(ident32[:, :], ident[:, :]).then_inc(ident32_ok, 1)
                w_clear()

                def stage_v(g, buf):
                    pool.nop(nofuse=True)
                    nc.gpsimd.tensor_copy(
                        v_st[:, buf, :, :, 0:DK],
                        v_all.rearrange("p b g t (h d) -> p (b g) t h d", d=DK)[:, bass.ds(g, 1)]
                        .rearrange("p g t h d -> p (g t) h d")).then_inc(v_staged, 1)

                def split(m):
                    pool.wait_ge(neg_ok, ONE + m + 1)
                    pool.wait_ge(neg_ps, ONE + m)
                    pool.nop(nofuse=True)
                    nc.gpsimd.tensor_copy(neg_parts[:, 0], neg[:, :]).then_inc(neg_step, 1)
                    pool.wait_ge(neg_step, ONE + m * 3 + 1)
                    nc.gpsimd.tensor_tensor(neg_rest[:, :], neg[:, :], neg_parts[:, 0], ALU.subtract).then_inc(neg_step, 1)
                    pool.wait_ge(neg_step, ONE + m * 3 + 2)
                    pool.nop(nofuse=True)
                    nc.gpsimd.tensor_copy(neg_parts[:, 1], neg_rest[:, :]).then_inc(neg_step, 1)
                    pool.wait_ge(neg_step, ONE + m * 3 + 3)
                    nc.gpsimd.tensor_tensor(neg_parts[:, 2], neg_rest[:, :], neg_parts[:, 1], ALU.subtract).then_inc(neg_split, 1)
                    pool.wait_ge(neg_split, ONE + m + 1)

                stage_v(0, 0)
                with pool.Fori(0, AHEAD) as c:
                    split(c)

                def body(g, buf, last):
                    if not last:
                        pool.wait_ge(pv_done, ONE + g * NC * NT)
                        pool.nop(nofuse=True)
                        stage_v(g + 1, 1 - buf)
                    with pool.Fori(AHEAD, NC if last else NC + AHEAD) as c:
                        split(g * NC + c)
                groups(pool, body)

            @block.tensor
            def _(pe):
                def max_blocks(m, buf, c, first, end, loads=None):
                    for i in range(first, end):
                        h, st, tc = i // 16, i // 4 % 4, i % 4
                        if i % 16 == 0 and loads is not None:
                            pe.wait_ge(loaded[buf][h], ONE + loads)
                        before = item(i) - 3
                        if before == NEG:
                            pe.wait_ge(neg_t, ONE + m)
                        elif before > NEG:
                            pe.wait_ge(m_maxed, ONE + m * BLK + before + 2)
                        elif before >= 0:
                            pe.wait_ge(m_maxed, ONE + m * BLK + before + 3)
                        else:
                            pe.wait_ge(m_maxed, ONE + m * BLK + (1, 2, 0)[i])
                        nc.tensor.matmul(bank(i), q_st[0:KQ, buf, bass.ds(c, 1), h, st * P:(st + 1) * P].rearrange("p c n -> p (c n)"),
                                         k_st[0:KQ, buf, h, tc * CH:(tc + 1) * CH],
                                         start=True, stop=True).then_inc(m_scored, 1)

                def transpose_neg(m, read):
                    pe.wait_ge(neg_split, ONE + m + 1)
                    pe.wait_ge(m_maxed, ONE + read)
                    pe.nop(nofuse=True)
                    nc.tensor.transpose(ps_n, neg_parts[:, :, :].rearrange("p a m -> p (a m)"),
                                        ident[:, :]).then_inc(neg_ps, 1)

                def values(buf, t):
                    for h in range(HG):
                        last = nc.tensor.matmul(ps_o[h * VW:(h + 1) * VW, :], v_st[:, buf, t, h],
                                                probs[:, t % 2, h], start=t == 0, stop=t == NT - 1)
                    last.then_inc(pv_done, 1)

                def chunk(g, buf, c, v_buf, m_buf, m_c, with_neg):
                    e = g * NC + c
                    pe.wait_ge(neg_in, ONE + 16 * PARTS * (e + 1))
                    taken = 0

                    def maximum():
                        nonlocal taken
                        if m_buf is not None:
                            loads = 16 * len(Q_PART) * (g + (3 if buf else 2)) if m_buf != buf else None
                            max_blocks(e + AHEAD, m_buf, m_c, taken, taken + 1, loads)
                            taken += 1

                    for t in range(NT):
                        maximum()
                        for half in range(2):
                            pe.wait_ge(exped, ONE + e * NT * 2 + t * 2 + half + 1)
                            for i in range(2):
                                last = nc.tensor.matmul(ps_s[half][:, i], k_st[0:KQM, buf, 2 * half + i, t * P:(t + 1) * P],
                                                        q_st[0:KQM, buf, bass.ds(c, 1), 2 * half + i].rearrange("p c n -> p (c n)"),
                                                        start=True, stop=True)
                                if i == 1:
                                    last.then_inc(scored, 1)
                                if i == half:
                                    maximum()
                        if with_neg and t == 3:
                            if m_buf is None:
                                transpose_neg(e + 1, G * NC * BLK + 2)
                            else:
                                transpose_neg(e + 1, (e + AHEAD) * BLK + NEG)
                        maximum()
                        if t > 0 or v_buf is not None:
                            pe.wait_ge(exped, ONE + e * NT * 2 + t * 2 + 2)
                            if t == 1:
                                pe.wait_ge(o_copied, ONE + e)
                            values(v_buf if t == 0 else buf, (t - 1) % NT)

                pe.wait_ge(a_ident_ok, ONE + 1)
                pe.wait_ge(consts, ONE + 2)
                PER_BLOCK = 2
                W_BLOCKS = w_count // PER_BLOCK
                max_blocks(0, 0, 0, 0, BLK - W_BLOCKS, 16 * 2 * len(Q_PART))
                pe.wait_ge(ident32_ok, ONE + 1)
                for i in range(W_BLOCKS):
                    for j in range(PER_BLOCK):
                        w_transpose(pe, PER_BLOCK * i + j)
                    max_blocks(0, 0, 0, BLK - W_BLOCKS + i, BLK - W_BLOCKS + i + 1, 16 * 2 * len(Q_PART))
                max_blocks(1, 0, 1, 0, NEG)
                transpose_neg(0, BLK + NEG)
                max_blocks(1, 0, 1, NEG, BLK)
                pe.wait_ge(w_copied, ONE + w_count)

                def body(g, buf, first, last):
                    pe.wait_ge(v_staged, ONE + g + 1)
                    pe.nop(nofuse=True)
                    chunk(g, buf, 0, None if first else 1 - buf, buf, AHEAD, True)
                    with pe.Fori(1, NC - AHEAD) as c:
                        chunk(g, buf, c, buf, buf, c + AHEAD, True)
                    if last:
                        with pe.Fori(NC - AHEAD, NC - 1) as c:
                            chunk(g, buf, c, buf, None, None, True)
                        chunk(g, buf, NC - 1, buf, None, None, False)
                    else:
                        with pe.Fori(NC - AHEAD, NC) as c:
                            chunk(g, buf, c, buf, 1 - buf, c - (NC - AHEAD), True)
                groups_first(pe, body)
                pe.wait_ge(exped, ONE + G * NC * NT * 2 + 2)
                values(1, NT - 1)

            @block.scalar
            def _(act):
                def copy_neg(m):
                    act.wait_ge(neg_ps, ONE + m + 1)
                    act.wait_ge(neg_in, ONE + 16 * PARTS * m)
                    nc.scalar.activation(neg_rows[:, :], ps_n, ACT.Copy).then_inc(neg_t, 1)

                def copy_out(e):
                    act.wait_ge(pv_done, ONE + NT * e)
                    act.wait_ge(o_stored, ONE + 16 * HG * (e - 1))
                    nc.scalar.activation(o_sb[:, :], ps_o[:, :], ACT.Copy).then_inc(o_copied, 1)

                def chunk(g, c, first, with_neg):
                    e = g * NC + c
                    for t in range(NT):
                        if t >= 1 or not first:
                            act.wait_ge(pv_done, ONE + e * NT + t - 1)
                        for half in range(2):
                            if with_neg and t == 3 and half == 1:
                                copy_neg(e + 1)
                            act.wait_ge(scored, ONE + e * NT * 2 + t * 2 + half + 1)
                            nc.scalar.activation(probs[:, t % 2, 2 * half:2 * half + 2], ps_s[half][:, :, :], ACT.Exp,
                                                 scale=float(DK) ** -0.5).then_inc(exped, 1)
                        if t == 0 and not first:
                            copy_out(e)

                act.sem_inc(exped, 2)
                w_load(act)
                for i in range(w_count):
                    w_copy(act, i)
                w_store(act)
                copy_neg(0)

                def body(g, buf, first, last):
                    chunk(g, 0, first, True)
                    with act.Fori(1, NC - 1 if last else NC) as c:
                        chunk(g, c, False, True)
                    if last:
                        chunk(g, NC - 1, False, False)
                groups_first(act, body)
                copy_out(G * NC)
                act.wait_ge(w_stored, ONE + 8 * 16)

            @block.vector
            def _(dve):
                def maxima(m):
                    for i in range(BLK):
                        dve.wait_ge(m_scored, ONE + m * BLK + i + 1)
                        if i == 0:
                            dve.wait_ge(neg_ok, ONE + m)
                        nc.vector.reduce_max(mx[:, i // NC, i % NC:i % NC + 1], bank(i), AX.X).then_inc(m_maxed, 1)
                    dve.wait_ge(m_maxed, ONE + m * BLK + BLK + 2)
                    dve.wait_ge(neg_split, ONE + m)
                    nc.vector.reduce_max(neg[:, :], mx[:, :, :], AX.X, negate=True).then_inc(neg_ok, 1)

                for buf in range(2):
                    nc.vector.memset(k_st[96:128, buf].rearrange("p h s -> p (h s)").bitcast(FP32),
                                     TWO_BF16_ONES).then_inc(ones_ok, 1)
                dve.sem_inc(m_maxed, 2)
                with dve.Fori(0, G * NC) as m:
                    maxima(m)


def normalize(nc, dve, h, stats, mv, std, rstd, xn, sems, n):
    step, mv_ok, std_ok, xn_ok = sems
    for t in range(4):
        last = nc.vector.bn_stats(stats[:, t], h[:, t])
    last.then_inc(step, 1)
    dve.wait_ge(step, ONE + 2 * n + 1)
    dve.nop(nofuse=True)
    for t in range(4):
        last = nc.vector.bn_aggr(mv[:, t], stats[:, t])
    last.then_inc(mv_ok, 1)
    dve.wait_ge(std_ok, ONE + n + 1)
    nc.vector.reciprocal(rstd, std).then_inc(step, 1)
    dve.wait_ge(step, ONE + 2 * n + 2)
    for t in range(4):
        last = nc.vector.tensor_scalar(xn[:, t], h[:, t], mv[:, t, 0:1], rstd[:, t:t + 1], ALU.subtract, ALU.mult)
    last.then_inc(xn_ok, 1)


def batch_chunks(eng):
    with eng.Fori(0, B) as b:
        with eng.Fori(0, NC // 2) as j:
            for buf in range(2):
                yield b, j * 2 + buf, b * NC + j * 2 + buf, buf


def in_steps(eng, begin, finish):
    chunks = T // CH
    begin(0, 0)
    with eng.Fori(0, chunks // 2 - 1) as i:
        for buf in (1, 0):
            n = 2 * i + 2 - buf
            begin(n, buf)
            finish(n - 1, 1 - buf)
    begin(chunks - 1, 1)
    finish(chunks - 2, 0)
    finish(chunks - 1, 1)


def attention_out(nc, sem, o_scr, inv_scr, wo, bo, h_scr, xn_scr):
    with ExitStack() as ctx:
        def sb(name, shape, dt):
            return ctx.enter_context(nc.sbuf_tensor(name, shape, dt))

        def pb(name, shape, dt):
            return ctx.enter_context(nc.psum_tensor(name, shape, dt))

        ident = sb("o_ident", [P, P], FP32)
        w = sb("o_w", [P, KD, D], FP32)
        bias = sb("o_bias", [P, D], FP32)
        eps = sb("o_eps", [P, 1], FP32)
        o_in = sb("o_in", [P, 2, KD, CH], FP32)
        inv = sb("o_inv", [P, 2, KD, CH], FP32)
        sums = sb("o_sums", [P, CH], FP32)
        o_n = sb("o_n", [P, 2, KD, CH], FP32)
        h = sb("o_h", [P, 2, 4, D], FP32)
        xn = sb("o_xn", [P, 2, 4, D], FP32)
        xt = sb("o_xt", [P, 2, KD, CH], FP32)
        stats = sb("o_stats", [P, 4, 6], FP32)
        mv = sb("o_mv", [P, 4, 2], FP32)
        std, rstd = sb("o_std", [P, 4], FP32), sb("o_rstd", [P, 4], FP32)
        ps_h = pb("o_ps_h", [P, 2, 4, D], FP32)
        ps_t = pb("o_ps_t", [P, 2, KD, CH], FP32)

        w_in, cleared, ident_ok = sem("o_w_in"), sem("o_cleared"), sem("o_ident_ok")
        in_ok = [sem("o_in0"), sem("o_in1")]
        sums_in, inv_stored = sem("o_sums_in"), sem("o_inv_stored")
        inv_ok, on_ok, h_ps, h_ok = sem("o_inv_ok"), sem("o_on_ok"), sem("o_h_ps"), sem("o_h_ok")
        step, mv_ok, std_ok, xn_ok = sem("o_step"), sem("o_mv_ok"), sem("o_std_ok"), sem("o_xn_ok")
        eps_ok = sem("o_eps_ok")
        t_ps, t_ok = sem("o_t_ps"), sem("o_t_ok")
        h_stored, x_stored = [sem("o_hs0"), sem("o_hs1")], [sem("o_xs0"), sem("o_xs1")]

        with nc.Block() as block:
            @block.sync
            def _(sp):
                sp.dma_start(w[:, :, :], wo.rearrange("(k p) n -> p k n", p=P)).then_inc(w_in, 16)
                sp.dma_start(bias[:, :], bo.partition_broadcast(P)).then_inc(w_in, 16)
                heads = P // DK
                for b, c, n, buf in batch_chunks(sp):
                    sp.wait_ge(on_ok, ONE + n - buf)
                    for m in range(KD):
                        src = o_scr.rearrange("(b g) h r s -> b (g h) r s", b=B)[bass.ds(b, 1), m * heads:(m + 1) * heads, :,
                                                                               bass.ds(c * CH, CH)]
                        src = src.rearrange("b h r s -> (b h) r s")
                        sp.dma_start(o_in[:, buf, m], src[:, 0:DK]).then_inc(in_ok[buf], 16)
                    sp.wait_ge(inv_stored, ONE + 16 * NC)
                    for m in range(KD):
                        scale = inv_scr.rearrange("(b h) s -> b h s", b=B)[bass.ds(b, 1), m * heads:(m + 1) * heads,
                                                                           bass.ds(c * CH, CH)]
                        sp.dma_start(inv[:, buf, m], scale.rearrange("b h s -> (b h) s")[:, None, :]
                                     .to_broadcast([heads, DK, CH])).then_inc(in_ok[buf], 16)

            @block.gpsimd
            def _(pool):
                identity(nc.gpsimd, ident[:, :], cleared, ident_ok)
                nc.gpsimd.memset(eps[:, :], LN_EPS).then_inc(eps_ok, 1)

            @block.tensor
            def _(pe):
                pe.wait_ge(w_in, ONE + 32)
                pe.wait_ge(ident_ok, ONE + 1)

                def transposes(n, buf):
                    pe.wait_ge(xn_ok, ONE + n + 1)
                    pe.wait_ge(t_ok, ONE + n - buf)
                    for t in range(4):
                        for k in range(KD):
                            last = nc.tensor.transpose(ps_t[:, buf, k, t * P:(t + 1) * P], xn[:, buf, t, k * P:(k + 1) * P],
                                                       ident[:, :])
                    last.then_inc(t_ps, 1)

                def project(n, buf):
                    pe.wait_ge(on_ok, ONE + n + 1)
                    pe.wait_ge(h_ok, ONE + n - buf)
                    for t in range(4):
                        for k in range(KD):
                            last = nc.tensor.matmul(ps_h[:, buf, t], o_n[:, buf, k, t * P:(t + 1) * P], w[:, k],
                                                    start=k == 0, stop=k == KD - 1)
                    last.then_inc(h_ps, 1)

                in_steps(pe, project, transposes)

            @block.scalar
            def _(act):
                rows = B * H
                for q in range(NC):
                    act.dma_start(sums[q * rows:(q + 1) * rows, :],
                                  o_scr[:, :, DK, q * CH:(q + 1) * CH].rearrange("g h s -> (g h) s")).then_inc(sums_in, 16)
                act.wait_ge(inv_ok, ONE + 1)
                for q in range(NC):
                    act.dma_start(inv_scr[:, q * CH:(q + 1) * CH], sums[q * rows:(q + 1) * rows, :]).then_inc(inv_stored, 16)
                act.wait_ge(eps_ok, ONE + 1)
                for b, c, n, buf in batch_chunks(act):
                    act.wait_ge(mv_ok, ONE + n + 1)
                    nc.scalar.activation(std[:, :], mv[:, :, 1], ACT.Sqrt, bias=eps[:, :]).then_inc(std_ok, 1)
                    act.wait_ge(t_ps, ONE + n + 1)
                    act.wait_ge(x_stored[buf], ONE + (n - buf) * 8)
                    nc.scalar.activation(xt[:, buf], ps_t[:, buf], ACT.Copy).then_inc(t_ok, 1)
                    act.dma_start(h_scr[bass.ds(n * 4, 4)].rearrange("t p d -> p t d"), h[:, buf]).then_inc(h_stored[buf], 16)
                    act.wait_ge(t_ok, ONE + n + 1)
                    act.dma_start(xn_scr[bass.ds(b, 1), :, bass.ds(c * CH, CH)].rearrange("b (k p) s -> p (b k) s", p=P),
                                  xt[:, buf]).then_inc(x_stored[buf], 16)
                for buf in range(2):
                    act.wait_ge(h_stored[buf], ONE + 16 * B * NC // 2)
                    act.wait_ge(x_stored[buf], ONE + 16 * B * NC // 2)

            @block.vector
            def _(dve):
                def scale(n, buf):
                    dve.wait_ge(in_ok[buf], ONE + (n - buf) * 32 + 64)
                    dve.wait_ge(h_ps, ONE + n - buf)
                    nc.vector.tensor_tensor(o_n[:, buf], o_in[:, buf], inv[:, buf], ALU.mult).then_inc(on_ok, 1)

                def norm(n, buf):
                    dve.wait_ge(h_ps, ONE + n + 1)
                    dve.wait_ge(h_stored[buf], ONE + (n - buf) * 8)
                    nc.vector.tensor_tensor(h[:, buf], ps_h[:, buf], bias[:, None, :].to_broadcast([P, 4, D]),
                                            ALU.add).then_inc(h_ok, 1)
                    dve.wait_ge(h_ok, ONE + n + 1)
                    dve.wait_ge(t_ps, ONE + n - buf)
                    normalize(nc, dve, h[:, buf], stats, mv, std[:, :], rstd[:, :], xn[:, buf], (step, mv_ok, std_ok, xn_ok), n)

                dve.wait_ge(sums_in, ONE + 16 * NC)
                nc.vector.reciprocal(sums[:, :], sums[:, :]).then_inc(inv_ok, 1)
                dve.wait_ge(w_in, ONE + 32)
                in_steps(dve, scale, norm)


def mamba(nc, sem, tag, backward, w, win_scr, xp_scr, dtw_scr, xn_scr, y_scr):
    with ExitStack() as ctx:
        def sb(name, shape, dt):
            return ctx.enter_context(nc.sbuf_tensor(tag + name, shape, dt))

        def pb(name, shape, dt):
            return ctx.enter_context(nc.psum_tensor(tag + name, shape, dt))

        def sem_(name):
            return sem(tag + name)

        win = sb("win", [P, KD, 2 * DI], FP32)
        xc = sb("xc", [P, ND, S], FP32)
        zs = sb("zs", [P, ND, S], FP32)
        delta = sb("delta", [P, ND, S], FP32)
        du = sb("du", [P, ND, S], FP32)
        bc_parts = sb("bc_parts", [PARTS * DS, 2, S], BF16)
        sel = sb("sel", [PARTS * DS, DS, P], BF16)
        ident = sb("ident", [P, P], FP32)
        wxp = sb("wxp", [P, ND, XPW], FP32)
        wdt = sb("wdt", [R, DI], FP32)
        conv_w = sb("conv_w", [P, ND, DC], FP32)
        cols = sb("cols", [P, 3, ND], FP32)
        a_log = sb("a_log", [P, ND, DS], FP32)
        a_cur = sb("a_cur", [P, 2, DS], FP32)
        diag = sb("diag", [P, 2, P], FP32)
        carry = sb("carry", [P, DS, 2], FP32)

        PAD = DC - 1
        XH = S + PAD + 1
        words = KD * S + 2 * XH + 2 * CH + 2 * PARTS * CH // 2 + CH
        stage = sb("stage", [P, max(words, 12 * TC)], FP32)
        at = 0

        def carve(shape):
            nonlocal at
            size = 1
            for s in shape:
                size *= s
            view = stage[:, at:at + size]
            at += size
            names = "abc"[:len(shape)]
            if len(shape) == 1:
                return view
            return view.rearrange(f"p ({' '.join(names)}) -> p {' '.join(names)}", **dict(zip(names, shape)))

        xn = carve([KD, S])
        xh = carve([2, XH])
        dt_in = carve([2, CH])
        split = carve([2 * PARTS * CH // 2]).bitcast(BF16).rearrange("p (b a s) -> p b a s", b=2, a=PARTS)
        rest = carve([CH])
        at = 0
        bc = carve([4, TC]).rearrange("p (n i) s -> p n i s", i=2)
        da = carve([4, TC])
        hs = carve([4, TC])

        ps_y = pb("ps_y", [P, 2, TC], FP32)
        ps_bc = [pb(f"ps_bc{i}", [P, TC], FP32) for i in range(2)]
        NH = TC // CH

        w_in, cleared, ident_ok = sem_("w_in"), sem_("cleared"), sem_("ident_ok")
        sel_step, sel_ok, a_step = sem_("sel_step"), sem_("sel_ok"), sem_("a_step")
        win_in = [sem_("win_x_in"), sem_("win_z_in")]
        xn_in = [sem_(f"xn_in{c}") for c in range(NC)]
        up_ps, up_ok = sem_("up_ps"), sem_("up_ok")
        pad_ok, conv_step, conv_ok, xc_ok = sem_("pad_ok"), sem_("conv_step"), sem_("conv_ok"), sem_("xc_ok")
        xp_ps, dt_ok, part1, rest_ok = sem_("xp_ps"), sem_("dt_ok"), sem_("part1"), sem_("rest_ok")
        part2, part3 = sem_("part2"), sem_("part3")
        bc_in = [sem_("bc_in0"), sem_("bc_in1")]
        dl_ps, dl_abs, dl_relu = sem_("dl_ps"), sem_("dl_abs"), sem_("dl_relu")
        dl_exp, dl_log, dl_sum, du_ok = sem_("dl_exp"), sem_("dl_log"), sem_("dl_sum"), sem_("du_ok")
        bc_ps = [sem_("b_ps"), sem_("c_ps")]
        bc_ok = [sem_("b_ok"), sem_("c_ok")]
        acur_ok, da_ok, h_ok = sem_("acur_ok"), sem_("da_ok"), sem_("h_ok")
        u_ok = sem_("u_ok")
        g_ok = sem_("g_ok")
        last_g_ok = sem_("last_g_ok")
        summed = sem_("summed")
        y_ok = sem_("y_ok")
        carry_ok, diag_ok, stored = sem_("carry_ok"), sem_("diag_ok"), sem_("stored")

        NCP = ND // 2
        NTC = S // TC
        STEPS = NTC * DS
        TILES = 2 * STEPS
        PER_TC = 2 * DS

        ORDER = list(range(NC))[::-1] if backward else list(range(NC))
        UPS = 2 * ND * NC

        def when(tc):
            return (NTC - 1) - tc if backward else tc

        def pairs(eng, body):
            def of_batch(b):
                with eng.Fori(0, NCP) as dp:
                    body(b * NCP + dp, dp, b)
            return of_batch

        def span(tile, dp, i, tc):
            return tile[:, bass.ds(dp * 2 + i, 1), when(tc) * TC:(when(tc) + 1) * TC].rearrange("p a s -> p (a s)")

        with nc.Block() as block:
            @block.sync
            def _(sp):
                for half in range(2):
                    sp.dma_start(win[:, :, half * DI:(half + 1) * DI],
                                 win_scr[:, half * DI:(half + 1) * DI].rearrange("(k p) m -> p k m", p=P)).then_inc(win_in[half], 16)
                sp.dma_start(conv_w[:, :, :], w["conv_w"].rearrange("(k p) c -> p k c", p=P)).then_inc(w_in, 16)
                for i, name in enumerate(("conv_b", "dt_b", "D")):
                    sp.dma_start(cols[:, i], w[name].rearrange("(k p) -> p k", p=P),
                                 allow_slow_non_contiguous=True).then_inc(w_in, 16)
                sp.dma_start(a_log[:, :, :], w["A_log"].rearrange("(k p) n -> p k n", p=P)).then_inc(w_in, 16)
                sp.dma_start(wxp[:, :, :], xp_scr).then_inc(w_in, 16)
                sp.dma_start(wdt[:, :], dtw_scr).then_inc(w_in, 16)
                with sp.Fori(0, B) as b:
                    for p, c in enumerate(ORDER):
                        sp.wait_ge(part3, ONE + b * NC + p + 1)
                        for i in range(PARTS):
                            for j in range(2):
                                sp.dma_start(bc_parts[i * DS:(i + 1) * DS, j, c * CH:(c + 1) * CH],
                                             split[X_BC[j]:X_BC[j] + DS, p % 2, i]).then_inc(bc_in[p % 2], 16)
                    with sp.Fori(0, NCP) as dp:
                        for tc in range(NTC):
                            sp.wait_ge(y_ok, ONE + (b * NCP + dp) * NTC * 2 + 2 * tc + 3)
                            steps = slice(when(tc) * TC, (when(tc) + 1) * TC)
                            sp.dma_start(y_scr[bass.ds(b, 1), bass.ds(dp * 2 * P, 2 * P), steps]
                                         .rearrange("b (k p) s -> p (b k) s", p=P),
                                         zs[:, bass.ds(dp * 2, 2), steps]).then_inc(stored, 16)
                sp.wait_ge(stored, ONE + 16 * B * NCP * NTC)

            @block.gpsimd
            def _(pool):
                identity(nc.gpsimd, ident[:, :], cleared, ident_ok)
                pool.wait_ge(ident_ok, ONE + 1)
                nc.gpsimd.memset(sel[:, :, :], 0.0).then_inc(sel_step, 1)
                for i in range(PARTS):
                    pool.wait_ge(sel_step, ONE + i + 1)
                    nc.gpsimd.affine_select(out=sel[:, :, :], in_=sel[:, :, :], compare_op=ALU.not_equal, fill=1.0,
                                            base=-i * DS, pattern=[[-1, DS], [0, P]], channel_multiplier=1
                                            ).then_inc(sel_step, 1)
                pool.wait_ge(sel_step, ONE + PARTS + 1)
                pool.sem_inc(g_ok, 4)
                pool.sem_inc(sel_ok, 1)

                def body(pair, dp, b):
                    for k in range(TILES - 1):
                        m = k // 2
                        pool.wait_ge(bc_ok[1], ONE + pair * STEPS + m + 1)
                        pool.wait_ge(h_ok, ONE + pair * TILES + k + 1)
                        nc.gpsimd.tensor_tensor(da[:, k % 4], hs[:, k % 4], bc[:, m % 2, 1], ALU.mult).then_inc(g_ok, 1)
                    pool.wait_ge(g_ok, ONE + pair * TILES + TILES - 1 + 4)
                    pool.wait_ge(last_g_ok, ONE + pair + 1)
                    pool.sem_inc(g_ok, 1)

                stage_b = pairs(pool, body)
                with pool.Fori(0, B) as b:
                    for p, c in enumerate(ORDER[:-1]):
                        pool.wait_ge(dl_sum, ONE + b * NC + p + 1)
                        pool.wait_ge(xc_ok, ONE + ND * (b + 1))
                        nc.gpsimd.tensor_tensor(du[:, :, c * CH:(c + 1) * CH], delta[:, :, c * CH:(c + 1) * CH],
                                                xc[:, :, c * CH:(c + 1) * CH], ALU.mult).then_inc(du_ok, 1)
                    stage_b(b)

            @block.tensor
            def _(pe):
                def up(b, m):
                    for c in range(NC):
                        pe.wait_ge(up_ok, ONE + b * UPS + m * NC + c + 1)
                        if m == 0:
                            pe.wait_ge(xn_in[c], ONE + 16 * (b + 1))
                        for k in range(KD):
                            last = nc.tensor.matmul(ps_y[:, c // NH, (c % NH) * CH:(c % NH + 1) * CH],
                                                    win[:, k, m * P:(m + 1) * P], xn[:, k, c * CH:(c + 1) * CH],
                                                    start=k == 0, stop=k == KD - 1)
                        last.then_inc(up_ps, 1)

                def spread(pair, m, j):
                    if m >= STEPS:
                        return
                    pe.wait_ge(bc_ok[j], ONE + pair * STEPS + m)
                    pe.nop(nofuse=True)
                    for i in range(NH):
                        at = when(m // DS) * TC + i * CH
                        last = nc.tensor.matmul(ps_bc[j][:, i * CH:(i + 1) * CH], sel[:, m % DS],
                                                bc_parts[:, j, at:at + CH], start=True, stop=True)
                    last.then_inc(bc_ps[j], 1)

                def add_skip(pair, dp, tc, i, c):
                    pe.wait_ge(diag_ok, ONE + pair * 2 + i + 1)
                    pe.nop(nofuse=True)
                    at = when(tc) * TC + c * CH
                    nc.tensor.matmul(ps_y[:, i, c * CH:(c + 1) * CH], diag[:, i],
                                     xc[:, bass.ds(dp * 2 + i, 1), at:at + CH].rearrange("p a s -> p (a s)"),
                                     start=False, stop=False)

                SKIPS = [3, 6, 9, 12]

                def body(pair, dp, b):
                    spread(pair, 0, 0)
                    spread(pair, 0, 1)
                    spread(pair, 1, 0)
                    spread(pair, 1, 1)
                    spread(pair, 2, 0)
                    for k in range(TILES):
                        m, i = divmod(k, 2)
                        tc, n = divmod(m, DS)
                        if k == 0:
                            pe.wait_ge(dl_relu, ONE + (b + 1) * NC * ND)
                        if n == 0:
                            pe.wait_ge(y_ok, ONE + (pair * NTC + tc) * 2 + i)
                        pe.wait_ge(g_ok, ONE + pair * TILES + k + 5)
                        for c in range(NH):
                            last = nc.tensor.matmul(ps_y[:, i, c * CH:(c + 1) * CH], ident[:, :],
                                                    da[:, k % 4, c * CH:(c + 1) * CH],
                                                    start=n == 0, stop=n == DS - 1)
                        last.then_inc(summed, 1)
                        if m == DS - 3 and i == 0:
                            for buf in range(2):
                                pe.wait_ge(bc_in[buf], ONE + (b + 1) * 16 * PARTS * NC)
                        if i == 0:
                            spread(pair, m + 2, 1)
                            spread(pair, m + 3, 0)
                        if i == 1 and n in SKIPS:
                            add_skip(pair, dp, tc, *divmod(SKIPS.index(n), NH))

                stage_b = pairs(pe, body)

                def project(b, p):
                    if p >= 2:
                        pe.wait_ge(part1, ONE + b * NC + p - 1)
                        pe.wait_ge(rest_ok, ONE + b * NC + p - 1)
                        pe.wait_ge(dt_ok, ONE + b * NC + p - 1)
                    c = ORDER[p]
                    for k in range(ND):
                        last = nc.tensor.matmul(ps_bc[0][0:XPW, p % 2 * CH:(p % 2 + 1) * CH], wxp[:, k],
                                                xc[:, k, c * CH:(c + 1) * CH], start=k == 0, stop=k == ND - 1)
                    last.then_inc(xp_ps, 1)

                def deltas(b, p):
                    pe.wait_ge(dt_ok, ONE + b * NC + p + 1)
                    for dt in range(ND):
                        if p:
                            pe.wait_ge(dl_relu, ONE + (b * NC + p - 1) * ND + dt + 1)
                        nc.tensor.matmul(ps_y[:, dt // NH, (dt % NH) * CH:(dt % NH + 1) * CH], wdt[:, dt * P:(dt + 1) * P],
                                         dt_in[0:R, p % 2], start=True, stop=True).then_inc(dl_ps, 1)

                pe.wait_ge(win_in[0], ONE + 16)
                pe.sem_inc(summed, 4)
                with pe.Fori(0, B) as b:
                    pe.wait_ge(y_ok, ONE + b * NCP * NTC * 2 + 1)
                    for m in range(2 * ND):
                        if m == ND:
                            pe.wait_ge(win_in[1], ONE + 16)
                        up(b, m)
                    pe.wait_ge(w_in, ONE + 7 * 16)
                    pe.wait_ge(xc_ok, ONE + ND * (b + 1))
                    project(b, 0)
                    project(b, 1)
                    pe.wait_ge(up_ok, ONE + (b + 1) * UPS + 4)
                    for p in range(NC):
                        deltas(b, p)
                        if p + 2 < NC:
                            project(b, p + 2)
                    pe.wait_ge(rest_ok, ONE + (b + 1) * NC)
                    pe.wait_ge(ident_ok, ONE + 1)
                    pe.wait_ge(sel_ok, ONE + 1)
                    for buf in range(2):
                        pe.wait_ge(bc_in[buf], ONE + b * 16 * PARTS * NC + 16 * PARTS * 2 * (TC // CH) // 2)
                    pe.nop(nofuse=True)
                    stage_b(b)

            @block.scalar
            def _(act):
                act.sem_inc(up_ok, 4)

                def copy(pair, m, j, used):
                    if m >= STEPS:
                        return
                    act.wait_ge(bc_ps[j], ONE + pair * STEPS + m + 1)
                    act.wait_ge(used, ONE + pair * TILES + 2 * m + 2)
                    nc.scalar.activation(bc[:, m % 2, j], ps_bc[j][:, :], ACT.Copy).then_inc(bc_ok[j], 1)

                def body(pair, dp, b):
                    act.wait_ge(da_ok, ONE + pair * TILES)
                    act.nop(nofuse=True)
                    nc.scalar.activation(a_cur[:, :, :], a_log[:, bass.ds(dp * 2, 2), :], ACT.Exp).then_inc(a_step, 1)
                    act.wait_ge(a_step, ONE + pair + 1)
                    nc.scalar.activation(a_cur[:, :, :], a_cur[:, :, :], ACT.Copy, scale=-1.0).then_inc(acur_ok, 1)
                    copy(pair, 0, 0, u_ok)
                    act.wait_ge(acur_ok, ONE + pair + 1)
                    for k in range(TILES):
                        m, i = divmod(k, 2)
                        if k == PER_TC:
                            act.wait_ge(dl_sum, ONE + (b + 1) * NC)
                        act.wait_ge(summed, ONE + pair * TILES + k + 1)
                        act.nop(nofuse=True)
                        nc.scalar.activation(da[:, k % 4], span(delta, dp, i, m // DS), ACT.Exp,
                                             scale=a_cur[:, i, m % DS:m % DS + 1]).then_inc(da_ok, 1)
                        if i == 0:
                            copy(pair, m, 1, g_ok)
                            copy(pair, m + 1, 0, u_ok)

                stage_b = pairs(act, body)
                def bank(c):
                    return ps_y[:, c // NH, (c % NH) * CH:(c % NH + 1) * CH]

                def take_x(b, dt):
                    for c in range(NC):
                        act.wait_ge(up_ps, ONE + b * UPS + dt * NC + c + 1)
                        if dt >= 2 and c == 0:
                            act.wait_ge(conv_ok, ONE + b * ND + dt - 1)
                        off = (0 if backward else PAD) + c * CH
                        nc.scalar.activation(xh[:, dt % 2, off:off + CH], bank(c), ACT.Copy).then_inc(up_ok, 1)

                def take_z(b, dt):
                    for c in range(NC):
                        act.wait_ge(up_ps, ONE + b * UPS + (ND + dt) * NC + c + 1)
                        nc.scalar.activation(zs[:, dt, c * CH:(c + 1) * CH], bank(c), ACT.Silu).then_inc(up_ok, 1)

                def silu_x(b, dt):
                    act.wait_ge(conv_ok, ONE + b * ND + dt + 1)
                    nc.scalar.activation(xc[:, dt], xc[:, dt], ACT.Silu).then_inc(xc_ok, 1)

                def delta_exps(b, p):
                    cols_c = slice(ORDER[p] * CH, (ORDER[p] + 1) * CH)
                    for dt in range(ND):
                        act.wait_ge(dl_ps, ONE + (b * NC + p) * ND + dt + 1)
                        nc.scalar.activation(delta[:, dt, cols_c], bank(dt), ACT.Abs, bias=cols[:, 1, dt:dt + 1]
                                             ).then_inc(dl_abs, 1)
                    act.wait_ge(dl_abs, ONE + (b * NC + p + 1) * ND)
                    nc.scalar.activation(delta[:, :, cols_c], delta[:, :, cols_c], ACT.Exp, scale=-1.0).then_inc(dl_exp, 1)

                def delta_logs(b, p):
                    cols_c = slice(ORDER[p] * CH, (ORDER[p] + 1) * CH)
                    act.wait_ge(dl_exp, ONE + b * NC + p + 1)
                    nc.scalar.activation(delta[:, :, cols_c], delta[:, :, cols_c], ACT.Ln, bias=1.0).then_inc(dl_log, 1)

                with act.Fori(0, B) as b:
                    act.wait_ge(g_ok, ONE + b * NCP * TILES + 4)
                    for c in range(NC):
                        act.dma_start(xn[:, :, c * CH:(c + 1) * CH],
                                      xn_scr[bass.ds(b, 1), :, c * CH:(c + 1) * CH].rearrange("b (k p) s -> p (b k) s", p=P)
                                      ).then_inc(xn_in[c], 16)
                    take_x(b, 0)
                    take_x(b, 1)
                    take_x(b, 2)
                    silu_x(b, 0)
                    take_x(b, 3)
                    silu_x(b, 1)
                    act.wait_ge(stored, ONE + 16 * NCP * NTC * b)
                    take_z(b, 0)
                    silu_x(b, 2)
                    take_z(b, 1)
                    silu_x(b, 3)
                    take_z(b, 2)
                    take_z(b, 3)
                    for p in range(NC):
                        act.wait_ge(xp_ps, ONE + b * NC + p + 1)
                        if p >= 2:
                            act.wait_ge(dl_ps, ONE + (b * NC + p - 1) * ND)
                            act.wait_ge(bc_in[p % 2], ONE + b * 16 * PARTS * NC + 16 * PARTS * 2)
                        bank_p = slice(p % 2 * CH, (p % 2 + 1) * CH)
                        nc.scalar.activation(dt_in[0:R, p % 2], ps_bc[0][X_DT:X_DT + R, bank_p], ACT.Copy).then_inc(dt_ok, 1)
                        nc.scalar.activation(split[0:X_DT - 16, p % 2, 0], ps_bc[0][0:X_DT - 16, bank_p], ACT.Copy).then_inc(part1, 1)
                        if p:
                            delta_exps(b, p - 1)
                        act.wait_ge(rest_ok, ONE + b * NC + p + 1)
                        nc.scalar.activation(split[0:X_DT - 16, p % 2, 1], rest[0:X_DT - 16, :], ACT.Copy).then_inc(part2, 1)
                        if p == NC // 2:
                            for done in range(NC // 2):
                                delta_logs(b, done)
                    for done in range(NC // 2, NC - 1):
                        delta_logs(b, done)
                    delta_exps(b, NC - 1)
                    delta_logs(b, NC - 1)
                    act.wait_ge(dl_sum, ONE + b * NC + TC // CH)
                    stage_b(b)

            @block.vector
            def _(dve):
                dve.wait_ge(w_in, ONE + 7 * 16)
                dve.wait_ge(ident_ok, ONE + 1)
                dve.sem_inc(u_ok, 2)
                dve.sem_inc(y_ok, 1)

                def body(pair, dp, b):
                    first = pair * TILES

                    def inputs(k):
                        if k >= TILES:
                            return
                        m, i = divmod(k, 2)
                        if i == 0:
                            dve.wait_ge(bc_ok[0], ONE + pair * STEPS + m + 1)
                        dve.wait_ge(g_ok, ONE + first + k + 1)
                        if i == 0 and 2 <= m < DS + 2:
                            dve.wait_ge(carry_ok, ONE + pair * DS + m - 1)
                            dve.nop(nofuse=True)
                        nc.vector.tensor_tensor(hs[:, k % 4], span(du, dp, i, m // DS), bc[:, m % 2, 0],
                                                ALU.mult).then_inc(u_ok, 1)

                    def scan(k):
                        m, i = divmod(k, 2)
                        tc, n = divmod(m, DS)
                        dve.wait_ge(da_ok, ONE + first + k + 1)
                        dve.wait_ge(u_ok, ONE + first + k + 3)
                        rev = slice(None, None, -1) if backward else slice(None)
                        nc.vector.tensor_tensor_scan(hs[:, k % 4, rev], da[:, k % 4, rev], hs[:, k % 4, rev],
                                                     carry[:, n, i:i + 1] if tc else 0.0, ALU.mult, ALU.add
                                                     ).then_inc(h_ok, 1)

                    def keep(m):
                        if 0 <= m < DS:
                            dve.wait_ge(h_ok, ONE + first + 2 * m + 2)
                            end = 0 if backward else TC - 1
                            k = 2 * m % 4
                            nc.vector.tensor_copy(carry[:, m, :], hs[:, k:k + 2, end]).then_inc(carry_ok, 1)

                    def gate(tc, i):
                        dve.wait_ge(summed, ONE + first + tc * PER_TC + PER_TC + 4 - 1 + i)
                        nc.vector.tensor_tensor(span(zs, dp, i, tc), ps_y[:, i], span(zs, dp, i, tc), ALU.mult
                                                ).then_inc(y_ok, 1)

                    for i in range(2):
                        nc.vector.tensor_scalar(diag[:, i], ident[:, :], cols[:, 2, bass.ds(dp * 2 + i, 1)], None,
                                                ALU.mult).then_inc(diag_ok, 1)
                    inputs(0)
                    for k in range(TILES):
                        inputs(k + 1)
                        if k % 2 == 0:
                            keep(k // 2 - 1)
                        scan(k)
                        if k - PER_TC in (GATE_AT, GATE_AT + 1):
                            gate(0, k - PER_TC - GATE_AT)
                    k = TILES - 1
                    dve.wait_ge(h_ok, ONE + first + TILES)
                    dve.wait_ge(bc_ok[1], ONE + pair * STEPS + STEPS)
                    nc.vector.tensor_tensor(da[:, k % 4], hs[:, k % 4], bc[:, k // 2 % 2, 1], ALU.mult).then_inc(last_g_ok, 1)
                    for i in range(2):
                        gate(1, i)

                GATE_AT = 1
                stage_b = pairs(dve, body)

                def delta_relus(b, p):
                    cols_c = slice(ORDER[p] * CH, (ORDER[p] + 1) * CH)
                    for dt in range(ND):
                        dve.wait_ge(dl_abs, ONE + (b * NC + p) * ND + dt + 1)
                        nc.vector.tensor_scalar(du[:, dt, cols_c], ps_y[:, dt // NH, (dt % NH) * CH:(dt % NH + 1) * CH],
                                                cols[:, 1, dt:dt + 1], 0.0, ALU.add, ALU.max).then_inc(dl_relu, 1)

                def delta_sums(b, p):
                    cols_c = slice(ORDER[p] * CH, (ORDER[p] + 1) * CH)
                    dve.wait_ge(dl_relu, ONE + (b * NC + p + 1) * ND)
                    dve.wait_ge(dl_log, ONE + b * NC + p + 1)
                    nc.vector.tensor_tensor(delta[:, :, cols_c], delta[:, :, cols_c], du[:, :, cols_c], ALU.add).then_inc(dl_sum, 1)

                with dve.Fori(0, B) as b:
                    pad = slice(S, S + PAD) if backward else slice(0, PAD)
                    nc.vector.memset(xh[:, :, pad], 0.0).then_inc(pad_ok, 1)
                    dve.wait_ge(pad_ok, ONE + b + 1)
                    for dt in range(ND):
                        dve.wait_ge(up_ok, ONE + b * UPS + (dt + 1) * NC + 4)
                        for tap in range(DC):
                            lo = PAD - tap if backward else tap
                            src = xh[:, dt % 2, lo:lo + S]
                            if tap == 0:
                                nc.vector.tensor_scalar(xc[:, dt], src, conv_w[:, dt, 0:1], cols[:, 0, dt:dt + 1],
                                                        ALU.mult, ALU.add).then_inc(conv_step, 1)
                            else:
                                dve.wait_ge(conv_step, ONE + (b * ND + dt) * (DC - 1) + tap)
                                nc.vector.scalar_tensor_tensor(out=xc[:, dt], in0=src, scalar=conv_w[:, dt, tap:tap + 1],
                                                               in1=xc[:, dt], op0=ALU.mult, op1=ALU.add
                                                               ).then_inc(conv_ok if tap == DC - 1 else conv_step, 1)
                    for p in range(NC):
                        dve.wait_ge(part1, ONE + b * NC + p + 1)
                        if p:
                            dve.wait_ge(part3, ONE + b * NC + p)
                        bank_p = slice(p % 2 * CH, (p % 2 + 1) * CH)
                        nc.vector.tensor_tensor(rest[0:X_DT - 16, :], ps_bc[0][0:X_DT - 16, bank_p], split[0:X_DT - 16, p % 2, 0],
                                                ALU.subtract).then_inc(rest_ok, 1)
                        if p:
                            delta_relus(b, p - 1)
                        dve.wait_ge(part2, ONE + b * NC + p + 1)
                        nc.vector.tensor_tensor(split[0:X_DT - 16, p % 2, 2], rest[0:X_DT - 16, :], split[0:X_DT - 16, p % 2, 1],
                                                ALU.subtract).then_inc(part3, 1)
                        if p == NC // 2:
                            for done in range(NC // 2):
                                delta_sums(b, done)
                    for done in range(NC // 2, NC - 1):
                        delta_sums(b, done)
                    delta_relus(b, NC - 1)
                    delta_sums(b, NC - 1)
                    cols_c = slice(ORDER[-1] * CH, (ORDER[-1] + 1) * CH)
                    dve.wait_ge(dl_sum, ONE + (b + 1) * NC)
                    nc.vector.tensor_tensor(du[:, :, cols_c], delta[:, :, cols_c], xc[:, :, cols_c], ALU.mult).then_inc(du_ok, 1)
                    dve.wait_ge(du_ok, ONE + (b + 1) * NC)
                    for buf in range(2):
                        dve.wait_ge(bc_in[buf], ONE + (b + 1) * 16 * PARTS * NC)
                    dve.nop(nofuse=True)
                    stage_b(b)


def mamba_out_and_ffn(nc, sem, y_scr, ow_scr, h_scr, u1, v1, b1, u2, v2, b2, out):
    NF = FF // P
    NY = 2 * DI // P
    NCH = T // CH
    with ExitStack() as ctx:
        def sb(name, shape, dt):
            return ctx.enter_context(nc.sbuf_tensor("ffn_" + name, shape, dt))

        def pb(name, shape, dt):
            return ctx.enter_context(nc.psum_tensor("ffn_" + name, shape, dt))

        ident = sb("ident", [P, P], FP32)
        wo = sb("wo", [P, NY, D], FP32)
        wu1 = sb("u1", [P, KD, RK], FP32)
        wv1 = sb("v1", [RK, FF], FP32)
        bias1 = sb("b1", [P, NF], FP32)
        wu2 = sb("u2", [P, NF, RK], FP32)
        wv2 = sb("v2", [RK, D], FP32)
        bias2 = sb("b2", [P, D], FP32)
        eps = sb("eps", [P, 1], FP32)
        y = sb("y", [P, 2, NY, CH], FP32)
        h = sb("h", [P, 2, 4, D], FP32)
        xn = sb("xn", [P, 2, 4, D], FP32)
        xt = sb("xt", [P, KD, CH], FP32)
        pt = sb("pt", [RK, CH], FP32)
        hid = sb("hid", [P, 2, NF, CH], FP32)
        qt = sb("qt", [RK, CH], FP32)
        res = sb("res", [P, 2, 4, D], FP32)
        stats = sb("stats", [P, 4, 6], FP32)
        mv = sb("mv", [P, 4, 2], FP32)
        std, rstd = sb("std", [P, 4], FP32), sb("rstd", [P, 4], FP32)
        ps_h = pb("ps_h", [P, 4, D], FP32)
        ps_t = pb("ps_t", [P, KD, CH], FP32)
        ps_g = [pb(f"ps_g{i}", [P, CH], FP32) for i in range(2)]
        ps_pq = pb("ps_pq", [RK, CH], FP32)

        def s_(name, start=ONE):
            return sem("ffn_" + name, start)

        w_in, cleared, ident_ok, eps_ok = s_("w_in"), s_("cleared"), s_("ident_ok"), s_("eps_ok")
        wo_in = s_("wo_in")
        y_in = [s_("y_in0"), s_("y_in1")]
        h_ps, h_ok = s_("h_ps"), s_("h_ok")
        step, mv_ok, std_ok, xn_ok = s_("step"), s_("mv_ok"), s_("std_ok"), s_("xn_ok")
        t_ps, t_ok, p_ps, p_ok = s_("t_ps"), s_("t_ok"), s_("p_ps"), s_("p_ok")
        g_ps, g_ok, q_ps, q_ok, o_ps = s_("g_ps"), s_("g_ok"), s_("q_ps"), s_("q_ok"), s_("o_ps")
        hb_ok, res_ok = s_("hb_ok"), s_("res_ok")
        stored = [s_("stored0"), s_("stored1")]

        def chunks(eng, body):
            with eng.Fori(0, NCH // 2 - 1) as i:
                for buf in range(2):
                    body(2 * i + buf, buf, False)
            body(NCH - 2, 0, False)
            body(NCH - 1, 1, True)

        with nc.Block() as block:
            @block.sync
            def _(sp):
                for z in range(2):
                    sp.dma_start(wo[:, z * ND:(z + 1) * ND], ow_scr[z]).then_inc(wo_in, 16)
                for b, c, n, buf in batch_chunks(sp):
                    sp.wait_ge(h_ps, ONE + n - buf)
                    sp.wait_ge(hb_ok, ONE + n - buf)
                    for z in range(2):
                        sp.dma_start(y[:, buf, z * ND:(z + 1) * ND],
                                     y_scr[z, bass.ds(b, 1), :, bass.ds(c * CH, CH)].rearrange("b (k p) s -> p (b k) s", p=P)
                                     ).then_inc(y_in[buf], 16)
                    sp.dma_start(h[:, buf], h_scr[bass.ds(n * 4, 4)].rearrange("t p d -> p t d")).then_inc(y_in[buf], 16)

            @block.gpsimd
            def _(pool):
                identity(nc.gpsimd, ident[:, :], cleared, ident_ok)
                nc.gpsimd.memset(eps[:, :], LN_EPS).then_inc(eps_ok, 1)

            @block.tensor
            def _(pe):
                def project(n, buf):
                    pe.wait_ge(y_in[buf], ONE + (n - buf) * 24 + 48)
                    pe.wait_ge(h_ok, ONE + n)
                    for t in range(4):
                        for k in range(NY):
                            last = nc.tensor.matmul(ps_h[:, t], y[:, buf, k, t * P:(t + 1) * P], wo[:, k],
                                                    start=k == 0, stop=k == NY - 1)
                    last.then_inc(h_ps, 1)

                def transposes(n, buf):
                    pe.wait_ge(xn_ok, ONE + n + 1)
                    pe.wait_ge(t_ok, ONE + n)
                    for t in range(4):
                        for k in range(KD):
                            last = nc.tensor.transpose(ps_t[:, k, t * P:(t + 1) * P], xn[:, buf, t, k * P:(k + 1) * P], ident[:, :])
                    last.then_inc(t_ps, 1)

                def body(n, buf, last_chunk):
                    pe.wait_ge(t_ok, ONE + n + 1)
                    pe.wait_ge(q_ok, ONE + n)
                    for k in range(KD):
                        last = nc.tensor.matmul(ps_pq[:, :], wu1[:, k], xt[:, k], start=k == 0, stop=k == KD - 1)
                    last.then_inc(p_ps, 1)
                    if not last_chunk:
                        pe.wait_ge(res_ok, ONE + n)
                        project(n + 1, 1 - buf)
                    pe.wait_ge(p_ok, ONE + n + 1)

                    def down(k):
                        pe.wait_ge(g_ok, ONE + n * NF + k + 3)
                        return nc.tensor.matmul(ps_pq[:, :], wu2[:, k], hid[:, buf, k], start=k == 0, stop=k == NF - 1)

                    for m in range(NF):
                        pe.wait_ge(g_ok, ONE + n * NF + m + 1)
                        nc.tensor.matmul(ps_g[m % 2][:, :], wv1[:, m * P:(m + 1) * P], pt[:, :], start=True, stop=True
                                         ).then_inc(g_ps, 1)
                        if m >= 2:
                            down(m - 2)
                    down(NF - 2)
                    down(NF - 1).then_inc(q_ps, 1)
                    if not last_chunk:
                        transposes(n + 1, 1 - buf)
                        pe.wait_ge(h_ok, ONE + n + 2)
                    pe.wait_ge(q_ok, ONE + n + 1)
                    for t in range(4):
                        last = nc.tensor.matmul(ps_h[:, t], qt[:, t * P:(t + 1) * P], wv2[:, :], start=True, stop=True)
                    last.then_inc(o_ps, 1)

                pe.wait_ge(wo_in, ONE + 2 * 16)
                project(0, 0)
                pe.wait_ge(w_in, ONE + 6 * 16)
                pe.wait_ge(ident_ok, ONE + 1)
                transposes(0, 0)
                chunks(pe, body)

            @block.scalar
            def _(act):
                def root(n):
                    act.wait_ge(mv_ok, ONE + n + 1)
                    nc.scalar.activation(std[:, :], mv[:, :, 1], ACT.Sqrt, bias=eps[:, :]).then_inc(std_ok, 1)

                def copy_t(n):
                    act.wait_ge(t_ps, ONE + n + 1)
                    nc.scalar.activation(xt[:, :, :], ps_t[:, :, :], ACT.Copy).then_inc(t_ok, 1)

                def body(n, buf, last_chunk):
                    act.wait_ge(p_ps, ONE + n + 1)
                    nc.scalar.activation(pt[:, :], ps_pq[:, :], ACT.Copy).then_inc(p_ok, 1)
                    for m in range(NF):
                        if m == ROOT_AT and not last_chunk:
                            root(n + 1)
                        act.wait_ge(g_ps, ONE + n * NF + m + 1)
                        nc.scalar.activation(hid[:, buf, m], ps_g[m % 2][:, :], ACT.Gelu_apprx_tanh,
                                             bias=bias1[:, m:m + 1]).then_inc(g_ok, 1)
                    act.wait_ge(q_ps, ONE + n + 1)
                    nc.scalar.activation(qt[:, :], ps_pq[:, :], ACT.Copy).then_inc(q_ok, 1)
                    if not last_chunk:
                        copy_t(n + 1)
                    act.wait_ge(res_ok, ONE + n + 1)
                    act.dma_start(out[bass.ds(n * 4, 4)].rearrange("t p d -> p t d"), res[:, buf]).then_inc(stored[buf], 16)

                ROOT_AT = 3
                act.dma_start(bias2[:, :], b2.partition_broadcast(P)).then_inc(w_in, 16)
                act.dma_start(wu1[:, :, :], u1.rearrange("(k p) r -> p k r", p=P)).then_inc(w_in, 16)
                act.dma_start(bias1[:, :], b1.rearrange("(k p) -> p k", p=P), allow_slow_non_contiguous=True).then_inc(w_in, 16)
                act.dma_start(wv1[:, :], v1).then_inc(w_in, 16)
                act.dma_start(wu2[:, :, :], u2.rearrange("(k p) r -> p k r", p=P)).then_inc(w_in, 16)
                act.dma_start(wv2[:, :], v2).then_inc(w_in, 16)
                act.wait_ge(eps_ok, ONE + 1)
                act.wait_ge(w_in, ONE + 6 * 16)
                act.sem_inc(g_ok, 2)
                root(0)
                copy_t(0)
                chunks(act, body)
                for buf in range(2):
                    act.wait_ge(stored[buf], ONE + 16 * NCH // 2)

            @block.vector
            def _(dve):
                def norm(n, buf):
                    dve.wait_ge(h_ps, ONE + n + 1)
                    dve.wait_ge(y_in[buf], ONE + (n - buf) * 24 + 48)
                    nc.vector.tensor_tensor(h[:, buf], ps_h[:, :, :], h[:, buf], ALU.add).then_inc(h_ok, 1)
                    dve.wait_ge(h_ok, ONE + n + 1)
                    normalize(nc, dve, h[:, buf], stats, mv, std[:, :], rstd[:, :], xn[:, buf], (step, mv_ok, std_ok, xn_ok), n)
                    dve.wait_ge(stored[buf], ONE + (n - buf) * 8)
                    nc.vector.tensor_tensor(res[:, buf], h[:, buf], bias2[:, None, :].to_broadcast([P, 4, D]),
                                            ALU.add).then_inc(hb_ok, 1)

                def finish(n, buf):
                    dve.wait_ge(hb_ok, ONE + n + 1)
                    dve.wait_ge(o_ps, ONE + n + 1)
                    nc.vector.tensor_tensor(res[:, buf], ps_h[:, :, :], res[:, buf], ALU.add).then_inc(res_ok, 1)

                def body(n, buf, last_chunk):
                    if not last_chunk:
                        norm(n + 1, 1 - buf)
                    finish(n, buf)

                dve.wait_ge(w_in, ONE + 6 * 16)
                norm(0, 0)
                chunks(dve, body)


def lm_tower(nc, a, out):
    def scratch(name, shape, dt):
        return nc.dram_tensor(name, shape, dt, kind="Internal").ap()

    q_scr = scratch("q_scr", [PARTS, B, D, S], BF16)
    k_scr = scratch("k_scr", [PARTS, B, D, S], BF16)
    o_scr = scratch("o_scr", [G, HG, DK + 1, S], FP32)
    inv_scr = scratch("inv_scr", [B * H, S], FP32)
    h_scr = scratch("h_scr", [T // P, P, D], FP32)
    xn_scr = scratch("xn_scr", [B, D, S], FP32)
    y_scr = scratch("y_scr", [2, B, DI, S], FP32)
    win_scr = scratch("win_scr", [2, D, 2 * DI], FP32)
    xp_scr = scratch("xp_scr", [2, P, ND, XPW], FP32)
    dtw_scr = scratch("dtw_scr", [2, R, DI], FP32)
    ow_scr = scratch("ow_scr", [2, P, ND, D], FP32)
    names = ("in_w", "conv_w", "conv_b", "xproj_w", "dt_w", "dt_b", "A_log", "D", "out_w")
    dirs = [{n: a[f"L0_attn_{z}_{n}"] for n in names} for z in "fb"]

    with nc.sbuf_tensor("v_all", [P, B, H // HG, NT, HG * DK], FP32) as v_all:
        with semaphores(nc) as sem:
            embed_and_project(nc, sem, a["x"], a["L0_tok_emb"], [a[f"L0_tok_w{n}"] for n in "qkv"],
                              [a[f"L0_tok_b{n}"] for n in "qkv"], q_scr, k_scr, v_all)
        with semaphores(nc) as sem:
            attention(nc, sem, q_scr, k_scr, v_all, o_scr, (dirs, win_scr, xp_scr, dtw_scr, ow_scr))
    with semaphores(nc) as sem:
        attention_out(nc, sem, o_scr, inv_scr, a["L0_tok_wo"], a["L0_tok_bo"], h_scr, xn_scr)
    for z in range(2):
        with semaphores(nc) as sem:
            mamba(nc, sem, "fb"[z] + "_", z == 1, dirs[z], win_scr[z], xp_scr[z], dtw_scr[z], xn_scr, y_scr[z])
    with semaphores(nc) as sem:
        mamba_out_and_ffn(nc, sem, y_scr, ow_scr, h_scr, a["L0_ffn_U1"], a["L0_ffn_V1"], a["L0_ffn_b1"],
                          a["L0_ffn_U2"], a["L0_ffn_V2"], a["L0_ffn_b2"],
                          out.rearrange("b (t p) d -> (b t) p d", p=P))


def kernel(**inputs):
    import concourse.bacc as bacc
    from concourse.bass_utils import run_bass_kernel_spmd

    nc = bacc.Bacc("TRN2", target_bir_lowering=False, num_devices=1)
    arrays, args = {}, {}
    for name, value in inputs.items():
        value = np.ascontiguousarray(value)
        arrays[f"in_{name}_dram"] = value
        args[name] = nc.dram_tensor(f"in_{name}_dram", value.shape, mybir.dt.from_np(value.dtype), kind="ExternalInput").ap()
    out = nc.dram_tensor("out_0_dram", (B, S, D), FP32, kind="ExternalOutput").ap()
    lm_tower(nc, args, out)
    result = run_bass_kernel_spmd(nc, [arrays], core_ids=[0])
    return result.results[0]["out_0_dram"]
```
